# Optimizing a Trainium2 kernel written in Bass

```python
import numpy as np
import jax
import jax.numpy as jnp

def _softmax(x, axis=-1):
    return jax.nn.softmax(x, axis=axis)

def _gelu(x):
    return jax.nn.gelu(x, approximate=True)

def _silu(x):
    return jax.nn.silu(x)

def _sigmoid(x):
    return jax.nn.sigmoid(x)

def _layernorm(x, axis=-1, eps=1e-05):
    m = jnp.mean(x, axis=axis, keepdims=True)
    v = jnp.var(x, axis=axis, keepdims=True)
    return (x - m) / jnp.sqrt(v + eps)

def _scatter_add(tgt, idx, src, axis=0):
    return tgt.at[idx].add(src)

def _segment_sum(src, seg, n):
    return jax.ops.segment_sum(src, seg, n)
kernel_name = 'mk_gnn_preln_d4_gnn_r64_e985da'

def setup_inputs(seed: int=0):
    np.random.seed(seed)
    _w = jnp.asarray

    def _rec_inputs():
        import jax
        import jax.numpy as jnp
        _gk = jax.random.key(seed)
        x = -0.000202 + 1 * jax.random.normal(jax.random.fold_in(_gk, 1), (100000, 128), jnp.float32)
        src = jax.random.randint(jax.random.fold_in(_gk, 2), (50000,), 0, 100000, jnp.int32)
        dst = jnp.minimum((100000 * jax.random.uniform(jax.random.fold_in(_gk, 3), (50000,)) ** 2.0).astype(jnp.int32), 99999)
        _o = jnp.argsort(dst, stable=True)
        src = src[_o]
        dst = dst[_o]
        edge_weight = jax.random.uniform(jax.random.fold_in(_gk, 12), (50000,), jnp.float32, 0.0, 0.999998)
        return (x, src, dst, edge_weight)
    x, src, dst, edge_weight = _rec_inputs()

    def _L0_gnn_setup():
        import jax, jax.numpy as jnp
        import numpy as np
        N_NODES = 50000
        N_EDGES = 12500
        IN_CH, HID_CH, OUT_CH = (128, 256, 128)

        def _glorot(key, shape):
            fan_in, fan_out = (shape[1], shape[0])
            lim = float(np.sqrt(6.0 / (fan_in + fan_out)))
            return jax.random.uniform(key, shape, jnp.float32, -lim, lim)

        def _sage_conv(x, src, dst, Wl, bl, Wr, n_nodes):
            msg = x[src]
            agg = jax.ops.segment_sum(msg, dst, num_segments=n_nodes)
            deg = jax.ops.segment_sum(jnp.ones((src.shape[0],), x.dtype), dst, num_segments=n_nodes)
            mean = agg / jnp.maximum(deg, 1.0)[:, None]
            return mean @ Wl.T + bl + x @ Wr.T
        key = jax.random.key(seed)
        ks = jax.random.split(key, 8)
        x = jax.random.normal(ks[0], (N_NODES, IN_CH), jnp.float32)
        edge_index = jax.random.randint(ks[1], (2, N_EDGES), 0, N_NODES, jnp.int64)
        return {'x': x, 'edge_index': edge_index, 'W1l': _glorot(ks[2], (HID_CH, IN_CH)), 'b1l': jnp.zeros((HID_CH,), jnp.float32), 'W1r': _glorot(ks[3], (HID_CH, IN_CH)), 'W2l': _glorot(ks[4], (OUT_CH, HID_CH)), 'b2l': jnp.zeros((OUT_CH,), jnp.float32), 'W2r': _glorot(ks[5], (OUT_CH, HID_CH))}
    _L0_gnn_all = _L0_gnn_setup()
    _L0_gnn_in = {k: v for k, v in _L0_gnn_all.items() if k in ('W1l', 'b1l', 'W1r', 'W2l', 'b2l', 'W2r')}
    del _L0_gnn_all

    def _L1_gnn_setup():
        import jax, jax.numpy as jnp
        import numpy as np
        ALPHA = 0.2
        LN_EPS = 1e-05
        key = jax.random.key(seed)
        ks = jax.random.split(key, 6)
        N, E, D = (100000, 9375, 128)
        x = jax.random.normal(ks[0], (N, D), dtype=jnp.float32)
        edge_index = jax.random.randint(ks[1], (2, E), 0, N, dtype=jnp.int64)
        W1 = jax.random.normal(ks[2], (D, D // 2), dtype=jnp.float32) * (1.0 / np.sqrt(D))
        b1 = jnp.zeros((D // 2,), dtype=jnp.float32)
        W2 = jax.random.normal(ks[3], (D // 2, D), dtype=jnp.float32) * (1.0 / np.sqrt(D // 2))
        b2 = jnp.zeros((D,), dtype=jnp.float32)
        gamma = jnp.ones((D,), dtype=jnp.float32)
        beta = jnp.zeros((D,), dtype=jnp.float32)
        return {'x': x, 'edge_index': edge_index, 'W1': W1, 'b1': b1, 'W2': W2, 'b2': b2, 'gamma': gamma, 'beta': beta}
    _L1_gnn_all = _L1_gnn_setup()
    _L1_gnn_in = {k: v for k, v in _L1_gnn_all.items() if k in ('W1', 'b1', 'W2', 'b2', 'gamma', 'beta')}
    del _L1_gnn_all

    def _L2_gnn_setup():
        import jax, jax.numpy as jnp
        import numpy as np
        N, E = (50000, 10000)
        D_IN, D_OUT, N_BASES = (128, 128, 8)
        key = jax.random.key(seed)
        k1, k2, k3, k4, k5, k6 = jax.random.split(key, 6)
        x = jax.random.normal(k1, (N, D_IN), dtype=jnp.float32)
        edge_index = jax.random.randint(k2, (2, E), 0, N, dtype=jnp.int64)
        bases = jax.random.normal(k3, (N_BASES, D_IN, D_OUT), dtype=jnp.float32) * 0.05
        comp = jax.random.normal(k4, (1, N_BASES), dtype=jnp.float32)
        root = jax.random.normal(k5, (D_IN, D_OUT), dtype=jnp.float32) * 0.05
        bias = jax.random.normal(k6, (D_OUT,), dtype=jnp.float32) * 0.01
        return {'x': x, 'edge_index': edge_index, 'bases': bases, 'comp': comp, 'root': root, 'bias': bias}
    _L2_gnn_all = _L2_gnn_setup()
    _L2_gnn_in = {k: v for k, v in _L2_gnn_all.items() if k in ('bases', 'comp', 'root', 'bias')}
    del _L2_gnn_all

    def _L3_gnn_setup():
        import jax, jax.numpy as jnp
        import numpy as np
        EPS = 0.0
        key = jax.random.key(seed)
        kx, ke, kw, k1, k2 = jax.random.split(key, 5)
        N, E, D, H = (100000, 9375, 128, 128)
        x = jax.random.normal(kx, (N, D), dtype=jnp.float32)
        edge_index = jax.random.randint(ke, (2, E), 0, N, dtype=jnp.int64)
        edge_weight = jax.random.uniform(kw, (E,), dtype=jnp.float32)
        W1 = jax.random.normal(k1, (D, H), dtype=jnp.float32) * (1.0 / np.sqrt(D))
        b1 = jnp.zeros((H,), dtype=jnp.float32)
        W2 = jax.random.normal(k2, (H, D), dtype=jnp.float32) * (1.0 / np.sqrt(H))
        b2 = jnp.zeros((D,), dtype=jnp.float32)
        return {'x': x, 'edge_index': edge_index, 'edge_weight': edge_weight, 'W1': W1, 'b1': b1, 'W2': W2, 'b2': b2}
    _L3_gnn_all = _L3_gnn_setup()
    _L3_gnn_in = {k: v for k, v in _L3_gnn_all.items() if k in ('W1', 'b1', 'W2', 'b2')}
    del _L3_gnn_all
    return {'x': x, 'src': src, 'dst': dst, 'edge_weight': edge_weight, 'L0_gnn_W1l': _L0_gnn_in['W1l'], 'L0_gnn_b1l': _L0_gnn_in['b1l'], 'L0_gnn_W1r': _L0_gnn_in['W1r'], 'L0_gnn_W2l': _L0_gnn_in['W2l'], 'L0_gnn_b2l': _L0_gnn_in['b2l'], 'L0_gnn_W2r': _L0_gnn_in['W2r'], 'L1_gnn_W1': _L1_gnn_in['W1'], 'L1_gnn_b1': _L1_gnn_in['b1'], 'L1_gnn_W2': _L1_gnn_in['W2'], 'L1_gnn_b2': _L1_gnn_in['b2'], 'L1_gnn_gamma': _L1_gnn_in['gamma'], 'L1_gnn_beta': _L1_gnn_in['beta'], 'L2_gnn_bases': _L2_gnn_in['bases'], 'L2_gnn_comp': _L2_gnn_in['comp'], 'L2_gnn_root': _L2_gnn_in['root'], 'L2_gnn_bias': _L2_gnn_in['bias'], 'L3_gnn_W1': _L3_gnn_in['W1'], 'L3_gnn_b1': _L3_gnn_in['b1'], 'L3_gnn_W2': _L3_gnn_in['W2'], 'L3_gnn_b2': _L3_gnn_in['b2']}

def reference(x, src, dst, edge_weight, L0_gnn_W1l, L0_gnn_b1l, L0_gnn_W1r, L0_gnn_W2l, L0_gnn_b2l, L0_gnn_W2r, L1_gnn_W1, L1_gnn_b1, L1_gnn_W2, L1_gnn_b2, L1_gnn_gamma, L1_gnn_beta, L2_gnn_bases, L2_gnn_comp, L2_gnn_root, L2_gnn_bias, L3_gnn_W1, L3_gnn_b1, L3_gnn_W2, L3_gnn_b2):
    import jax
    import jax.numpy as jnp

    def _L0_gnn_ref(x, edge_index, W1l, b1l, W1r, W2l, b2l, W2r):
        import jax, jax.numpy as jnp
        import numpy as np
        N_NODES = 50000
        N_EDGES = 12500
        IN_CH, HID_CH, OUT_CH = (128, 256, 128)

        def _glorot(key, shape):
            fan_in, fan_out = (shape[1], shape[0])
            lim = float(np.sqrt(6.0 / (fan_in + fan_out)))
            return jax.random.uniform(key, shape, jnp.float32, -lim, lim)

        def _sage_conv(x, src, dst, Wl, bl, Wr, n_nodes):
            msg = x[src]
            agg = jax.ops.segment_sum(msg, dst, num_segments=n_nodes)
            deg = jax.ops.segment_sum(jnp.ones((src.shape[0],), x.dtype), dst, num_segments=n_nodes)
            mean = agg / jnp.maximum(deg, 1.0)[:, None]
            return mean @ Wl.T + bl + x @ Wr.T
        src, dst = (edge_index[0], edge_index[1])
        n = x.shape[0]
        h = _sage_conv(x, src, dst, W1l, b1l, W1r, n)
        h = jax.nn.relu(h)
        out = _sage_conv(h, src, dst, W2l, b2l, W2r, n)
        return out

    def _L1_gnn_ref(x, edge_index, W1, b1, W2, b2, gamma, beta):
        import jax, jax.numpy as jnp
        import numpy as np
        ALPHA = 0.2
        LN_EPS = 1e-05
        N = x.shape[0]
        src, dst = (edge_index[0], edge_index[1])
        msg_sum = jax.ops.segment_sum(x[src], dst, num_segments=N)
        cnt = jax.ops.segment_sum(jnp.ones_like(dst, dtype=x.dtype), dst, num_segments=N)
        local_mean = msg_sum / jnp.maximum(cnt, 1.0)[:, None]
        feature_diff = jnp.tanh(jnp.linalg.norm(x - local_mean, axis=1, keepdims=True))
        enhanced = jax.nn.relu(x @ W1 + b1) @ W2 + b2
        h = x + ALPHA * enhanced * feature_diff
        mu = jnp.mean(h, axis=-1, keepdims=True)
        var = jnp.var(h, axis=-1, keepdims=True)
        return (h - mu) * jax.lax.rsqrt(var + LN_EPS) * gamma + beta

    def _L2_gnn_ref(x, edge_index, bases, comp, root, bias):
        import jax, jax.numpy as jnp
        import numpy as np
        N, E = (50000, 10000)
        D_IN, D_OUT, N_BASES = (128, 128, 8)
        W = jnp.einsum('b,bio->io', comp[0], bases)
        src = edge_index[0]
        dst = edge_index[1]
        agg = jax.ops.segment_sum(x[src], dst, num_segments=x.shape[0])
        out = agg @ W + x @ root + bias
        return out

    def _L3_gnn_ref(x, edge_index, edge_weight, W1, b1, W2, b2):
        import jax, jax.numpy as jnp
        import numpy as np
        EPS = 0.0
        N = x.shape[0]
        src, dst = (edge_index[0], edge_index[1])
        msg = edge_weight[:, None] * x[src]
        agg = jax.ops.segment_sum(msg, dst, num_segments=N)
        out = (1.0 + EPS) * x + agg
        h = jax.nn.relu(out @ W1 + b1)
        return h @ W2 + b2
    edge_index = jnp.stack([src, dst])
    h = jnp.maximum(_layernorm(x, axis=-1), 0.0)
    x = x + _L0_gnn_ref(h, edge_index, L0_gnn_W1l, L0_gnn_b1l, L0_gnn_W1r, L0_gnn_W2l, L0_gnn_b2l, L0_gnn_W2r)
    h = jnp.maximum(_layernorm(x, axis=-1), 0.0)
    x = x + _L1_gnn_ref(h, edge_index, L1_gnn_W1, L1_gnn_b1, L1_gnn_W2, L1_gnn_b2, L1_gnn_gamma, L1_gnn_beta)
    h = jnp.maximum(_layernorm(x, axis=-1), 0.0)
    x = x + _L2_gnn_ref(h, edge_index, L2_gnn_bases, L2_gnn_comp, L2_gnn_root, L2_gnn_bias)
    h = jnp.maximum(_layernorm(x, axis=-1), 0.0)
    x = x + _L3_gnn_ref(h, edge_index, edge_weight, L3_gnn_W1, L3_gnn_b1, L3_gnn_W2, L3_gnn_b2)
    return x

_drawn_inputs = setup_inputs


def setup_inputs(seed=0):
    import zlib

    import numpy as np

    out = dict(_drawn_inputs(seed))
    spreads = {'L0_gnn_b1l': (0.0, 0.1),
     'L0_gnn_b2l': (0.0, 0.1),
     'L1_gnn_b1': (0.0, 0.8),
     'L1_gnn_b2': (0.0, 0.465),
     'L1_gnn_gamma': (1.0, 0.2),
     'L1_gnn_beta': (0.0, 0.1),
     'L3_gnn_b1': (0.0, 0.291),
     'L3_gnn_b2': (0.0, 0.1)}
    factors = {'L2_gnn_bias': 8.0}
    for name, (base, spread) in spreads.items():
        noise = np.random.default_rng([zlib.crc32(name.encode()), seed]).standard_normal(out[name].shape)
        drawn = base * np.exp(spread * noise) if base else spread * noise
        out[name] = jnp.asarray(drawn.astype(out[name].dtype))
    for name, factor in factors.items():
        out[name] = (out[name] * factor).astype(out[name].dtype)
    return out
```

```python
import concourse.bass as bass
from concourse import mybir
from contextlib import ExitStack

P = 128
D = 128
HID = 256
HALF = 64
BLK = 4
GROUP = P * BLK
MAX_MAIN = 6
OVER = 8
RING = 4
EPS = 1e-5
ALPHA = 0.2
REC = 4

F32 = mybir.dt.float32
F32R = mybir.dt.float32r
I32 = mybir.dt.int32
ALU = mybir.AluOpType
ACT = mybir.ActivationFunctionType
AX = mybir.AxisListType


def slot(group, ring):
    return group[1] % ring


def turn(group, ring):
    t, k = group
    return t * (RING // ring) + k // ring


def number(group):
    return group[0] * RING + group[1]


def before(group):
    return (group[1] - 2) % RING, group[0] + (group[1] - 2) // RING + 1


def static(group):
    return isinstance(group[0], int)


def very_first(group):
    return static(group) and number(group) == 0


def ahead(group, n):
    return (group[0], group[1] + n)


class Shape:

    def __init__(self, nodes, edges):
        self.nodes, self.edges = nodes, edges
        self.groups = -(-nodes // (GROUP * RING)) * RING
        self.tail_group = nodes // GROUP
        self.tail = nodes - self.tail_group * GROUP
        self.padded = self.groups * GROUP
        self.per_part = -(-(edges + 1 + MAX_MAIN * P + OVER * P) // P)
        while edges % self.per_part:
            self.per_part += 1
        self.edge_parts = edges // self.per_part
        self.table = self.groups + RING + 1
        first, second = RING * (self.groups // 64), RING * (self.groups * 17 // 256)
        cuts = [c for c in (0, first, second, self.groups) if c == 0 or c >= 2 * RING]
        cuts = sorted(set(cuts))
        mains = (2 * MAX_MAIN // 3, MAX_MAIN // 3) if len(cuts) < 4 else (MAX_MAIN, 2 * MAX_MAIN // 3, MAX_MAIN // 3)
        self.spans = [(a, b, m) for a, b, m in zip(cuts, cuts[1:], mains)]


def gnn_kernel(nc, x, src, dst, edge_weight, W1l, b1l, W1r, W2cat, b2l, C1, c1, C2, c2, gamma, beta,
               bases, comp, root, bias, V1, v1, V2, v2, out):
    s = Shape(x.shape[0], src.shape[0])
    assert s.edge_parts <= P and P * s.per_part >= s.edges + (MAX_MAIN + OVER) * P and s.tail % BLK == 0

    records = nc.dram_tensor("edge_records", [P * s.per_part + s.edges + OVER * P, REC], I32).ap()
    y_dram = nc.dram_tensor("sage_partial", [s.padded, D], F32).ap()
    p_dram = nc.dram_tensor("sage_projected", [s.padded, D], F32).ap()
    x1_dram = nc.dram_tensor("x_after_sage", [s.padded, D], F32).ap()
    x2_dram = nc.dram_tensor("x_after_contrast", [s.padded, D], F32).ap()
    x3_dram = nc.dram_tensor("x_after_basis", [s.padded, D], F32).ap()

    with ExitStack() as ctx:
        def sb(name, shape, dt=F32):
            return ctx.enter_context(nc.sbuf_tensor(name, shape, dt))

        k = {}
        k["table"] = sb("group_table", [1, s.table * REC], I32)
        k["base"] = sb("group_base", [P, s.table])
        k["iota"] = sb("node_of_column", [P, GROUP])
        k["ident"] = sb("identity", [P, P])
        k["eps"] = sb("eps", [P, 1])
        k["inv"] = sb("inverse_degree", [P, s.groups * BLK])
        k["W1l"] = sb("W1l_s", [P, HID])
        k["W1r"] = sb("W1r_s", [P, HID])
        k["b1l"] = sb("b1l_s", [P, 2])
        k["W2"] = sb("W2_s", [P, 2, 2 * D])
        k["b2l"] = sb("b2l_s", [P, D])
        k["C1"] = sb("C1_s", [P, HALF])
        k["c1"] = sb("c1_s", [HALF, 1])
        k["C2"] = sb("C2_s", [HALF + 1, D])
        k["gamma"] = sb("gamma_s", [P, D])
        k["beta"] = sb("beta_s", [P, D])
        k["W"] = sb("basis_W", [P, D])
        k["root"] = sb("root_s", [P, D])
        k["bias"] = sb("bias_s", [P, D])
        k["V1"] = sb("V1_s", [P, D])
        k["v1"] = sb("v1_s", [P, 1])
        k["V2"] = sb("V2_s", [P, D])
        k["v2"] = sb("v2_s", [P, D])

        setup(nc, s, k, src, dst, edge_weight, W1l, b1l, W1r, W2cat, b2l, C1, c1, C2, c2, gamma, beta,
              bases, comp, root, bias, V1, v1, V2, v2, records)
        for kind, x_of, rows, to, projected in (
                ("sage1", x, x, y_dram, p_dram), ("sage2", y_dram, p_dram, x1_dram, None),
                ("contrast", x1_dram, x1_dram, x2_dram, None), ("basis", x2_dram, x2_dram, x3_dram, None),
                ("weighted", x3_dram, x3_dram, out, None)):
            for span in s.spans:
                node_pass(nc, s, k, kind, span, records, x_of, rows, to, projected)


def setup(nc, s, k, src, dst, edge_weight, W1l, b1l, W1r, W2cat, b2l, C1, c1, C2, c2, gamma, beta,
          bases, comp, root, bias, V1, v1, V2, v2, records):
    E, J, T = s.edges, s.per_part, s.table
    with ExitStack() as ctx:
        def sb(name, shape, dt=F32):
            return ctx.enter_context(nc.sbuf_tensor(name, shape, dt))

        def sem(name):
            return ctx.enter_context(nc.semaphore("setup_" + name))

        src_i = sb("src_i", [P, J], I32)
        dst_i = sb("dst_i", [P, J], I32)
        next_i = sb("next_i", [P, J], I32)
        w_in = sb("w_in", [P, J])
        dst_f = sb("dst_f", [P, J])
        next_f = sb("next_f", [P, J])
        rec = sb("rec", [P, J, REC], I32)
        base_i = sb("base_i", [P, T], I32)
        iota_i = sb("iota_i", [P, GROUP], I32)
        below = sb("below", [P, T + 1])
        hit = sb("hit", [P, J])
        ones = sb("ones", [P, 1])
        bases_s = sb("bases_s", [P, 8, D])
        comp_s = sb("comp_s", [P, 8])
        w_acc = sb("w_acc", [P, 2, D])
        bound = sb("bound", [1, T + 1])
        unsorted = sb("unsorted", [1, 1])
        lo_f = sb("lo_f", [1, T])
        count_f = sb("count_f", [1, T])
        rounds_i = sb("rounds_i", [1, T], I32)
        rounds_f = sb("rounds_f", [1, T + 1])
        zero_f = sb("zero_f", [1, T + 1])
        prefix_f = sb("prefix_f", [1, T + 1])
        sums = ctx.enter_context(nc.psum_tensor("bound_sums", [1, 512], F32))

        edges_in = sem("edges_in")
        consts_in = sem("consts_in")
        records_out = sem("records_out")
        cleared = sem("cleared")
        iotas = sem("iotas")
        step = sem("vector_step")
        counted = sem("counted")
        summed = sem("summed")
        built = sem("records_built")

        n_edge_loads = 5 if s.edge_parts > 1 else 4
        consts = [(k["W1l"][:, :], W1l), (k["W1r"][:, :], W1r), (k["b1l"][:, :], b1l),
                  (k["W2"][:, 0, :], W2cat[0:P, :]), (k["W2"][:, 1, :], W2cat[P:HID, :]), (k["b2l"][:, :], b2l),
                  (k["C1"][:, :], C1), (k["c1"][:, :], c1), (k["C2"][0:HALF, :], C2),
                  (k["C2"][HALF:HALF + 1, :], c2), (k["gamma"][:, :], gamma), (k["beta"][:, :], beta),
                  (k["root"][:, :], root), (k["bias"][:, :], bias), (k["V1"][:, :], V1), (k["v1"][:, :], v1),
                  (k["V2"][:, :], V2), (k["v2"][:, :], v2), (comp_s[:, :], comp),
                  (bases_s[:, :, :], bases.rearrange("b i o -> i b o"))]
        block = ctx.enter_context(nc.Block())

        @block.sync
        def _(sp):
            def rows(a, n):
                return a[0:n * J].rearrange("(p j) -> p j", j=J)

            Q = s.edge_parts
            sp.wait_ge(cleared, 3)
            sp.dma_start(src_i[0:Q, :], rows(src, Q)).then_inc(edges_in, 16)
            sp.dma_start(dst_i[0:Q, :], rows(dst, Q)).then_inc(edges_in, 16)
            sp.dma_start(w_in[0:Q, :], rows(edge_weight, Q)).then_inc(edges_in, 16)
            sp.dma_start(next_i[0:Q - 1, :], dst[1:(Q - 1) * J + 1].rearrange("(p j) -> p j", j=J)).then_inc(edges_in, 16)
            sp.dma_start(next_i[Q - 1:Q, 0:J - 1], dst[(Q - 1) * J + 1:E].rearrange("(a j) -> a j", a=1)).then_inc(edges_in, 16)
            sp.wait_ge(built, 1)
            sp.dma_start(records[0:P * J, :].rearrange("(p j) c -> p (j c)", j=J), rec[:, :, :].rearrange("p j c -> p (j c)")).then_inc(records_out, 16)
            sp.wait_ge(records_out, 16)

        @block.scalar
        def _(act):
            for to, of in consts:
                act.dma_start(to, of).then_inc(consts_in, 16)
            act.wait_ge(consts_in, 16 * len(consts))

        @block.gpsimd
        def _(pool):
            pool.memset(src_i[:, :], 0)
            pool.memset(w_in[:, :], 0.0)
            pool.memset(dst_i[:, :], 1 << 23).then_inc(cleared, 1)
            pool.memset(next_i[:, :], 1 << 23).then_inc(cleared, 1)
            pool.memset(rec[:, :, :], 0).then_inc(cleared, 1)
            pool.memset(k["ident"][:, :], 0.0).then_inc(iotas, 1)
            pool.wait_ge(iotas, 1)
            pool.affine_select(out=k["ident"][:, :], in_=k["ident"][:, :], compare_op=ALU.not_equal, fill=1.0,
                               base=0, pattern=[[-1, P]], channel_multiplier=1)
            pool.memset(k["eps"][:, :], EPS)
            pool.iota(base_i[:, :], pattern=[[GROUP, T]], base=0, channel_multiplier=0)
            pool.iota(iota_i[:, :], pattern=[[1, BLK], [BLK, P]], base=0, channel_multiplier=0).then_inc(iotas, 1)

        @block.vector
        def _(dve):
            dve.memset(ones[:, :], 1.0)
            dve.memset(zero_f[:, :], 0.0)
            dve.memset(rounds_f[:, :], 0.0)
            dve.memset(k["table"][:, :], 0).then_inc(step, 1)
            dve.wait_ge(iotas, 2)
            dve.tensor_copy(k["base"][:, :], base_i[:, :])
            dve.tensor_copy(k["iota"][:, :], iota_i[:, :]).then_inc(step, 1)
            dve.wait_ge(edges_in, 16 * 5)
            dve.tensor_copy(dst_f[:, :], dst_i[:, :])
            dve.tensor_copy(next_f[:, :], next_i[:, :]).then_inc(step, 1)
            dve.wait_ge(step, 3)
            dve.tensor_copy(rec[:, :, 0], src_i[:, :])
            dve.tensor_copy(rec[:, :, 1], dst_f[:, :].bitcast(I32))
            dve.tensor_copy(rec[:, :, 2], w_in[:, :].bitcast(I32)).then_inc(built, 1)
            dve.tensor_tensor(hit[:, :], next_f[:, :], dst_f[:, :], ALU.is_lt).then_inc(step, 1)
            dve.wait_ge(step, 4)
            dve.tensor_reduce(below[:, T:T + 1], hit[:, :], AX.X, ALU.add).then_inc(step, 1)
            dve.wait_ge(step, 5)
            for g in range(T):
                dve.tensor_scalar(hit[:, :], dst_f[:, :], float(g * GROUP), 0.0, ALU.is_lt, ALU.add,
                                  accum_out=below[:, g:g + 1]).then_inc(step, 1)
                dve.wait_ge(step, 6 + g)
            dve.tensor_scalar(hit[:, 0:1], hit[:, 0:1], 0.0, None, ALU.mult).then_inc(counted, 1)
            dve.wait_ge(summed, 1)
            n = 6 + T - 1

            def link(ins):
                nonlocal n
                n += 1
                ins.then_inc(step, 1)
                dve.wait_ge(step, n)

            link(dve.tensor_copy(bound[:, :], sums[:, 0:T + 1]))
            link(dve.tensor_scalar(unsorted[:, :], bound[:, T:T + 1], 1.0, None, ALU.min))
            link(dve.tensor_scalar(lo_f[:, :], bound[:, 0:T], unsorted[:, 0:1], None, ALU.mult))
            link(dve.tensor_tensor(lo_f[:, :], bound[:, 0:T], lo_f[:, :], ALU.subtract))
            link(dve.memset(count_f[:, :], 0.0))
            link(dve.tensor_tensor(count_f[:, 0:T - 1], bound[:, 1:T], bound[:, 0:T - 1], ALU.subtract))
            link(dve.tensor_scalar(hit[0:1, 0:T], count_f[:, :], -1.0, float(E), ALU.mult, ALU.add))
            link(dve.tensor_scalar(hit[0:1, 0:T], hit[0:1, 0:T], unsorted[:, 0:1], None, ALU.mult))
            link(dve.tensor_tensor(count_f[:, :], count_f[:, :], hit[0:1, 0:T], ALU.add))
            for a, b, main in s.spans:
                b = T if b == s.groups else b
                link(dve.tensor_scalar(count_f[:, a:b], count_f[:, a:b], float(-main * P), 0.0, ALU.add, ALU.max))
            link(dve.tensor_scalar(count_f[:, :], count_f[:, :], float(OVER * P - 1), None, ALU.add))
            link(dve.memset(count_f[:, s.groups:T], 0.0))
            link(dve.tensor_copy(rounds_i[:, :], count_f[:, :]))
            link(dve.tensor_scalar(rounds_i[:, :], rounds_i[:, :], (OVER * P).bit_length() - 1, None, ALU.arith_shift_right))
            link(dve.tensor_copy(rounds_f[:, 1:T + 1], rounds_i[:, :]))
            link(dve.memset(prefix_f[:, :], 0.0))
            for a, b, _ in s.spans:
                link(dve.tensor_tensor_scan(prefix_f[:, a + 1:b], rounds_f[:, a + 1:b], zero_f[:, a + 1:b], 0.0, ALU.add, ALU.add))
            tab = k["table"][:, :].rearrange("a (g c) -> a g c", c=REC)
            dve.tensor_copy(tab[:, :, 0], lo_f[:, :])
            dve.tensor_copy(tab[:, :, 1], rounds_i[:, :])
            dve.tensor_copy(tab[:, :, 2], prefix_f[:, 0:T])
            dve.wait_ge(consts_in, 16 * len(consts))
            link(dve.tensor_scalar(w_acc[:, 0, :], bases_s[:, 0, :], comp_s[:, 0:1], None, ALU.mult))
            for b in range(1, 8):
                to = k["W"][:, :] if b == 7 else w_acc[:, b % 2, :]
                link(dve.scalar_tensor_tensor(to, bases_s[:, b, :], comp_s[:, b:b + 1], w_acc[:, (b - 1) % 2, :], ALU.mult, ALU.add))

        @block.tensor
        def _(pe):
            pe.wait_ge(counted, 1)
            pe.matmul(sums[:, 0:T + 1], ones[:, :], below[:, :], start=True, stop=True).then_inc(summed, 1)


def node_pass(nc, s, k, kind, span, records, x_dram, rows_dram, out_dram, p_dram):
    base_group, end_group, MAIN = span
    GROUPS = end_group - base_group
    LAG = {"sage1": 1, "sage2": 0, "contrast": 2, "basis": 1, "weighted": 1}[kind]
    KEEP = RING if kind == "contrast" else 2
    normed = kind != "sage2"
    node_major = kind in ("sage1", "sage2", "contrast")
    degree = kind == "sage1"
    weighted = kind == "weighted"
    final = kind == "weighted"
    cols = MAIN + BLK
    width = D + 2 if degree else D

    with ExitStack() as ctx:
        def sb(name, shape, dt=F32):
            return ctx.enter_context(nc.sbuf_tensor(f"{kind}{base_group}_{name}", shape, dt))

        def pb(name, cols):
            return ctx.enter_context(nc.psum_tensor(f"{kind}{base_group}_{name}", [P, cols], F32))

        made = []

        def sem(name):
            made.append(nc.alloc_semaphore(f"{kind}{base_group}_{name}"))
            return made[-1]

        def sems(name, n):
            return [sem(f"{name}{i}") for i in range(n)]

        meta = sb("meta", [P, RING, MAIN, REC], I32)
        raw = sb("raw", [P, RING, MAIN, D])
        xin = sb("xin", [P, RING, BLK, D])
        msg = sb("msg", [P, 2, MAIN, D])
        hi = sb("msg_hi", [P, 2, MAIN, width], F32R)
        lo = sb("msg_lo", [P, 2, MAIN, D], F32R)
        rel = sb("rel_dst", [P, 2, MAIN])
        S = sb("onehot", [P, 2, MAIN, GROUP], F32R)
        st = sb("bn", [P, cols, 6])
        mv = sb("mean_var", [P, cols, 2])
        std = sb("std", [P, cols])
        rstd = sb("rstd", [P, 2, cols])
        nb = sb("neg_mean_rstd", [P, 2, cols])
        h = sb("h", [P, KEEP, BLK, D])
        xb = sb("x_plus_bias", [P, KEEP, BLK, D])
        o_s = sb("out_tile", [P, 2, BLK, D])
        zero_s = sb("zero", [1, 1])
        tick_s = sb("tick", [1, 2])
        meta_o = sb("ometa", [P, OVER, REC], I32)
        raw_o = sb("oraw", [P, OVER, D])
        msg_o = sb("omsg", [P, OVER, D])
        hi_o = sb("omsg_hi", [P, OVER, width], F32R)
        lo_o = sb("omsg_lo", [P, OVER, D], F32R)
        rel_o = sb("orel_dst", [P, OVER])
        S_o = sb("oonehot", [P, OVER, GROUP], F32R)
        st_o = sb("obn", [P, OVER, 6])
        mv_o = sb("omean_var", [P, OVER, 2])
        std_o = sb("ostd", [P, OVER])
        rstd_o = sb("orstd", [P, OVER])
        nb_o = sb("oneg_mean_rstd", [P, OVER])
        if degree:
            deg = sb("deg", [P, BLK])
            invg = sb("inv_deg", [P, BLK])
            mean = sb("mean", [P, BLK, D])
            hT = sb("hT", [P, GROUP])
            mT = sb("meanT", [P, GROUP])
            HT = sb("hiddenT", [P, 2, GROUP])
            p_s = sb("p_tile", [P, 2, BLK, D])
            agg = pb("agg", 1024)
            tr = pb("transposed", 1024)
            hid = pb("hidden", 1024)
            outp = pb("out", 1024)
            sums = agg[:, :].rearrange("p (k c) -> p k c", k=2)[:, :, 0:2 * width].rearrange("p k (j c) -> p k j c", c=width)
        else:
            agg = pb("agg", 512)
        if kind == "sage2":
            invg = sb("inv_deg", [P, BLK])
        if kind == "contrast":
            invg = sb("inv_deg", [P, BLK])
            diff = sb("diff", [P, BLK, D])
            sq = sb("sq", [P, BLK, D])
            ssq = sb("ssq", [P, BLK])
            nrm = sb("norm", [P, BLK])
            th = sb("tanh", [P, BLK])
            ta = sb("alpha_tanh", [P, BLK])
            hT = sb("hT", [P, GROUP])
            hc = sb("hiddenT", [HALF + 1, GROUP])
            e_s = sb("enhanced", [P, BLK, D])
            st2 = sb("bn2", [P, BLK, 6])
            mv2 = sb("mean_var2", [P, BLK, 2])
            std2 = sb("std2", [P, BLK])
            rstd2 = sb("rstd2", [P, BLK])
            nb2 = sb("nb2", [P, BLK])
            n_s = sb("normed", [P, BLK, D])
            ng_s = sb("normed_gamma", [P, BLK, D])
            tr = pb("transposed", 512)
            hid = pb("hidden", 512)
            outp = pb("out", 512)
        if kind == "basis":
            aT = sb("aggT", [P, GROUP])
            hT = sb("hT", [P, GROUP])
            tr = pb("transposed", 512)
            outp = pb("out", 512)
        if kind == "weighted":
            zT = sb("zT", [P, GROUP])
            gT = sb("hiddenT", [P, GROUP])
            hid = pb("hidden", 512)
            outp = pb("out", 512)

        meta_in = sems("meta_in", RING)
        x_in = sems("x_in", RING)
        raw_in = [sems(f"raw_in{c}_", RING) for c in range(MAIN)]
        seg = sems("onehot_built", RING)
        stats = sem("stats")
        moments = sem("moments")
        std_ready = sem("std")
        rstd_ready = sem("rstd")
        coef = sem("coef")
        relset = sem("rel")
        rows_ready = sems("rows_ready", RING)
        lo_ready = sems("lo_ready", RING)
        h_ready = sems("h_ready", RING)
        xb_ready = sems("xb_ready", RING)
        agg_done = sems("agg_done", RING)
        agg_free = sem("agg_free")
        out_ready = sems("out_ready", 2)
        stored = sems("stored", 2)
        cleared = sem("cleared")
        zeroed = sem("zeroed")
        tick = sem("tick")
        o_tick = sem("otick")
        meta_o_in = sem("ometa_in")
        raw_o_in = sems("oraw_in", OVER)
        o_stats = sem("ostats")
        o_moments = sem("omoments")
        o_std = sem("ostd")
        o_rstd = sem("orstd")
        o_coef = sem("ocoef")
        o_rel = sem("orel")
        o_seg = sem("oonehot_built")
        o_rows = sem("orows_ready")
        o_lo = sem("olo_ready")
        o_agg = sem("oagg_done")
        if weighted:
            unweighted = sem("unweighted")
            o_unweighted = sem("ounweighted")
        else:
            unweighted = o_unweighted = None
        if degree:
            p_ready = sems("p_ready", 2)
            p_stored = sems("p_stored", 2)
        dense = {n: sem(n) for n in {
            "sage1": ["deg_max", "inv_done", "mean_ready", "hT_psum", "mT_psum", "hT_ready", "mT_ready", "hid_a",
                      "hid_b", "HT_a", "HT_b", "out_psum"],
            "sage2": ["inv_copied"],
            "contrast": ["inv_copied", "diff_done", "sq_done", "ssq_done", "norm_done", "tanh_done", "ta_done", "hT_psum", "hT_ready",
                         "hid_psum", "hc_ready", "out_psum", "e_done", "st2_done", "mv2_done", "std2_done",
                         "rstd2_done", "coef2", "n_ready", "ng_ready"],
            "basis": ["hT_psum", "hT_ready", "aT_ready", "out_psum"],
            "weighted": ["zT_ready", "hid_psum", "gT_ready", "out_psum"],
        }[kind]}
        passed = ExitStack()
        block = passed.enter_context(nc.Block())

        mf = meta[:, :, :, :].bitcast(F32)
        mof = meta_o[:, :, :].bitcast(F32)

        def node_group(group):
            return number(group) + base_group

        def done(count):
            return max(count, 0) if isinstance(count, int) else count

        def quads(eng, step, last=None):
            turns = GROUPS // RING
            end = turns if last is None else turns - 1
            for q in range(RING):
                step((0, q))
            if end > 1:
                with eng.Fori(1, end) as t:
                    for q in range(RING):
                        step((t, q))
            if last is not None:
                for q in range(RING):
                    last((turns - 1, q))

        final_group = (GROUPS // RING - 1, RING - 1)

        def table(eng, group, word, most):
            at = node_group(group) * REC + word
            return eng.value_load(k["table"][0:1, bass.ds(at, 1)], min_val=0, max_val=most)

        def rounds_of(eng, group, body):
            most = -(-s.edges // (OVER * P))
            n = table(eng, group, 1, most)
            with eng.If(n > 0):
                before = table(eng, group, 2, most * s.table)
                with eng.Fori(0, n) as i:
                    body(i, before + i)

        def rows_of(dram, g, n=GROUP):
            return dram[bass.ds(g * GROUP, n), :].rearrange("(p b) f -> p (b f)", b=BLK)

        @block.sync
        def _(sp):
            def load_meta(group):
                r, u = slot(group, RING), turn(group, RING)
                for c in range(MAIN):
                    sp.wait_ge(raw_in[c][r], u * 16)
                sp.wait_ge(seg[r], u)
                if weighted:
                    sp.wait_ge(lo_ready[r], u)
                    sp.wait_ge(rows_ready[r], u)
                first = table(sp, group, 0, s.edges)
                sp.dma_start(meta[:, r, :, :].rearrange("p c w -> p (c w)"),
                             records[bass.ds(first, MAIN * P), :].rearrange("(p c) w -> p (c w)", c=MAIN)
                             ).then_inc(meta_in[r], 16)

            def load_x(group, where, parts=P):
                r, u = slot(group, RING), turn(group, RING)
                if normed:
                    sp.wait_ge(xb_ready[r], u)
                    sp.wait_ge(h_ready[r], u)
                else:
                    sp.wait_ge(out_ready[slot(group, 2)], done(turn(group, 2) - 1))
                sp.dma_start(xin[0:parts, r, :, :].rearrange("p b f -> p (b f)"), rows_of(x_dram, where, parts * BLK)
                             ).then_inc(x_in[r], 16)

            def x_or_tail(group):
                g = node_group(group)
                if g < s.tail_group or (x_dram.shape[0] > s.nodes and g < s.groups):
                    load_x(group, g)
                elif g == s.tail_group and s.tail:
                    load_x(group, g, s.tail // BLK)
                else:
                    load_x(group, 0)

            def overflow(group):
                most = -(-s.edges // (OVER * P))
                n = table(sp, group, 1, most)
                with sp.If(n > 0):
                    first = table(sp, group, 0, s.edges)
                    before = table(sp, group, 2, s.table * most)
                    with sp.Fori(0, n) as i:
                        o = before + i
                        sp.wait_ge(o_rows, o + 1)
                        sp.wait_ge(o_seg, o + 1)
                        if weighted:
                            sp.wait_ge(o_lo, o + 1)
                        at = first + MAIN * P + i * (OVER * P)
                        sp.dma_start(meta_o[:, :, :].rearrange("p c w -> p (c w)"),
                                     records[bass.ds(at, OVER * P), :].rearrange("(p c) w -> p (c w)", c=OVER)
                                     ).then_inc(meta_o_in, 16)

            def store(group, parts=P):
                q, g = slot(group, 2), node_group(group)
                if degree:
                    sp.wait_ge(p_ready[q], turn(group, 2) + 1)
                    sp.dma_start(rows_of(p_dram, g), p_s[:, q, :, :].rearrange("p b f -> p (b f)")).then_inc(p_stored[q], 16)
                sp.wait_ge(out_ready[q], turn(group, 2) + 1)
                sp.dma_start(rows_of(out_dram, g, parts * BLK), o_s[0:parts, q, :, :].rearrange("p b f -> p (b f)")
                             ).then_inc(stored[q], 16)

            def store_if(group):
                if static(group) and number(group) < 0:
                    return
                if static(group) and final and node_group(group) >= s.tail_group:
                    if node_group(group) == s.tail_group and s.tail:
                        store(group, s.tail // BLK)
                    return
                store(group)

            def step(group):
                load_meta(ahead(group, 4))
                load_x(ahead(group, 3), node_group(ahead(group, 3)))
                overflow(group)
                store_if(ahead(group, -LAG))

            def last(group):
                load_meta(ahead(group, 4))
                x_or_tail(ahead(group, 3))
                overflow(group)
                store_if(ahead(group, -LAG))

            for g in range(4):
                load_meta((0, g))
            for g in range(3):
                load_x((0, g), base_group + g)
            quads(sp, step, last)
            for lag in range(LAG - 1, -1, -1):
                store_if(ahead(final_group, -lag))
            full = GROUPS if not final else min(GROUPS, s.tail_group + (s.tail > 0) - base_group)
            for q in range(2):
                n = (full + 1 - q) // 2
                sp.wait_ge(stored[q], 16 * n)
                if degree:
                    sp.wait_ge(p_stored[q], 16 * n)
            for r in range(RING):
                sp.wait_ge(meta_in[r], 16 * ((GROUPS + 4 + RING - 1 - r) // RING))
                sp.wait_ge(x_in[r], 16 * ((GROUPS + 3 + RING - 1 - r) // RING))
                for c in range(MAIN):
                    sp.wait_ge(raw_in[c][r], 16 * ((GROUPS + 3 + RING - 1 - r) // RING))

        bias_of = {"sage1": "b2l", "contrast": "beta", "basis": "bias", "weighted": "v2"}

        @block.gpsimd
        def _(pool):
            pool.memset(zero_s[:, :], 0.0).then_inc(zeroed, 1)
            pool.memset(tick_s[:, 0:1], 0.0).then_inc(tick, 1)
            pool.memset(tick_s[:, 1:2], 0.0).then_inc(o_tick, 1)
            pool.wait_ge(zeroed, 1)
            if degree:
                for pad in (hi[:, :, :, D:D + 2], hi_o[:, :, D:D + 2]):
                    one = pad.bitcast(F32)
                    pool.memset(one[..., 0:1], 1.0)
                    pool.memset(one[..., 1:2], 0.0).then_inc(cleared, 1)
            if kind == "contrast":
                pool.memset(hc[HALF:HALF + 1, :], 1.0).then_inc(cleared, 1)
                pool.wait_ge(cleared, 1)

            def carry(n, sem_):
                pool.wait_ge(sem_, n)
                pool.tensor_tensor(tick_s[:, 0:1], zero_s[:, :], zero_s[:, :], ALU.add).then_inc(sem_, 1)

            def gather(group):
                r, u = slot(group, RING), turn(group, RING)
                pool.wait_ge(meta_in[r], (u + 1) * 16)
                pool.wait_ge(rows_ready[r], u)
                if not normed:
                    pool.wait_ge(lo_ready[r], u)
                if not static(group):
                    carry(number(group) - (RING + 2), tick)
                for c in range(MAIN):
                    pool.indirect_dma_start(raw[:, r, c, :], None, rows_dram,
                                            bass.IndirectOffsetOnAxis(ap=meta[:, r, c, 0:1], axis=0)
                                            ).then_inc(raw_in[c][r], 16)

            def add_bias(group):
                r, q = slot(group, RING), slot(group, 2)
                pool.wait_ge(x_in[r], (turn(group, RING) + 1) * 16)
                pool.wait_ge(out_ready[q], done(turn(group, 2) - (KEEP // 2 - 1)))
                b = k[bias_of[kind]][:, :]
                pool.tensor_tensor(xb[:, slot(group, KEEP), :, :], xin[:, r, :, :], b.unsqueeze(1).to_broadcast([P, BLK, D]), ALU.add
                                   ).then_inc(xb_ready[r], 1)

            def overflow(i, o):
                pool.wait_ge(meta_o_in, (o + 1) * 16)
                pool.wait_ge(o_rows, o + 1)
                if not normed:
                    pool.wait_ge(o_lo, o + 1)
                pool.wait_ge(o_tick, o + 1)
                pool.tensor_tensor(tick_s[:, 1:2], zero_s[:, :], zero_s[:, :], ALU.add).then_inc(o_tick, 1)
                for j in range(OVER):
                    pool.indirect_dma_start(raw_o[:, j, :], None, rows_dram,
                                            bass.IndirectOffsetOnAxis(ap=meta_o[:, j, 0:1], axis=0)
                                            ).then_inc(raw_o_in[j], 16)

            def times_gamma(group):
                pool.wait_ge(dense["n_ready"], number(group) + 1)
                p = ahead(group, -1)
                pool.wait_ge(out_ready[slot(p, 2)], turn(p, 2) + 1)
                pool.tensor_tensor(ng_s[:, :, :], n_s[:, :, :], k["gamma"][:, :].unsqueeze(1).to_broadcast([P, BLK, D]),
                                   ALU.mult).then_inc(dense["ng_ready"], 1)

            def step(group):
                rounds_of(pool, group, overflow)
                gather(ahead(group, 3))
                if normed:
                    add_bias(ahead(group, 1))
                if kind == "contrast" and not very_first(group):
                    times_gamma(ahead(group, -1))

            for g in range(3):
                gather((0, g))
            if normed:
                add_bias((0, 0))
            quads(pool, step)
            if kind == "contrast":
                times_gamma(final_group)

        @block.vector
        def _(dve):
            def ln_moments(group):
                r, g = slot(group, RING), number(group)
                for c in range(MAIN):
                    dve.wait_ge(raw_in[c][r], (turn(group, RING) + 1) * 16)
                dve.wait_ge(x_in[r], (turn(group, RING) + 1) * 16)
                dve.wait_ge(std_ready, g)
                for c in range(cols):
                    of = raw[:, r, c, :] if c < MAIN else xin[:, r, c - MAIN, :]
                    last = dve.bn_stats(st[:, c, :], of)
                last.then_inc(stats, 1)
                dve.wait_ge(stats, g + 1)
                relative(group)
                for c in range(cols):
                    last = dve.bn_aggr(mv[:, c, :], st[:, c, :])
                last.then_inc(moments, 1)

            def ln_coefficients(group):
                q, g = slot(group, 2), number(group)
                dve.wait_ge(std_ready, g + 1)
                p = ahead(group, -2)
                dve.wait_ge(h_ready[slot(p, RING)], turn(p, RING) + 1)
                dve.wait_ge(rows_ready[slot(p, RING)], turn(p, RING) + 1)
                dve.reciprocal(rstd[:, q, :], std[:, :]).then_inc(rstd_ready, 1)
                dve.wait_ge(rstd_ready, g + 1)
                dve.scalar_tensor_tensor(nb[:, q, :], mv[:, :, 0], -1.0, rstd[:, q, :], ALU.mult, ALU.mult).then_inc(coef, 1)

            def relative(group):
                r, q, g = slot(group, RING), slot(group, 2), number(group)
                dve.wait_ge(meta_in[r], (turn(group, RING) + 1) * 16)
                dve.tensor_tensor(rel[:, q, :], mf[:, r, :, 1], k["base"][:, bass.ds(g + base_group, 1)].to_broadcast([P, MAIN]), ALU.subtract
                                  ).then_inc(relset, 1)

            def one_hot(group):
                r, q, g = slot(group, RING), slot(group, 2), number(group)
                if not normed:
                    relative(group)
                dve.wait_ge(relset, g + 1)
                for c in range(MAIN):
                    last = dve.tensor_scalar(S[:, q, c, :], k["iota"][:, :], rel[:, q, c:c + 1], None, ALU.is_equal)
                last.then_inc(seg[r], 1)

            def low_parts(group):
                r, q, g = slot(group, RING), slot(group, 2), number(group)
                dve.wait_ge(rows_ready[r], turn(group, RING) + 1)
                if weighted:
                    for c in range(MAIN):
                        last = dve.scalar_tensor_tensor(lo[:, q, c, :], msg[:, q, c, :], mf[:, r, c, 2:3], hi[:, q, c, 0:D].bitcast(F32),
                                                        ALU.mult, ALU.subtract)
                    last.then_inc(lo_ready[r], 1)
                    return
                of = msg[:, q, :, :] if normed else raw[:, r, :, :]
                dve.tensor_tensor(lo[:, q, :, :], of, hi[:, q, :, 0:D].bitcast(F32), ALU.subtract).then_inc(lo_ready[r], 1)

            def overflow(group):
                g = node_group(group)

                def relative_over(o):
                    dve.wait_ge(meta_o_in, (o + 1) * 16)
                    dve.tensor_tensor(rel_o[:, :], mof[:, :, 1], k["base"][:, bass.ds(g, 1)].to_broadcast([P, OVER]), ALU.subtract
                                      ).then_inc(o_rel, 1)

                def body(i, o):
                    if normed:
                        for j in range(OVER):
                            dve.wait_ge(raw_o_in[j], (o + 1) * 16)
                            last = dve.bn_stats(st_o[:, j, :], raw_o[:, j, :])
                        last.then_inc(o_stats, 1)
                        dve.wait_ge(o_stats, o + 1)
                        relative_over(o)
                        for j in range(OVER):
                            last = dve.bn_aggr(mv_o[:, j, :], st_o[:, j, :])
                        last.then_inc(o_moments, 1)
                    else:
                        relative_over(o)
                    dve.wait_ge(o_agg, o + 1)
                    dve.wait_ge(o_rel, o + 1)
                    for j in range(OVER):
                        last = dve.tensor_scalar(S_o[:, j, :], k["iota"][:, :], rel_o[:, j:j + 1], None, ALU.is_equal)
                    last.then_inc(o_seg, 1)
                    if normed:
                        dve.wait_ge(o_std, o + 1)
                        dve.wait_ge(o_rows, o + 1)
                        dve.reciprocal(rstd_o[:, :], std_o[:, :]).then_inc(o_rstd, 1)
                        dve.wait_ge(o_rstd, o + 1)
                        dve.scalar_tensor_tensor(nb_o[:, :], mv_o[:, :, 0], -1.0, rstd_o[:, :], ALU.mult, ALU.mult).then_inc(o_coef, 1)
                    dve.wait_ge(o_rows, o + 2)
                    if weighted:
                        for j in range(OVER):
                            last = dve.scalar_tensor_tensor(lo_o[:, j, :], msg_o[:, j, :], mof[:, j, 2:3], hi_o[:, j, 0:D].bitcast(F32),
                                                            ALU.mult, ALU.subtract)
                        last.then_inc(o_lo, 1)
                        return
                    of = msg_o[:, :, :] if normed else raw_o[:, :, :]
                    dve.tensor_tensor(lo_o[:, :, :], of, hi_o[:, :, 0:D].bitcast(F32), ALU.subtract).then_inc(o_lo, 1)

                rounds_of(dve, group, body)

            def prepare(group):
                w, need = before(group)
                dve.wait_ge(agg_done[w], need)
                one_hot(group)
                low_parts(group)

            def out_sum(group):
                q = slot(group, 2)
                if kind == "contrast":
                    dve.wait_ge(dense["ng_ready"], number(group) + 1)
                    term = ng_s[:, :, :]
                else:
                    dve.wait_ge(dense["out_psum"], number(group) + 1)
                    term = (outp[:, GROUP:2 * GROUP] if kind == "sage1" else outp[:, :]).rearrange("p (b c) -> p b c", b=BLK)
                dve.wait_ge(stored[q], turn(group, 2) * 16)
                dve.wait_ge(xb_ready[slot(group, RING)], turn(group, RING) + 1)
                dve.tensor_tensor(o_s[:, q, :, :], term, xb[:, slot(group, KEEP), :, :], ALU.add).then_inc(out_ready[q], 1)

            def copy_hT(group, read):
                dve.wait_ge(dense["hT_psum"], number(group) + 1)
                dve.wait_ge(dense[read], number(group))
                dve.tensor_copy(hT[:, :], tr[:, 0:GROUP]).then_inc(dense["hT_ready"], 1)

            def degree_mean(group):
                g = number(group)
                dve.wait_ge(agg_done[slot(group, RING)], turn(group, RING) + 1)
                dve.tensor_scalar(deg[:, :].rearrange("p (k j) -> p k j", k=2), sums[:, :, :, D], 1.0, None, ALU.max
                                  ).then_inc(dense["deg_max"], 1)
                dve.wait_ge(dense["deg_max"], g + 1)
                dve.reciprocal(k["inv"][:, bass.ds(node_group(group) * BLK, BLK)], deg[:, :])
                dve.reciprocal(invg[:, :], deg[:, :]).then_inc(dense["inv_done"], 1)
                dve.wait_ge(dense["inv_done"], g + 1)
                dve.wait_ge(dense["mT_psum"], g)
                dve.tensor_tensor(mean[:, :, :].rearrange("p (k j) f -> p k j f", k=2), sums[:, :, :, 0:D],
                                  invg[:, :].rearrange("p (k j) -> p k j", k=2).unsqueeze(3).to_broadcast([P, 2, 2, D]), ALU.mult
                                  ).then_inc(dense["mean_ready"], 1)

            def inverse_degree(group):
                dve.tensor_copy(invg[:, :], k["inv"][:, bass.ds(node_group(group) * BLK, BLK)]).then_inc(dense["inv_copied"], 1)
                dve.wait_ge(dense["inv_copied"], number(group) + 1)

            def neighbour_difference(group):
                inverse_degree(group)
                dve.wait_ge(agg_done[slot(group, RING)], turn(group, RING) + 1)
                dve.wait_ge(dense["sq_done"], number(group))
                for b in range(BLK):
                    last = dve.scalar_tensor_tensor(diff[:, b, :], agg[:, b * D:(b + 1) * D], invg[:, b:b + 1],
                                                    h[:, slot(group, KEEP), b, :], ALU.mult, ALU.subtract)
                last.then_inc(dense["diff_done"], 1)

            def square_sum(group):
                g = number(group)
                dve.wait_ge(dense["sq_done"], g + 1)
                dve.wait_ge(dense["norm_done"], g)
                dve.tensor_reduce(ssq[:, :], sq[:, :, :], AX.X, ALU.add).then_inc(dense["ssq_done"], 1)

            def enhance(group):
                g = number(group)
                dve.wait_ge(dense["tanh_done"], g + 1)
                dve.tensor_scalar(ta[:, :], th[:, :], ALPHA, None, ALU.mult).then_inc(dense["ta_done"], 1)
                dve.wait_ge(dense["ta_done"], g + 1)
                dve.wait_ge(dense["out_psum"], g + 1)
                dve.wait_ge(dense["n_ready"], g)
                for b in range(BLK):
                    last = dve.scalar_tensor_tensor(e_s[:, b, :], outp[:, b * D:(b + 1) * D], ta[:, b:b + 1],
                                                    h[:, slot(group, KEEP), b, :], ALU.mult, ALU.add)
                last.then_inc(dense["e_done"], 1)
                dve.wait_ge(dense["e_done"], g + 1)
                dve.wait_ge(dense["mv2_done"], g)
                for b in range(BLK):
                    last = dve.bn_stats(st2[:, b, :], e_s[:, b, :])
                last.then_inc(dense["st2_done"], 1)
                dve.wait_ge(dense["st2_done"], g + 1)

            def enhanced_moments(group):
                for b in range(BLK):
                    last = dve.bn_aggr(mv2[:, b, :], st2[:, b, :])
                last.then_inc(dense["mv2_done"], 1)

            def enhanced_coefficients(group):
                g = number(group)
                dve.wait_ge(dense["std2_done"], g + 1)
                dve.reciprocal(rstd2[:, :], std2[:, :]).then_inc(dense["rstd2_done"], 1)
                dve.wait_ge(dense["rstd2_done"], g + 1)
                dve.scalar_tensor_tensor(nb2[:, :], mv2[:, :, 0], -1.0, rstd2[:, :], ALU.mult, ALU.mult).then_inc(dense["coef2"], 1)

            def step(group):
                g, q, r = number(group), slot(group, 2), slot(group, RING)
                d = dense
                prev = None if very_first(group) else ahead(group, -1)
                overflow(group)
                if normed:
                    ln_moments(ahead(group, 2))
                if kind == "sage1":
                    degree_mean(group)
                    copy_hT(group, "hid_b")
                    ln_coefficients(ahead(group, 2))
                    prepare(ahead(group, 1))
                    if prev:
                        out_sum(prev)
                if kind == "sage2":
                    prepare(ahead(group, 1))
                    inverse_degree(group)
                    dve.wait_ge(agg_done[r], turn(group, RING) + 1)
                    dve.wait_ge(x_in[r], (turn(group, RING) + 1) * 16)
                    dve.wait_ge(stored[q], turn(group, 2) * 16)
                    for b in range(BLK):
                        last = dve.scalar_tensor_tensor(o_s[:, q, b, :], agg[:, b * D:(b + 1) * D], invg[:, b:b + 1],
                                                        xin[:, r, b, :], ALU.mult, ALU.add)
                    last.then_inc(out_ready[q], 1)
                if kind == "contrast":
                    if not (static(group) and number(group) < 2):
                        out_sum(ahead(group, -2))
                    neighbour_difference(group)
                    copy_hT(group, "hid_psum")
                    if prev:
                        enhance(prev)
                    square_sum(group)
                    if prev:
                        enhanced_moments(prev)
                    prepare(ahead(group, 1))
                    ln_coefficients(ahead(group, 2))
                    if prev:
                        enhanced_coefficients(prev)
                if kind == "basis":
                    if prev:
                        out_sum(prev)
                    copy_hT(group, "out_psum")
                    dve.wait_ge(agg_done[r], turn(group, RING) + 1)
                    dve.tensor_copy(aT[:, :], agg[:, :]).then_inc(d["aT_ready"], 1)
                    ln_coefficients(ahead(group, 2))
                    prepare(ahead(group, 1))
                if kind == "weighted":
                    if prev:
                        out_sum(prev)
                    dve.wait_ge(agg_done[r], turn(group, RING) + 1)
                    dve.wait_ge(d["hid_psum"], g)
                    dve.tensor_copy(zT[:, :], agg[:, :]).then_inc(d["zT_ready"], 1)
                    ln_coefficients(ahead(group, 2))
                    prepare(ahead(group, 1))

            dve.sem_inc(o_seg, 1)
            dve.sem_inc(o_lo, 1)
            dve.sem_inc(o_coef, 1)
            if degree:
                dve.wait_ge(cleared, 2)
            if normed:
                for g in range(2):
                    ln_moments((0, g))
                    ln_coefficients((0, g))
            prepare((0, 0))
            quads(dve, step)
            if kind == "contrast":
                out_sum(ahead(final_group, -1))
                enhance(final_group)
                enhanced_moments(final_group)
                enhanced_coefficients(final_group)
            if LAG:
                out_sum(final_group)

        @block.scalar
        def _(act):
            def ln_std(group):
                g = number(group)
                act.wait_ge(moments, g + 1)
                act.wait_ge(rstd_ready, g)
                act.activation(std[:, :], mv[:, :, 1], ACT.Sqrt, bias=k["eps"][:, 0:1]).then_inc(std_ready, 1)

            def normal_rows(to, hi_to, of, bias, scale, weight, ready, count):
                ins = act.activation(to, of, ACT.Relu, bias=bias, scale=scale)
                if weighted:
                    ins.then_inc(ready, 1)
                    act.wait_ge(ready, count)
                    return act.activation(hi_to, to, ACT.Copy, scale=weight)
                return act.activation(hi_to, of, ACT.Relu, bias=bias, scale=scale)

            def rows(group):
                r, q, g = slot(group, RING), slot(group, 2), number(group)
                w, need = before(group)
                act.wait_ge(agg_done[w], need)
                if weighted:
                    p = ahead(group, -2)
                    act.wait_ge(lo_ready[slot(p, RING)], turn(p, RING) + 1)
                if normed:
                    act.wait_ge(coef, g + 1)
                    for c in range(MAIN):
                        last = normal_rows(msg[:, q, c, :], hi[:, q, c, 0:D], raw[:, r, c, :], nb[:, q, c:c + 1], rstd[:, q, c:c + 1],
                                           mf[:, r, c, 2:3], unweighted, g * MAIN + c + 1)
                else:
                    for c in range(MAIN):
                        act.wait_ge(raw_in[c][r], (turn(group, RING) + 1) * 16)
                    last = act.activation(hi[:, q, :, 0:D], raw[:, r, :, :], ACT.Copy)
                last.then_inc(rows_ready[r], 1)

            def own(group):
                r, q, g = slot(group, RING), slot(group, 2), number(group)
                act.wait_ge(coef, g + 1)
                if kind == "contrast":
                    act.wait_ge(dense["e_done"], done(g - 3))
                elif kind == "weighted":
                    w, need = before(group)
                    act.wait_ge(agg_done[w], need)
                if kind != "weighted":
                    act.wait_ge(dense["hT_psum"], done(g - KEEP + 1))
                for b in range(BLK):
                    c = MAIN + b
                    last = act.activation(h[:, slot(group, KEEP), b, :], xin[:, r, b, :], ACT.Relu, bias=nb[:, q, c:c + 1], scale=rstd[:, q, c:c + 1])
                last.then_inc(h_ready[r], 1)

            def overflow(i, o):
                if normed:
                    act.wait_ge(o_moments, o + 1)
                    act.wait_ge(o_coef, o + 1)
                    act.activation(std_o[:, :], mv_o[:, :, 1], ACT.Sqrt, bias=k["eps"][:, 0:1]).then_inc(o_std, 1)
                    act.wait_ge(o_coef, o + 2)
                act.wait_ge(o_agg, o + 1)
                if weighted:
                    act.wait_ge(o_lo, o + 1)
                if normed:
                    for j in range(OVER):
                        last = normal_rows(msg_o[:, j, :], hi_o[:, j, 0:D], raw_o[:, j, :], nb_o[:, j:j + 1], rstd_o[:, j:j + 1],
                                           mof[:, j, 2:3], o_unweighted, o * OVER + j + 1)
                else:
                    for j in range(OVER):
                        act.wait_ge(raw_o_in[j], (o + 1) * 16)
                    last = act.activation(hi_o[:, :, 0:D], raw_o[:, :, :], ACT.Copy)
                last.then_inc(o_rows, 1)

            def projection(group):
                q = slot(group, 2)
                act.wait_ge(dense["out_psum"], number(group) + 1)
                act.wait_ge(p_stored[q], turn(group, 2) * 16)
                op = outp[:, 0:GROUP].rearrange("p (b c) -> p b c", b=BLK)
                act.activation(p_s[:, q, :, :], op, ACT.Copy).then_inc(p_ready[q], 1)

            def enhanced_std(group):
                g = number(group)
                act.wait_ge(dense["mv2_done"], g + 1)
                act.wait_ge(dense["rstd2_done"], g)
                act.activation(std2[:, :], mv2[:, :, 1], ACT.Sqrt, bias=k["eps"][:, 0:1]).then_inc(dense["std2_done"], 1)

            def enhanced_norm(group):
                g = number(group)
                act.wait_ge(dense["coef2"], g + 1)
                act.wait_ge(dense["ng_ready"], g)
                for b in range(BLK):
                    last = act.activation(n_s[:, b, :], e_s[:, b, :], ACT.Identity, bias=nb2[:, b:b + 1], scale=rstd2[:, b:b + 1])
                last.then_inc(dense["n_ready"], 1)

            def step(group):
                g, q = number(group), slot(group, 2)
                d = dense
                nxt, prev = ahead(group, 1), None if very_first(group) else ahead(group, -1)
                rounds_of(act, group, overflow)
                rows(nxt)
                if kind == "sage1":
                    ln_std(ahead(group, 2))
                    own(nxt)
                    if prev:
                        projection(prev)
                    act.wait_ge(d["mT_psum"], g + 1)
                    act.wait_ge(d["hid_b"], g)
                    act.activation(mT[:, :], tr[:, GROUP:2 * GROUP], ACT.Copy).then_inc(d["mT_ready"], 1)
                    for m, (psum, ready) in enumerate((("hid_a", "HT_a"), ("hid_b", "HT_b"))):
                        act.wait_ge(d[psum], g + 1)
                        act.wait_ge(d["out_psum"], g)
                        act.activation(HT[:, m, :], hid[:, m * 512:(m + 1) * 512], ACT.Relu, bias=k["b1l"][:, m:m + 1]).then_inc(d[ready], 1)
                if kind == "contrast":
                    act.wait_ge(d["diff_done"], g + 1)
                    act.wait_ge(d["ssq_done"], g)
                    act.activation(sq[:, :, :], diff[:, :, :], ACT.Square).then_inc(d["sq_done"], 1)
                    act.wait_ge(d["hid_psum"], g + 1)
                    act.wait_ge(d["out_psum"], g)
                    act.activation(hc[0:HALF, :], hid[0:HALF, :], ACT.Relu, bias=k["c1"][:, 0:1]).then_inc(d["hc_ready"], 1)
                    own(nxt)
                    ln_std(ahead(group, 2))
                    act.wait_ge(d["ssq_done"], g + 1)
                    act.activation(nrm[:, :], ssq[:, :], ACT.Sqrt).then_inc(d["norm_done"], 1)
                    if prev:
                        enhanced_std(prev)
                    act.wait_ge(d["norm_done"], g + 1)
                    act.wait_ge(d["ta_done"], g)
                    act.activation(th[:, :], nrm[:, :], ACT.Tanh).then_inc(d["tanh_done"], 1)
                    if prev:
                        enhanced_norm(prev)
                if kind == "basis":
                    ln_std(ahead(group, 2))
                    own(nxt)
                if kind == "weighted":
                    ln_std(ahead(group, 2))
                    act.wait_ge(d["hid_psum"], g + 1)
                    act.wait_ge(d["out_psum"], g)
                    act.activation(gT[:, :], hid[:, :], ACT.Relu, bias=k["v1"][:, 0:1]).then_inc(d["gT_ready"], 1)
                    own(nxt)

            act.sem_inc(o_rows, 1)
            if normed:
                ln_std((0, 0))
                ln_std((0, 1))
                own((0, 0))
            rows((0, 0))
            quads(act, step)
            if kind == "sage1":
                projection(final_group)
            if kind == "contrast":
                enhanced_std(final_group)
                enhanced_norm(final_group)

        @block.tensor
        def _(pe):
            def sum_chunk(S_c, hi_c, lo_c, first, last):
                if node_major:
                    for b in range(BLK):
                        W_ = S_c[:, b * P:(b + 1) * P]
                        if degree:
                            at = (b // 2) * 512 + (b % 2) * width
                            one = first and b % 2 == 0
                        else:
                            at = b * D
                            one = first and b == 0
                        pe.matmul(agg[:, at:at + width], W_, hi_c[:, 0:width], start=one, stop=False, skip_group_check=True)
                        ins = pe.matmul(agg[:, at:at + D], W_, lo_c, start=False, stop=last, skip_group_check=True)
                else:
                    pe.matmul(agg[:, :], hi_c, S_c, start=first, stop=False, skip_group_check=True)
                    ins = pe.matmul(agg[:, :], lo_c, S_c, start=False, stop=last, skip_group_check=True)
                return ins

            def overflow(i, o):
                pe.wait_ge(o_lo, o + 2)
                pe.wait_ge(o_seg, o + 2)
                for j in range(OVER):
                    ins = sum_chunk(S_o[:, j, :], hi_o[:, j, :], lo_o[:, j, :], False, False)
                ins.then_inc(o_agg, 1)

            def transposes(psum, of):
                for b in range(BLK):
                    ins = pe.transpose(psum[:, b * P:(b + 1) * P], of[:, b, :], k["ident"][:, :])
                return ins

            def outputs(group):
                g, prev = number(group), ahead(group, -1)
                pe.wait_ge(dense["HT_a"], g + 1)
                pe.wait_ge(dense["HT_b"], g + 1)
                pe.wait_ge(out_ready[slot(prev, 2)], turn(prev, 2) + 1)
                pe.wait_ge(p_ready[slot(prev, 2)], turn(prev, 2) + 1)
                for half in range(2):
                    for b in range(BLK):
                        at = half * GROUP + b * D
                        for m in range(2):
                            ins = pe.matmul(outp[:, at:at + D], HT[:, m, b * P:(b + 1) * P],
                                            k["W2"][:, m, half * D:(half + 1) * D], start=m == 0, stop=m == 1)
                ins.then_inc(dense["out_psum"], 1)

            def step(group):
                g, q, r = number(group), slot(group, 2), slot(group, RING)
                d = dense
                pe.wait_ge(lo_ready[r], turn(group, RING) + 1)
                pe.wait_ge(seg[r], turn(group, RING) + 1)
                if kind == "sage1":
                    pe.wait_ge(d["mean_ready"], g)
                elif kind == "basis":
                    pe.wait_ge(d["aT_ready"], g)
                elif kind == "weighted":
                    pe.wait_ge(d["zT_ready"], g)
                elif kind == "contrast":
                    pe.wait_ge(d["diff_done"], g)
                else:
                    pe.wait_ge(out_ready[(q + 1) % 2], turn(ahead(group, 1), 2))
                sum_chunk(S[:, q, 0, :], hi[:, q, 0, :], lo[:, q, 0, :], True, False)
                rounds_of(pe, group, overflow)
                if kind == "weighted":
                    for c in range(1, MAIN):
                        sum_chunk(S[:, q, c, :], hi[:, q, c, :], lo[:, q, c, :], False, False)
                    pe.wait_ge(h_ready[r], turn(group, RING) + 1)
                    for b in range(BLK):
                        ins = pe.matmul(agg[:, b * P:(b + 1) * P], h[:, q, b, :], k["ident"][:, :], start=False, stop=b == BLK - 1,
                                        skip_group_check=True)
                    ins.then_inc(agg_done[r], 1)
                    pe.wait_ge(d["zT_ready"], g + 1)
                    pe.wait_ge(d["gT_ready"], g)
                    pe.matmul(hid[:, :], k["V1"][:, :], zT[:, :], start=True, stop=True).then_inc(d["hid_psum"], 1)
                    pe.wait_ge(d["gT_ready"], g + 1)
                    pe.wait_ge(out_ready[(q + 1) % 2], turn(ahead(group, 1), 2))
                    for b in range(BLK):
                        ins = pe.matmul(outp[:, b * D:(b + 1) * D], gT[:, b * P:(b + 1) * P], k["V2"][:, :], start=True, stop=True)
                    ins.then_inc(d["out_psum"], 1)
                    return
                for c in range(1, MAIN):
                    ins = sum_chunk(S[:, q, c, :], hi[:, q, c, :], lo[:, q, c, :], False, c == MAIN - 1)
                ins.then_inc(agg_done[r], 1)
                if kind == "sage2":
                    return
                pe.wait_ge(h_ready[r], turn(group, RING) + 1)
                pe.wait_ge(d["hT_ready"], g)
                transposes(tr[:, 0:GROUP], h[:, slot(group, KEEP), :, :]).then_inc(d["hT_psum"], 1)
                if kind == "sage1":
                    if not very_first(group):
                        outputs(ahead(group, -1))
                    pe.wait_ge(d["mean_ready"], g + 1)
                    pe.wait_ge(d["mT_ready"], g)
                    transposes(tr[:, GROUP:2 * GROUP], mean[:, :, :]).then_inc(d["mT_psum"], 1)
                    pe.wait_ge(d["hT_ready"], g + 1)
                    pe.wait_ge(d["HT_b"], g)
                    for m in range(2):
                        pe.matmul(hid[:, m * 512:(m + 1) * 512], k["W1r"][:, m * P:(m + 1) * P], hT[:, :], start=True, stop=False)
                    pe.wait_ge(d["mT_ready"], g + 1)
                    for m, name in enumerate(("hid_a", "hid_b")):
                        pe.matmul(hid[:, m * 512:(m + 1) * 512], k["W1l"][:, m * P:(m + 1) * P], mT[:, :], start=False, stop=True
                                  ).then_inc(d[name], 1)
                if kind == "contrast":
                    pe.wait_ge(d["hT_ready"], g + 1)
                    pe.wait_ge(d["hc_ready"], g)
                    pe.matmul(hid[0:HALF, :], k["C1"][:, :], hT[:, :], start=True, stop=True).then_inc(d["hid_psum"], 1)
                    pe.wait_ge(d["hc_ready"], g + 1)
                    pe.wait_ge(cleared, 1)
                    pe.wait_ge(d["e_done"], g)
                    for b in range(BLK):
                        ins = pe.matmul(outp[:, b * D:(b + 1) * D], hc[:, b * P:(b + 1) * P], k["C2"][:, :], start=True, stop=True)
                    ins.then_inc(d["out_psum"], 1)
                if kind == "basis":
                    pe.wait_ge(d["hT_ready"], g + 1)
                    pe.wait_ge(d["aT_ready"], g + 1)
                    pe.wait_ge(out_ready[(q + 1) % 2], turn(ahead(group, 1), 2))
                    for b in range(BLK):
                        pe.matmul(outp[:, b * D:(b + 1) * D], hT[:, b * P:(b + 1) * P], k["root"][:, :], start=True, stop=False)
                        ins = pe.matmul(outp[:, b * D:(b + 1) * D], aT[:, b * P:(b + 1) * P], k["W"][:, :], start=False, stop=True)
                    ins.then_inc(d["out_psum"], 1)

            pe.sem_inc(o_agg, 1)
            quads(pe, step)
            if kind == "sage1":
                outputs(final_group)

        passed.close()
        nc.clear_and_free_semaphores(made)
        nc.all_engine_barrier()


def kernel(**inputs):
    import numpy as np
    import concourse.bacc as bacc
    from concourse import mybir as mb
    from concourse.bass_utils import run_bass_kernel_spmd as run

    a = {n: np.asarray(v) for n, v in inputs.items()}

    def rows(v):
        return np.ascontiguousarray(np.broadcast_to(v.reshape(1, -1), (128, v.size)))

    given = [
        ("x", a["x"]), ("src", a["src"]), ("dst", a["dst"]), ("edge_weight", a["edge_weight"]),
        ("W1l", a["L0_gnn_W1l"].T), ("b1l", a["L0_gnn_b1l"].reshape(2, 128).T), ("W1r", a["L0_gnn_W1r"].T),
        ("W2cat", np.concatenate([a["L0_gnn_W2l"].T, a["L0_gnn_W2r"].T], axis=1)), ("b2l", rows(a["L0_gnn_b2l"])),
        ("C1", a["L1_gnn_W1"]), ("c1", a["L1_gnn_b1"].reshape(-1, 1)), ("C2", a["L1_gnn_W2"]),
        ("c2", a["L1_gnn_b2"].reshape(1, -1)), ("gamma", rows(a["L1_gnn_gamma"])), ("beta", rows(a["L1_gnn_beta"])),
        ("bases", a["L2_gnn_bases"]), ("comp", rows(a["L2_gnn_comp"])), ("root", a["L2_gnn_root"]),
        ("bias", rows(a["L2_gnn_bias"])), ("V1", a["L3_gnn_W1"]), ("v1", a["L3_gnn_b1"].reshape(-1, 1)),
        ("V2", a["L3_gnn_W2"]), ("v2", rows(a["L3_gnn_b2"])),
    ]
    nc = bacc.Bacc("TRN2", target_bir_lowering=False, num_devices=1)
    arrays, args = {}, []
    for name, v in given:
        v = np.ascontiguousarray(v)
        arrays[f"in_{name}"] = v
        args.append(nc.dram_tensor(f"in_{name}", v.shape, mb.dt.from_np(v.dtype), kind="ExternalInput").ap())
    out = nc.dram_tensor("out_x", a["x"].shape, mb.dt.from_np(np.dtype("float32")), kind="ExternalOutput").ap()
    gnn_kernel(nc, *args, out)
    r = run(nc, [arrays], core_ids=[0])
    return r.results[0]["out_x"]
```

```python
import concourse.bass as bass
from concourse import mybir
from contextlib import ExitStack

P = 128
D = 128
HID = 256
HALF = 64
BLK = 4
GROUP = P * BLK
CHUNKS = (12, 5, 2)
MAX_MAIN = CHUNKS[0]
OVER = 8
RING = 4
EPS = 1e-5
ALPHA = 0.2
REC = 4

F32 = mybir.dt.float32
F32R = mybir.dt.float32r
I32 = mybir.dt.int32
ALU = mybir.AluOpType
ACT = mybir.ActivationFunctionType
AX = mybir.AxisListType


def slot(group, ring):
    return group[1] % ring


def turn(group, ring):
    t, k = group
    return t * (RING // ring) + k // ring


def number(group):
    return group[0] * RING + group[1]


def before(group):
    return (group[1] - 2) % RING, group[0] + (group[1] - 2) // RING + 1


def static(group):
    return isinstance(group[0], int)


def very_first(group):
    return static(group) and number(group) == 0


def ahead(group, n):
    return (group[0], group[1] + n)


class Shape:

    def __init__(self, nodes, edges):
        self.nodes, self.edges = nodes, edges
        self.groups = -(-nodes // (GROUP * RING)) * RING
        self.tail_group = nodes // GROUP
        self.tail = nodes - self.tail_group * GROUP
        self.padded = self.groups * GROUP
        self.per_part = -(-(edges + 1 + MAX_MAIN * P + OVER * P) // P)
        while edges % self.per_part:
            self.per_part += 1
        self.edge_parts = edges // self.per_part
        self.table = self.groups + RING + 2
        cuts = [c for c in (RING * (self.groups // 96), RING * (self.groups * 20 // 256)) if c >= 2 * RING]
        cuts = [0] + cuts + [self.groups]
        self.spans = [(a, b, m) for a, b, m in zip(cuts, cuts[1:], CHUNKS[-len(cuts) + 1:])]


def gnn_kernel(nc, x, src, dst, edge_weight, W1l, b1l, W1r, W2cat, b2l, C1, c1, C2, c2, gamma, beta,
               bases, comp, root, bias, V1, v1, V2, v2, out):
    s = Shape(x.shape[0], src.shape[0])
    assert s.edge_parts <= P and P * s.per_part >= s.edges + (MAX_MAIN + OVER) * P and s.tail % BLK == 0

    records = nc.dram_tensor("edge_records", [P * s.per_part + s.edges + OVER * P, REC], I32).ap()
    y_dram = nc.dram_tensor("sage_partial", [s.padded, D], F32).ap()
    p_dram = nc.dram_tensor("sage_projected", [s.padded, D], F32).ap()
    x1_dram = nc.dram_tensor("x_after_sage", [s.padded, D], F32).ap()
    x2_dram = nc.dram_tensor("x_after_contrast", [s.padded, D], F32).ap()
    x3_dram = nc.dram_tensor("x_after_basis", [s.padded, D], F32).ap()

    with ExitStack() as ctx:
        def sb(name, shape, dt=F32):
            return ctx.enter_context(nc.sbuf_tensor(name, shape, dt))

        k = {}
        k["table"] = sb("group_table", [1, s.table * REC], I32)
        k["base"] = sb("group_base", [P, s.table])
        k["iota"] = sb("node_of_column", [P, GROUP])
        k["ident"] = sb("identity", [P, P])
        k["eps"] = sb("eps", [P, 1])
        k["inv"] = sb("inverse_degree", [P, s.groups * BLK])
        k["W1l"] = sb("W1l_s", [P, HID])
        k["W1r"] = sb("W1r_s", [P, HID])
        k["b1l"] = sb("b1l_s", [P, 2])
        k["W2"] = sb("W2_s", [P, 2, 2 * D])
        k["b2l"] = sb("b2l_s", [P, D])
        k["C1"] = sb("C1_s", [P, HALF])
        k["c1"] = sb("c1_s", [HALF, 1])
        k["C2"] = sb("C2_s", [HALF + 1, D])
        k["gamma"] = sb("gamma_s", [P, D])
        k["beta"] = sb("beta_s", [P, D])
        k["W"] = sb("basis_W", [P, D])
        k["root"] = sb("root_s", [P, D])
        k["bias"] = sb("bias_s", [P, D])
        k["V1"] = sb("V1_s", [P, D])
        k["v1"] = sb("v1_s", [P, 1])
        k["V2"] = sb("V2_s", [P, D])
        k["v2"] = sb("v2_s", [P, D])

        setup(nc, s, k, src, dst, edge_weight, W1l, b1l, W1r, W2cat, b2l, C1, c1, C2, c2, gamma, beta,
              bases, comp, root, bias, V1, v1, V2, v2, records)
        for kind, x_of, rows, to, projected in (
                ("sage1", x, x, y_dram, p_dram), ("sage2", y_dram, p_dram, x1_dram, None),
                ("contrast", x1_dram, x1_dram, x2_dram, None), ("basis", x2_dram, x2_dram, x3_dram, None),
                ("weighted", x3_dram, x3_dram, out, None)):
            for span in s.spans:
                node_pass(nc, s, k, kind, span, records, x_of, rows, to, projected)


def setup(nc, s, k, src, dst, edge_weight, W1l, b1l, W1r, W2cat, b2l, C1, c1, C2, c2, gamma, beta,
          bases, comp, root, bias, V1, v1, V2, v2, records):
    E, J, T = s.edges, s.per_part, s.table
    with ExitStack() as ctx:
        def sb(name, shape, dt=F32):
            return ctx.enter_context(nc.sbuf_tensor(name, shape, dt))

        def sem(name):
            return ctx.enter_context(nc.semaphore("setup_" + name))

        src_i = sb("src_i", [P, J], I32)
        dst_i = sb("dst_i", [P, J], I32)
        next_i = sb("next_i", [P, J], I32)
        w_in = sb("w_in", [P, J])
        dst_f = sb("dst_f", [P, J])
        next_f = sb("next_f", [P, J])
        rec = sb("rec", [P, J, REC], I32)
        base_i = sb("base_i", [P, T], I32)
        iota_i = sb("iota_i", [P, GROUP], I32)
        below = sb("below", [P, T + 1])
        hit = sb("hit", [P, J])
        ones = sb("ones", [P, 1])
        bases_s = sb("bases_s", [P, 8, D])
        comp_s = sb("comp_s", [P, 8])
        w_acc = sb("w_acc", [P, 2, D])
        bound = sb("bound", [1, T + 1])
        unsorted = sb("unsorted", [1, 1])
        lo_f = sb("lo_f", [1, T])
        count_f = sb("count_f", [1, T])
        rounds_i = sb("rounds_i", [1, T], I32)
        rounds_f = sb("rounds_f", [1, T + 1])
        zero_f = sb("zero_f", [1, T + 1])
        prefix_f = sb("prefix_f", [1, T + 1])
        sums = ctx.enter_context(nc.psum_tensor("bound_sums", [1, 512], F32))

        edges_in = sem("edges_in")
        consts_in = sem("consts_in")
        records_out = sem("records_out")
        cleared = sem("cleared")
        iotas = sem("iotas")
        step = sem("vector_step")
        counted = sem("counted")
        summed = sem("summed")
        built = sem("records_built")

        n_edge_loads = 5 if s.edge_parts > 1 else 4
        consts = [(k["W1l"][:, :], W1l), (k["W1r"][:, :], W1r), (k["b1l"][:, :], b1l),
                  (k["W2"][:, 0, :], W2cat[0:P, :]), (k["W2"][:, 1, :], W2cat[P:HID, :]), (k["b2l"][:, :], b2l),
                  (k["C1"][:, :], C1), (k["c1"][:, :], c1), (k["C2"][0:HALF, :], C2),
                  (k["C2"][HALF:HALF + 1, :], c2), (k["gamma"][:, :], gamma), (k["beta"][:, :], beta),
                  (k["root"][:, :], root), (k["bias"][:, :], bias), (k["V1"][:, :], V1), (k["v1"][:, :], v1),
                  (k["V2"][:, :], V2), (k["v2"][:, :], v2), (comp_s[:, :], comp),
                  (bases_s[:, :, :], bases.rearrange("b i o -> i b o"))]
        block = ctx.enter_context(nc.Block())

        @block.sync
        def _(sp):
            def rows(a, n):
                return a[0:n * J].rearrange("(p j) -> p j", j=J)

            Q = s.edge_parts
            sp.wait_ge(cleared, 3)
            sp.dma_start(src_i[0:Q, :], rows(src, Q)).then_inc(edges_in, 16)
            sp.dma_start(dst_i[0:Q, :], rows(dst, Q)).then_inc(edges_in, 16)
            sp.dma_start(w_in[0:Q, :], rows(edge_weight, Q)).then_inc(edges_in, 16)
            sp.dma_start(next_i[0:Q - 1, :], dst[1:(Q - 1) * J + 1].rearrange("(p j) -> p j", j=J)).then_inc(edges_in, 16)
            sp.dma_start(next_i[Q - 1:Q, 0:J - 1], dst[(Q - 1) * J + 1:E].rearrange("(a j) -> a j", a=1)).then_inc(edges_in, 16)
            sp.wait_ge(built, 1)
            sp.dma_start(records[0:P * J, :].rearrange("(p j) c -> p (j c)", j=J), rec[:, :, :].rearrange("p j c -> p (j c)")).then_inc(records_out, 16)
            sp.wait_ge(records_out, 16)

        @block.scalar
        def _(act):
            for to, of in consts:
                act.dma_start(to, of).then_inc(consts_in, 16)
            act.wait_ge(consts_in, 16 * len(consts))

        @block.gpsimd
        def _(pool):
            pool.memset(src_i[:, :], 0)
            pool.memset(w_in[:, :], 0.0)
            pool.memset(dst_i[:, :], 1 << 23).then_inc(cleared, 1)
            pool.memset(next_i[:, :], 1 << 23).then_inc(cleared, 1)
            pool.memset(rec[:, :, :], 0).then_inc(cleared, 1)
            pool.memset(k["ident"][:, :], 0.0).then_inc(iotas, 1)
            pool.wait_ge(iotas, 1)
            pool.affine_select(out=k["ident"][:, :], in_=k["ident"][:, :], compare_op=ALU.not_equal, fill=1.0,
                               base=0, pattern=[[-1, P]], channel_multiplier=1)
            pool.memset(k["eps"][:, :], EPS)
            pool.iota(base_i[:, :], pattern=[[GROUP, T]], base=0, channel_multiplier=0)
            pool.iota(iota_i[:, :], pattern=[[1, BLK], [BLK, P]], base=0, channel_multiplier=0).then_inc(iotas, 1)

        @block.vector
        def _(dve):
            dve.memset(ones[:, :], 1.0)
            dve.memset(zero_f[:, :], 0.0)
            dve.memset(rounds_f[:, :], 0.0)
            dve.memset(k["table"][:, :], 0).then_inc(step, 1)
            dve.wait_ge(iotas, 2)
            dve.tensor_copy(k["base"][:, :], base_i[:, :])
            dve.tensor_copy(k["iota"][:, :], iota_i[:, :]).then_inc(step, 1)
            dve.wait_ge(edges_in, 16 * 5)
            dve.tensor_copy(dst_f[:, :], dst_i[:, :])
            dve.tensor_copy(next_f[:, :], next_i[:, :]).then_inc(step, 1)
            dve.wait_ge(step, 3)
            dve.tensor_copy(rec[:, :, 0], src_i[:, :])
            dve.tensor_copy(rec[:, :, 1], dst_f[:, :].bitcast(I32))
            dve.tensor_copy(rec[:, :, 2], w_in[:, :].bitcast(I32)).then_inc(built, 1)
            dve.tensor_tensor(hit[:, :], next_f[:, :], dst_f[:, :], ALU.is_lt).then_inc(step, 1)
            dve.wait_ge(step, 4)
            dve.tensor_reduce(below[:, T:T + 1], hit[:, :], AX.X, ALU.add).then_inc(step, 1)
            dve.wait_ge(step, 5)
            for g in range(T):
                dve.tensor_scalar(hit[:, :], dst_f[:, :], float(g * GROUP), 0.0, ALU.is_lt, ALU.add,
                                  accum_out=below[:, g:g + 1]).then_inc(step, 1)
                dve.wait_ge(step, 6 + g)
            dve.tensor_scalar(hit[:, 0:1], hit[:, 0:1], 0.0, None, ALU.mult).then_inc(counted, 1)
            dve.wait_ge(summed, 1)
            n = 6 + T - 1

            def link(ins):
                nonlocal n
                n += 1
                ins.then_inc(step, 1)
                dve.wait_ge(step, n)

            link(dve.tensor_copy(bound[:, :], sums[:, 0:T + 1]))
            link(dve.tensor_scalar(unsorted[:, :], bound[:, T:T + 1], 1.0, None, ALU.min))
            link(dve.tensor_scalar(lo_f[:, :], bound[:, 0:T], unsorted[:, 0:1], None, ALU.mult))
            link(dve.tensor_tensor(lo_f[:, :], bound[:, 0:T], lo_f[:, :], ALU.subtract))
            link(dve.memset(count_f[:, :], 0.0))
            link(dve.tensor_tensor(count_f[:, 0:T - 1], bound[:, 1:T], bound[:, 0:T - 1], ALU.subtract))
            link(dve.tensor_scalar(hit[0:1, 0:T], count_f[:, :], -1.0, float(E), ALU.mult, ALU.add))
            link(dve.tensor_scalar(hit[0:1, 0:T], hit[0:1, 0:T], unsorted[:, 0:1], None, ALU.mult))
            link(dve.tensor_tensor(count_f[:, :], count_f[:, :], hit[0:1, 0:T], ALU.add))
            for a, b, main in s.spans:
                b = T if b == s.groups else b
                link(dve.tensor_scalar(count_f[:, a:b], count_f[:, a:b], float(-main * P), 0.0, ALU.add, ALU.max))
            link(dve.tensor_scalar(count_f[:, :], count_f[:, :], float(OVER * P - 1), None, ALU.add))
            link(dve.memset(count_f[:, s.groups:T], 0.0))
            link(dve.tensor_copy(rounds_i[:, :], count_f[:, :]))
            link(dve.tensor_scalar(rounds_i[:, :], rounds_i[:, :], (OVER * P).bit_length() - 1, None, ALU.arith_shift_right))
            link(dve.tensor_copy(rounds_f[:, 1:T + 1], rounds_i[:, :]))
            link(dve.memset(prefix_f[:, :], 0.0))
            for a, b, _ in s.spans:
                link(dve.tensor_tensor_scan(prefix_f[:, a + 1:b], rounds_f[:, a + 1:b], zero_f[:, a + 1:b], 0.0, ALU.add, ALU.add))
            tab = k["table"][:, :].rearrange("a (g c) -> a g c", c=REC)
            dve.tensor_copy(tab[:, :, 0], lo_f[:, :])
            dve.tensor_copy(tab[:, :, 1], rounds_i[:, :])
            dve.tensor_copy(tab[:, :, 2], prefix_f[:, 0:T])
            dve.wait_ge(consts_in, 16 * len(consts))
            link(dve.tensor_scalar(w_acc[:, 0, :], bases_s[:, 0, :], comp_s[:, 0:1], None, ALU.mult))
            for b in range(1, 8):
                to = k["W"][:, :] if b == 7 else w_acc[:, b % 2, :]
                link(dve.scalar_tensor_tensor(to, bases_s[:, b, :], comp_s[:, b:b + 1], w_acc[:, (b - 1) % 2, :], ALU.mult, ALU.add))

        @block.tensor
        def _(pe):
            pe.wait_ge(counted, 1)
            pe.matmul(sums[:, 0:T + 1], ones[:, :], below[:, :], start=True, stop=True).then_inc(summed, 1)


def node_pass(nc, s, k, kind, span, records, x_dram, rows_dram, out_dram, p_dram):
    base_group, end_group, MAIN = span
    GROUPS = end_group - base_group
    LAG = {"sage1": 1, "sage2": 0, "contrast": 2, "basis": 1, "weighted": 1}[kind]
    KEEP = RING if kind == "contrast" else 2
    X_AHEAD = 3
    normed = kind != "sage2"
    node_major = kind in ("sage1", "sage2", "contrast")
    degree = kind == "sage1"
    weighted = kind == "weighted"
    final = kind == "weighted"
    cols = MAIN + BLK
    width = D + 2 if degree else D

    with ExitStack() as ctx:
        def sb(name, shape, dt=F32):
            return ctx.enter_context(nc.sbuf_tensor(f"{kind}{base_group}_{name}", shape, dt))

        def pb(name, cols):
            return ctx.enter_context(nc.psum_tensor(f"{kind}{base_group}_{name}", [P, cols], F32))

        made = []

        def sem(name):
            made.append(nc.alloc_semaphore(f"{kind}{base_group}_{name}"))
            return made[-1]

        def sems(name, n):
            return [sem(f"{name}{i}") for i in range(n)]

        meta = sb("meta", [P, RING, MAIN, REC], I32)
        raw = sb("raw", [P, RING, MAIN, D])
        xin = sb("xin", [P, RING, BLK, D])
        msg = sb("msg", [P, 2, MAIN, D])
        hi = sb("msg_hi", [P, 2, MAIN, width], F32R)
        lo = sb("msg_lo", [P, 2, MAIN, D], F32R)
        rel = sb("rel_dst", [P, 2, MAIN])
        S = sb("onehot", [P, 2, MAIN, GROUP], F32R)
        st = sb("bn", [P, cols, 6])
        mv = sb("mean_var", [P, 2, cols, 2])
        std = sb("std", [P, cols])
        if kind == "contrast":
            powers = cols + 2 * BLK
            exponents = sb("exponents", [P, powers])
            exponents_o = sb("oexponents", [P, OVER])
            pow_x = sb("pow_in", [P, 2, powers])
            rstd = sb("pow_out", [P, 2, powers])
            var_o = sb("ovar", [P, OVER])
        else:
            rstd = sb("rstd", [P, 2, cols])
        nb = sb("neg_mean_rstd", [P, 2, cols])
        h = sb("h", [P, KEEP, BLK, D])
        xb = sb("x_plus_bias", [P, RING, BLK, D])
        o_s = sb("out_tile", [P, 2, BLK, D])
        zero_s = sb("zero", [1, 1])
        tick_s = sb("tick", [1, 2])
        meta_o = sb("ometa", [P, OVER, REC], I32)
        raw_o = sb("oraw", [P, OVER, D])
        msg_o = sb("omsg", [P, OVER, D])
        hi_o = sb("omsg_hi", [P, OVER, width], F32R)
        lo_o = sb("omsg_lo", [P, OVER, D], F32R)
        rel_o = sb("orel_dst", [P, OVER])
        S_o = sb("oonehot", [P, OVER, GROUP], F32R)
        st_o = sb("obn", [P, OVER, 6])
        mv_o = sb("omean_var", [P, OVER, 2])
        std_o = sb("ostd", [P, OVER])
        rstd_o = sb("orstd", [P, OVER])
        nb_o = sb("oneg_mean_rstd", [P, OVER])
        if degree:
            deg = sb("deg", [P, BLK])
            invg = sb("inv_deg", [P, BLK])
            mean = sb("mean", [P, BLK, D])
            hT = sb("hT", [P, GROUP])
            mT = sb("meanT", [P, GROUP])
            HT = sb("hiddenT", [P, 2, GROUP])
            p_s = sb("p_tile", [P, 2, BLK, D])
            agg = pb("agg", 1024)
            tr = pb("transposed", 1024)
            hid = pb("hidden", 1024)
            outp = pb("out", 1024)
            sums = agg[:, :].rearrange("p (k c) -> p k c", k=2)[:, :, 0:2 * width].rearrange("p k (j c) -> p k j c", c=width)
        else:
            sum_banks = pb("agg", 1024)
        if kind == "sage2":
            invg = sb("inv_deg", [P, BLK])
        if kind == "contrast":
            invg = sb("inv_deg", [P, BLK])
            diff = sb("diff", [P, BLK, D])
            sq = sb("sq", [P, BLK, D])
            th = sb("tanh", [P, BLK])
            ta = sb("alpha_tanh", [P, BLK])
            hT = sb("hT", [P, GROUP])
            hc = sb("hiddenT", [HALF + 1, GROUP])
            e_s = sb("enhanced", [P, 2, BLK, D])
            st2 = sb("bn2", [P, BLK, 6])
            mv2 = sb("mean_var2", [P, BLK, 2])
            nb2 = sb("nb2", [P, BLK])
            n_s = sb("normed", [P, BLK, D])
            ng_s = sb("normed_gamma", [P, BLK, D])
            tr = pb("transposed", 512)
            hid = pb("hidden", 512)
            outp = pb("out", 512)
        if kind == "basis":
            aT = sb("aggT", [P, GROUP])
            hT = sb("hT", [P, GROUP])
            tr = pb("transposed", 512)
            outp = pb("out", 512)
        if kind == "weighted":
            zT = sb("zT", [P, GROUP])
            gT = sb("hiddenT", [P, GROUP])
            hid = pb("hidden", 512)
            outp = pb("out", 512)

        meta_in = sems("meta_in", RING)
        x_in = sems("x_in", RING)
        raw_in = [sems(f"raw_in{c}_", RING) for c in range(MAIN)]
        seg = sems("onehot_built", RING)
        stats = sem("stats")
        moments = sem("moments")
        std_ready = sem("std")
        rstd_ready = sem("rstd")
        coef = sem("coef")
        relset = sem("rel")
        rows_ready = sems("rows_ready", RING)
        lo_ready = sems("lo_ready", RING)
        h_ready = sems("h_ready", RING)
        xb_ready = sems("xb_ready", RING)
        agg_done = sems("agg_done", RING)
        agg_free = sem("agg_free")
        out_ready = sems("out_ready", 2)
        stored = sems("stored", 2)
        cleared = sem("cleared")
        zeroed = sem("zeroed")
        tick = sem("tick")
        o_tick = sem("otick")
        meta_o_in = sem("ometa_in")
        raw_o_in = sems("oraw_in", OVER)
        o_stats = sem("ostats")
        o_moments = sem("omoments")
        o_std = sem("ostd")
        o_rstd = sem("orstd")
        o_coef = sem("ocoef")
        o_rel = sem("orel")
        o_seg = sem("oonehot_built")
        o_rows = sem("orows_ready")
        o_lo = sem("olo_ready")
        o_agg = sem("oagg_done")
        if weighted:
            unweighted = sem("unweighted")
            o_unweighted = sem("ounweighted")
        else:
            unweighted = o_unweighted = None
        if degree:
            p_ready = sems("p_ready", 2)
            p_stored = sems("p_stored", 2)
        dense = {n: sem(n) for n in {
            "sage1": ["deg_max", "inv_done", "mean_ready", "hT_psum", "mT_psum", "hT_ready", "mT_ready", "hid_a",
                      "hid_b", "HT_a", "HT_b", "out_psum"],
            "sage2": ["inv_copied"],
            "contrast": ["inv_copied", "diff_done", "sq_done", "ssq_done", "pow_clear", "pow_in", "pow_done", "tanh_done",
                         "ta_done", "hT_psum", "hT_ready", "hid_psum", "hc_ready", "out_psum", "e_done", "st2_done",
                         "mv2_done", "coef2", "n_ready", "ng_ready", "o_var"],
            "basis": ["hT_psum", "hT_ready", "aT_ready", "out_psum"],
            "weighted": ["zT_ready", "hid_psum", "gT_ready", "out_psum"],
        }[kind]}
        passed = ExitStack()
        block = passed.enter_context(nc.Block())

        def agg_of(group):
            q = slot(group, 2)
            return agg[:, :] if degree else sum_banks[:, q * 512:(q + 1) * 512]

        mf = meta[:, :, :, :].bitcast(F32)
        mof = meta_o[:, :, :].bitcast(F32)

        def node_group(group):
            return number(group) + base_group

        def done(count):
            return max(count, 0) if isinstance(count, int) else count

        def quads(eng, step, last=None):
            turns = GROUPS // RING
            end = turns if last is None else turns - 1
            for q in range(RING):
                step((0, q))
            if end > 1:
                with eng.Fori(1, end) as t:
                    for q in range(RING):
                        step((t, q))
            if last is not None:
                for q in range(RING):
                    last((turns - 1, q))

        final_group = (GROUPS // RING - 1, RING - 1)

        def table(eng, group, word, most):
            at = node_group(group) * REC + word
            return eng.value_load(k["table"][0:1, bass.ds(at, 1)], min_val=0, max_val=most)

        def rounds_of(eng, group, body):
            most = -(-s.edges // (OVER * P))
            n = table(eng, group, 1, most)
            with eng.If(n > 0):
                before = table(eng, group, 2, most * s.table)
                with eng.Fori(0, n) as i:
                    body(i, before + i)

        def rows_of(dram, g, n=GROUP):
            return dram[bass.ds(g * GROUP, n), :].rearrange("(p b) f -> p (b f)", b=BLK)

        @block.sync
        def _(sp):
            def load_meta(group):
                r, u = slot(group, RING), turn(group, RING)
                for c in range(MAIN):
                    sp.wait_ge(raw_in[c][r], u * 16)
                sp.wait_ge(seg[r], u)
                if weighted:
                    sp.wait_ge(lo_ready[r], u)
                    sp.wait_ge(rows_ready[r], u)
                first = table(sp, group, 0, s.edges)
                sp.dma_start(meta[:, r, :, :].rearrange("p c w -> p (c w)"),
                             records[bass.ds(first, MAIN * P), :].rearrange("(p c) w -> p (c w)", c=MAIN)
                             ).then_inc(meta_in[r], 16)

            def load_x(group, where, parts=P):
                r, u = slot(group, RING), turn(group, RING)
                if normed:
                    sp.wait_ge(xb_ready[r], u)
                    sp.wait_ge(h_ready[r], u)
                else:
                    sp.wait_ge(out_ready[slot(group, 2)], done(turn(group, 2) - 1))
                sp.dma_start(xin[0:parts, r, :, :].rearrange("p b f -> p (b f)"), rows_of(x_dram, where, parts * BLK)
                             ).then_inc(x_in[r], 16)

            def x_or_tail(group):
                g = node_group(group)
                if g < s.tail_group or (x_dram.shape[0] > s.nodes and g < s.groups):
                    load_x(group, g)
                elif g == s.tail_group and s.tail:
                    load_x(group, g, s.tail // BLK)
                else:
                    load_x(group, 0)

            def overflow(group):
                most = -(-s.edges // (OVER * P))
                n = table(sp, group, 1, most)
                with sp.If(n > 0):
                    first = table(sp, group, 0, s.edges)
                    before = table(sp, group, 2, s.table * most)
                    with sp.Fori(0, n) as i:
                        o = before + i
                        sp.wait_ge(o_rows, o + 1)
                        sp.wait_ge(o_seg, o + 1)
                        if weighted:
                            sp.wait_ge(o_lo, o + 1)
                        at = first + MAIN * P + i * (OVER * P)
                        sp.dma_start(meta_o[:, :, :].rearrange("p c w -> p (c w)"),
                                     records[bass.ds(at, OVER * P), :].rearrange("(p c) w -> p (c w)", c=OVER)
                                     ).then_inc(meta_o_in, 16)

            def store(group, parts=P):
                q, g = slot(group, 2), node_group(group)
                if degree:
                    sp.wait_ge(p_ready[q], turn(group, 2) + 1)
                    sp.dma_start(rows_of(p_dram, g), p_s[:, q, :, :].rearrange("p b f -> p (b f)")).then_inc(p_stored[q], 16)
                sp.wait_ge(out_ready[q], turn(group, 2) + 1)
                sp.dma_start(rows_of(out_dram, g, parts * BLK), o_s[0:parts, q, :, :].rearrange("p b f -> p (b f)")
                             ).then_inc(stored[q], 16)

            def store_if(group):
                if static(group) and number(group) < 0:
                    return
                if static(group) and final and node_group(group) >= s.tail_group:
                    if node_group(group) == s.tail_group and s.tail:
                        store(group, s.tail // BLK)
                    return
                store(group)

            def step(group):
                overflow(group)
                load_x(ahead(group, X_AHEAD), node_group(ahead(group, X_AHEAD)))
                store_if(ahead(group, -LAG))
                load_meta(ahead(group, 5))

            def last(group):
                overflow(group)
                x_or_tail(ahead(group, X_AHEAD))
                store_if(ahead(group, -LAG))
                load_meta(ahead(group, 5))

            for g in range(RING):
                load_meta((0, g))
            for g in range(X_AHEAD):
                load_x((0, g), base_group + g)
            load_meta((0, RING))
            quads(sp, step, last)
            for lag in range(LAG - 1, -1, -1):
                store_if(ahead(final_group, -lag))
            full = GROUPS if not final else min(GROUPS, s.tail_group + (s.tail > 0) - base_group)
            for q in range(2):
                n = (full + 1 - q) // 2
                sp.wait_ge(stored[q], 16 * n)
                if degree:
                    sp.wait_ge(p_stored[q], 16 * n)
            for r in range(RING):
                sp.wait_ge(meta_in[r], 16 * ((GROUPS + 5 + RING - 1 - r) // RING))
                sp.wait_ge(x_in[r], 16 * ((GROUPS + X_AHEAD + RING - 1 - r) // RING))
                for c in range(MAIN):
                    sp.wait_ge(raw_in[c][r], 16 * ((GROUPS + 4 + RING - 1 - r) // RING))

        bias_of = {"sage1": "b2l", "contrast": "beta", "basis": "bias", "weighted": "v2"}

        @block.gpsimd
        def _(pool):
            pool.memset(zero_s[:, :], 0.0).then_inc(zeroed, 1)
            pool.memset(tick_s[:, 0:1], 0.0).then_inc(tick, 1)
            pool.memset(tick_s[:, 1:2], 0.0).then_inc(o_tick, 1)
            pool.wait_ge(zeroed, 1)
            if degree:
                for pad in (hi[:, :, :, D:D + 2], hi_o[:, :, D:D + 2]):
                    one = pad.bitcast(F32)
                    pool.memset(one[..., 0:1], 1.0)
                    pool.memset(one[..., 1:2], 0.0).then_inc(cleared, 1)
            if kind == "contrast":
                pool.memset(hc[HALF:HALF + 1, :], 1.0).then_inc(cleared, 1)
                pool.wait_ge(cleared, 1)
                pool.memset(exponents_o[:, :], -0.5)
                pool.memset(exponents[:, 0:cols], -0.5)
                pool.memset(exponents[:, cols:cols + BLK], 0.5)
                pool.memset(exponents[:, cols + BLK:powers], -0.5).then_inc(cleared, 1)
                pool.wait_ge(cleared, 2)

            def carry(n, sem_):
                pool.wait_ge(sem_, n)
                pool.tensor_tensor(tick_s[:, 0:1], zero_s[:, :], zero_s[:, :], ALU.add).then_inc(sem_, 1)

            def gather(group):
                r, u = slot(group, RING), turn(group, RING)
                pool.wait_ge(meta_in[r], (u + 1) * 16)
                pool.wait_ge(rows_ready[r], u)
                if not normed:
                    pool.wait_ge(lo_ready[r], u)
                if not static(group):
                    carry(number(group) - (2 * RING - 1), tick)
                for c in range(MAIN):
                    pool.indirect_dma_start(raw[:, r, c, :], None, rows_dram,
                                            bass.IndirectOffsetOnAxis(ap=meta[:, r, c, 0:1], axis=0)
                                            ).then_inc(raw_in[c][r], 16)

            def add_bias(group):
                r, q = slot(group, RING), slot(group, 2)
                pool.wait_ge(x_in[r], (turn(group, RING) + 1) * 16)
                pool.wait_ge(out_ready[q], done(turn(group, 2) - 1))
                b = k[bias_of[kind]][:, :]
                pool.tensor_tensor(xb[:, r, :, :], xin[:, r, :, :], b.unsqueeze(1).to_broadcast([P, BLK, D]), ALU.add
                                   ).then_inc(xb_ready[r], 1)

            def overflow(i, o):
                pool.wait_ge(meta_o_in, (o + 1) * 16)
                pool.wait_ge(o_rows, o + 1)
                if not normed:
                    pool.wait_ge(o_lo, o + 1)
                pool.wait_ge(o_tick, o + 1)
                pool.tensor_tensor(tick_s[:, 1:2], zero_s[:, :], zero_s[:, :], ALU.add).then_inc(o_tick, 1)
                for j in range(OVER):
                    pool.indirect_dma_start(raw_o[:, j, :], None, rows_dram,
                                            bass.IndirectOffsetOnAxis(ap=meta_o[:, j, 0:1], axis=0)
                                            ).then_inc(raw_o_in[j], 16)
                if kind == "contrast":
                    pool.wait_ge(dense["o_var"], o + 1)
                    pool.tensor_tensor(rstd_o[:, :], var_o[:, :], exponents_o[:, :], ALU.pow).then_inc(o_std, 1)

            def raise_powers(n):
                q, g = slot(n, 2), number(n)
                pool.wait_ge(dense["pow_in"], g + 1)
                p = ahead(n, -2)
                pool.wait_ge(coef, done(g - 1))
                pool.wait_ge(h_ready[slot(p, RING)], done(turn(p, RING) + 1))
                pool.wait_ge(rows_ready[slot(p, RING)], done(turn(p, RING) + 1))
                pool.wait_ge(dense["tanh_done"], done(g - 3))
                pool.wait_ge(dense["n_ready"], done(g - 4))
                pool.tensor_tensor(rstd[:, q, :], pow_x[:, q, :], exponents[:, :], ALU.pow).then_inc(dense["pow_done"], 1)

            def times_gamma(group):
                pool.wait_ge(dense["n_ready"], number(group) + 1)
                p = ahead(group, -1)
                pool.wait_ge(out_ready[slot(p, 2)], turn(p, 2) + 1)
                pool.tensor_tensor(ng_s[:, :, :], n_s[:, :, :], k["gamma"][:, :].unsqueeze(1).to_broadcast([P, BLK, D]),
                                   ALU.mult).then_inc(dense["ng_ready"], 1)

            def step(group):
                rounds_of(pool, group, overflow)
                gather(ahead(group, 4))
                if normed:
                    add_bias(ahead(group, 1))
                if kind == "contrast":
                    if not (static(group) and number(group) < 2):
                        times_gamma(ahead(group, -2))
                    raise_powers(ahead(group, 2))

            for g in range(RING):
                gather((0, g))
            if normed:
                add_bias((0, 0))
            if kind == "contrast":
                for g in range(2):
                    raise_powers((0, g))
            quads(pool, step)
            if kind == "contrast":
                times_gamma(ahead(final_group, -1))
                raise_powers(ahead(final_group, 3))
                times_gamma(final_group)

        @block.vector
        def _(dve):
            def ln_moments(group):
                r, g = slot(group, RING), number(group)
                for c in range(MAIN):
                    dve.wait_ge(raw_in[c][r], (turn(group, RING) + 1) * 16)
                dve.wait_ge(x_in[r], (turn(group, RING) + 1) * 16)
                if kind != "contrast":
                    dve.wait_ge(std_ready, done(g - 1))
                for c in range(cols):
                    of = raw[:, r, c, :] if c < MAIN else xin[:, r, c - MAIN, :]
                    last = dve.bn_stats(st[:, c, :], of)
                last.then_inc(stats, 1)
                dve.wait_ge(stats, g + 1)
                relative(group)
                for c in range(cols):
                    last = dve.bn_aggr(mv[:, slot(group, 2), c, :], st[:, c, :])
                last.then_inc(moments, 1)
                if kind == "contrast":
                    dve.wait_ge(moments, g + 1)
                    dve.wait_ge(dense["pow_done"], done(g - 1))
                    ins = dve.tensor_scalar(pow_x[:, slot(group, 2), 0:cols], mv[:, slot(group, 2), :, 1], EPS, None, ALU.add)
                    if static(group) and g < 2:
                        ins.then_inc(dense["pow_in"], 1)

            def ln_coefficients(group):
                q, g = slot(group, 2), number(group)
                dve.wait_ge(dense["pow_done"] if kind == "contrast" else std_ready, g + 1)
                p = ahead(group, -2)
                dve.wait_ge(h_ready[slot(p, RING)], turn(p, RING) + 1)
                dve.wait_ge(rows_ready[slot(p, RING)], turn(p, RING) + 1)
                if kind != "contrast":
                    dve.reciprocal(rstd[:, q, :], std[:, :]).then_inc(rstd_ready, 1)
                    dve.wait_ge(rstd_ready, g + 1)
                dve.scalar_tensor_tensor(nb[:, q, :], mv[:, q, :, 0], -1.0, rstd[:, q, 0:cols], ALU.mult, ALU.mult).then_inc(coef, 1)

            def relative(group):
                r, q, g = slot(group, RING), slot(group, 2), number(group)
                dve.wait_ge(meta_in[r], (turn(group, RING) + 1) * 16)
                dve.tensor_tensor(rel[:, q, :], mf[:, r, :, 1], k["base"][:, bass.ds(g + base_group, 1)].to_broadcast([P, MAIN]), ALU.subtract
                                  ).then_inc(relset, 1)

            def one_hot(group):
                r, q, g = slot(group, RING), slot(group, 2), number(group)
                if not normed:
                    relative(group)
                dve.wait_ge(relset, g + 1)
                for c in range(MAIN):
                    last = dve.tensor_scalar(S[:, q, c, :], k["iota"][:, :], rel[:, q, c:c + 1], None, ALU.is_equal)
                last.then_inc(seg[r], 1)

            def low_parts(group):
                r, q, g = slot(group, RING), slot(group, 2), number(group)
                dve.wait_ge(rows_ready[r], turn(group, RING) + 1)
                if weighted:
                    for c in range(MAIN):
                        last = dve.scalar_tensor_tensor(lo[:, q, c, :], msg[:, q, c, :], mf[:, r, c, 2:3], hi[:, q, c, 0:D].bitcast(F32),
                                                        ALU.mult, ALU.subtract)
                    last.then_inc(lo_ready[r], 1)
                    return
                of = msg[:, q, :, :] if normed else raw[:, r, :, :]
                dve.tensor_tensor(lo[:, q, :, :], of, hi[:, q, :, 0:D].bitcast(F32), ALU.subtract).then_inc(lo_ready[r], 1)

            def overflow(group):
                g = node_group(group)

                def relative_over(o):
                    dve.wait_ge(meta_o_in, (o + 1) * 16)
                    dve.tensor_tensor(rel_o[:, :], mof[:, :, 1], k["base"][:, bass.ds(g, 1)].to_broadcast([P, OVER]), ALU.subtract
                                      ).then_inc(o_rel, 1)

                def body(i, o):
                    if normed:
                        for j in range(OVER):
                            dve.wait_ge(raw_o_in[j], (o + 1) * 16)
                            last = dve.bn_stats(st_o[:, j, :], raw_o[:, j, :])
                        last.then_inc(o_stats, 1)
                        dve.wait_ge(o_stats, o + 1)
                        relative_over(o)
                        for j in range(OVER):
                            last = dve.bn_aggr(mv_o[:, j, :], st_o[:, j, :])
                        last.then_inc(o_moments, 1)
                        if kind == "contrast":
                            dve.wait_ge(o_moments, o + 1)
                            dve.tensor_scalar(var_o[:, :], mv_o[:, :, 1], EPS, None, ALU.add).then_inc(dense["o_var"], 1)
                    else:
                        relative_over(o)
                    dve.wait_ge(o_agg, o + 1)
                    dve.wait_ge(o_rel, o + 1)
                    for j in range(OVER):
                        last = dve.tensor_scalar(S_o[:, j, :], k["iota"][:, :], rel_o[:, j:j + 1], None, ALU.is_equal)
                    last.then_inc(o_seg, 1)
                    if normed:
                        dve.wait_ge(o_std, o + 1)
                        dve.wait_ge(o_rows, o + 1)
                        if kind != "contrast":
                            dve.reciprocal(rstd_o[:, :], std_o[:, :]).then_inc(o_rstd, 1)
                            dve.wait_ge(o_rstd, o + 1)
                        dve.scalar_tensor_tensor(nb_o[:, :], mv_o[:, :, 0], -1.0, rstd_o[:, :], ALU.mult, ALU.mult).then_inc(o_coef, 1)
                    dve.wait_ge(o_rows, o + 2)
                    if weighted:
                        for j in range(OVER):
                            last = dve.scalar_tensor_tensor(lo_o[:, j, :], msg_o[:, j, :], mof[:, j, 2:3], hi_o[:, j, 0:D].bitcast(F32),
                                                            ALU.mult, ALU.subtract)
                        last.then_inc(o_lo, 1)
                        return
                    of = msg_o[:, :, :] if normed else raw_o[:, :, :]
                    dve.tensor_tensor(lo_o[:, :, :], of, hi_o[:, :, 0:D].bitcast(F32), ALU.subtract).then_inc(o_lo, 1)

                rounds_of(dve, group, body)

            def prepare(group):
                w, need = before(group)
                dve.wait_ge(agg_done[w], need)
                one_hot(group)
                low_parts(group)

            def out_sum(group):
                q = slot(group, 2)
                if kind == "contrast":
                    dve.wait_ge(dense["ng_ready"], number(group) + 1)
                    term = ng_s[:, :, :]
                else:
                    dve.wait_ge(dense["out_psum"], number(group) + 1)
                    term = (outp[:, GROUP:2 * GROUP] if kind == "sage1" else outp[:, :]).rearrange("p (b c) -> p b c", b=BLK)
                dve.wait_ge(stored[q], turn(group, 2) * 16)
                dve.wait_ge(xb_ready[slot(group, RING)], turn(group, RING) + 1)
                dve.tensor_tensor(o_s[:, q, :, :], term, xb[:, slot(group, RING), :, :], ALU.add).then_inc(out_ready[q], 1)

            def copy_hT(group, read):
                dve.wait_ge(dense["hT_psum"], number(group) + 1)
                dve.wait_ge(dense[read], number(group))
                dve.tensor_copy(hT[:, :], tr[:, 0:GROUP]).then_inc(dense["hT_ready"], 1)

            def degree_mean(group):
                g = number(group)
                dve.wait_ge(agg_done[slot(group, RING)], turn(group, RING) + 1)
                dve.tensor_scalar(deg[:, :].rearrange("p (k j) -> p k j", k=2), sums[:, :, :, D], 1.0, None, ALU.max
                                  ).then_inc(dense["deg_max"], 1)
                dve.wait_ge(dense["deg_max"], g + 1)
                dve.reciprocal(k["inv"][:, bass.ds(node_group(group) * BLK, BLK)], deg[:, :])
                dve.reciprocal(invg[:, :], deg[:, :]).then_inc(dense["inv_done"], 1)
                dve.wait_ge(dense["inv_done"], g + 1)
                dve.wait_ge(dense["mT_psum"], g)
                dve.tensor_tensor(mean[:, :, :].rearrange("p (k j) f -> p k j f", k=2), sums[:, :, :, 0:D],
                                  invg[:, :].rearrange("p (k j) -> p k j", k=2).unsqueeze(3).to_broadcast([P, 2, 2, D]), ALU.mult
                                  ).then_inc(dense["mean_ready"], 1)

            def inverse_degree(group):
                dve.tensor_copy(invg[:, :], k["inv"][:, bass.ds(node_group(group) * BLK, BLK)]).then_inc(dense["inv_copied"], 1)
                dve.wait_ge(dense["inv_copied"], number(group) + 1)

            def neighbour_difference(group):
                inverse_degree(group)
                dve.wait_ge(agg_done[slot(group, RING)], turn(group, RING) + 1)
                dve.wait_ge(dense["sq_done"], number(group))
                dve.wait_ge(h_ready[slot(group, RING)], turn(group, RING) + 1)
                for b in range(BLK):
                    last = dve.scalar_tensor_tensor(diff[:, b, :], agg_of(group)[:, b * D:(b + 1) * D], invg[:, b:b + 1],
                                                    h[:, slot(group, KEEP), b, :], ALU.mult, ALU.subtract)
                last.then_inc(dense["diff_done"], 1)

            def square_sum(group):
                g, q = number(group), slot(group, 2)
                dve.wait_ge(dense["sq_done"], g + 1)
                dve.wait_ge(dense["pow_done"], g + 1)
                dve.tensor_reduce(pow_x[:, q, cols:cols + BLK], sq[:, :, :], AX.X, ALU.add).then_inc(dense["ssq_done"], 1)
                if very_first(group):
                    dve.memset(pow_x[:, q, cols + BLK:powers], 1.0).then_inc(dense["pow_in"], 1)

            def enhance(group):
                g, q = number(group), slot(group, 2)
                dve.wait_ge(dense["tanh_done"], g + 1)
                dve.tensor_scalar(ta[:, :], th[:, :], ALPHA, None, ALU.mult).then_inc(dense["ta_done"], 1)
                dve.wait_ge(dense["ta_done"], g + 1)
                dve.wait_ge(dense["out_psum"], g + 1)
                dve.wait_ge(dense["n_ready"], done(g - 1))
                for b in range(BLK):
                    last = dve.scalar_tensor_tensor(e_s[:, q, b, :], outp[:, b * D:(b + 1) * D], ta[:, b:b + 1],
                                                    h[:, slot(group, KEEP), b, :], ALU.mult, ALU.add)
                last.then_inc(dense["e_done"], 1)
                dve.wait_ge(dense["e_done"], g + 1)
                for b in range(BLK):
                    last = dve.bn_stats(st2[:, b, :], e_s[:, q, b, :])
                last.then_inc(dense["st2_done"], 1)
                dve.wait_ge(dense["st2_done"], g + 1)

            def enhanced_moments(group):
                g, q = number(group), slot(ahead(group, 3), 2)
                for b in range(BLK):
                    last = dve.bn_aggr(mv2[:, b, :], st2[:, b, :])
                last.then_inc(dense["mv2_done"], 1)
                dve.wait_ge(dense["mv2_done"], g + 1)
                dve.wait_ge(dense["pow_done"], g + 2)
                dve.tensor_scalar(pow_x[:, q, cols + BLK:powers], mv2[:, :, 1], EPS, None, ALU.add).then_inc(dense["pow_in"], 1)

            def enhanced_coefficients(group):
                g, q = number(group), slot(ahead(group, 3), 2)
                dve.wait_ge(dense["pow_done"], g + 4)
                dve.wait_ge(dense["n_ready"], g)
                dve.scalar_tensor_tensor(nb2[:, :], mv2[:, :, 0], -1.0, rstd[:, q, cols + BLK:powers], ALU.mult, ALU.mult
                                         ).then_inc(dense["coef2"], 1)

            def step(group):
                g, q, r = number(group), slot(group, 2), slot(group, RING)
                d = dense
                prev = None if very_first(group) else ahead(group, -1)
                overflow(group)
                if normed:
                    ln_moments(ahead(group, 2))
                if kind == "sage1":
                    degree_mean(group)
                    copy_hT(group, "hid_b")
                    ln_coefficients(ahead(group, 2))
                    prepare(ahead(group, 1))
                    if prev:
                        out_sum(prev)
                if kind == "sage2":
                    prepare(ahead(group, 1))
                    inverse_degree(group)
                    dve.wait_ge(agg_done[r], turn(group, RING) + 1)
                    dve.wait_ge(x_in[r], (turn(group, RING) + 1) * 16)
                    dve.wait_ge(stored[q], turn(group, 2) * 16)
                    for b in range(BLK):
                        last = dve.scalar_tensor_tensor(o_s[:, q, b, :], agg_of(group)[:, b * D:(b + 1) * D], invg[:, b:b + 1],
                                                        xin[:, r, b, :], ALU.mult, ALU.add)
                    last.then_inc(out_ready[q], 1)
                if kind == "contrast":
                    second = None if static(group) and number(group) < 2 else ahead(group, -2)
                    ln_coefficients(ahead(group, 1))
                    if second:
                        enhanced_coefficients(second)
                    neighbour_difference(group)
                    copy_hT(group, "hid_psum")
                    if prev:
                        enhance(prev)
                    square_sum(group)
                    if prev:
                        enhanced_moments(prev)
                    prepare(ahead(group, 1))
                    if second:
                        out_sum(second)
                if kind == "basis":
                    if prev:
                        out_sum(prev)
                    copy_hT(group, "out_psum")
                    dve.wait_ge(agg_done[r], turn(group, RING) + 1)
                    dve.tensor_copy(aT[:, :], agg_of(group)).then_inc(d["aT_ready"], 1)
                    ln_coefficients(ahead(group, 2))
                    prepare(ahead(group, 1))
                if kind == "weighted":
                    if prev:
                        out_sum(prev)
                    dve.wait_ge(agg_done[r], turn(group, RING) + 1)
                    dve.wait_ge(d["hid_psum"], g)
                    dve.tensor_copy(zT[:, :], agg_of(group)).then_inc(d["zT_ready"], 1)
                    ln_coefficients(ahead(group, 2))
                    prepare(ahead(group, 1))

            dve.sem_inc(o_seg, 1)
            dve.sem_inc(o_lo, 1)
            dve.sem_inc(o_coef, 1)
            if degree:
                dve.wait_ge(cleared, 2)
            if kind == "contrast":
                dve.memset(pow_x[:, :, :], 1.0).then_inc(dense["pow_clear"], 1)
                dve.wait_ge(dense["pow_clear"], 1)
            if normed:
                ln_moments((0, 0))
                ln_coefficients((0, 0))
                ln_moments((0, 1))
                if kind != "contrast":
                    ln_coefficients((0, 1))
            prepare((0, 0))
            quads(dve, step)
            if kind == "contrast":
                enhanced_coefficients(ahead(final_group, -1))
                enhance(final_group)
                enhanced_moments(final_group)
                out_sum(ahead(final_group, -1))
                enhanced_coefficients(final_group)
            if LAG:
                out_sum(final_group)

        @block.scalar
        def _(act):
            def ln_std(group):
                g = number(group)
                act.wait_ge(moments, g + 1)
                act.wait_ge(rstd_ready, g)
                act.activation(std[:, :], mv[:, slot(group, 2), :, 1], ACT.Sqrt, bias=k["eps"][:, 0:1]).then_inc(std_ready, 1)

            def normal_rows(to, hi_to, of, bias, scale, weight, ready, count):
                ins = act.activation(to, of, ACT.Relu, bias=bias, scale=scale)
                if weighted:
                    ins.then_inc(ready, 1)
                    act.wait_ge(ready, count)
                    return act.activation(hi_to, to, ACT.Copy, scale=weight)
                return act.activation(hi_to, of, ACT.Relu, bias=bias, scale=scale)

            def rows(group):
                r, q, g = slot(group, RING), slot(group, 2), number(group)
                w, need = before(group)
                act.wait_ge(agg_done[w], need)
                if weighted:
                    p = ahead(group, -2)
                    act.wait_ge(lo_ready[slot(p, RING)], turn(p, RING) + 1)
                if normed:
                    act.wait_ge(coef, g + 1)
                    for c in range(MAIN):
                        last = normal_rows(msg[:, q, c, :], hi[:, q, c, 0:D], raw[:, r, c, :], nb[:, q, c:c + 1], rstd[:, q, c:c + 1],
                                           mf[:, r, c, 2:3], unweighted, g * MAIN + c + 1)
                else:
                    for c in range(MAIN):
                        act.wait_ge(raw_in[c][r], (turn(group, RING) + 1) * 16)
                    last = act.activation(hi[:, q, :, 0:D], raw[:, r, :, :], ACT.Copy)
                last.then_inc(rows_ready[r], 1)

            def own(group):
                r, q, g = slot(group, RING), slot(group, 2), number(group)
                act.wait_ge(coef, g + 1)
                if kind == "contrast":
                    act.wait_ge(dense["e_done"], done(g - 3))
                elif kind == "weighted":
                    w, need = before(group)
                    act.wait_ge(agg_done[w], need)
                if kind != "weighted":
                    act.wait_ge(dense["hT_psum"], done(g - KEEP + 1))
                for b in range(BLK):
                    c = MAIN + b
                    last = act.activation(h[:, slot(group, KEEP), b, :], xin[:, r, b, :], ACT.Relu, bias=nb[:, q, c:c + 1], scale=rstd[:, q, c:c + 1])
                last.then_inc(h_ready[r], 1)

            def overflow(i, o):
                if normed:
                    if kind != "contrast":
                        act.wait_ge(o_moments, o + 1)
                        act.wait_ge(o_coef, o + 1)
                        act.activation(std_o[:, :], mv_o[:, :, 1], ACT.Sqrt, bias=k["eps"][:, 0:1]).then_inc(o_std, 1)
                    act.wait_ge(o_coef, o + 2)
                act.wait_ge(o_agg, o + 1)
                if weighted:
                    act.wait_ge(o_lo, o + 1)
                if normed:
                    for j in range(OVER):
                        last = normal_rows(msg_o[:, j, :], hi_o[:, j, 0:D], raw_o[:, j, :], nb_o[:, j:j + 1], rstd_o[:, j:j + 1],
                                           mof[:, j, 2:3], o_unweighted, o * OVER + j + 1)
                else:
                    for j in range(OVER):
                        act.wait_ge(raw_o_in[j], (o + 1) * 16)
                    last = act.activation(hi_o[:, :, 0:D], raw_o[:, :, :], ACT.Copy)
                last.then_inc(o_rows, 1)

            def projection(group):
                q = slot(group, 2)
                act.wait_ge(dense["out_psum"], number(group) + 1)
                act.wait_ge(p_stored[q], turn(group, 2) * 16)
                op = outp[:, 0:GROUP].rearrange("p (b c) -> p b c", b=BLK)
                act.activation(p_s[:, q, :, :], op, ACT.Copy).then_inc(p_ready[q], 1)

            def tanh(group):
                act.wait_ge(dense["pow_done"], number(group) + 3)
                act.wait_ge(dense["ta_done"], number(group))
                act.activation(th[:, :], rstd[:, slot(group, 2), cols:cols + BLK], ACT.Tanh).then_inc(dense["tanh_done"], 1)

            def enhanced_norm(group):
                g = number(group)
                act.wait_ge(dense["coef2"], g + 1)
                act.wait_ge(dense["ng_ready"], g)
                for b in range(BLK):
                    c = cols + BLK + b
                    last = act.activation(n_s[:, b, :], e_s[:, slot(group, 2), b, :], ACT.Identity, bias=nb2[:, b:b + 1],
                                          scale=rstd[:, slot(ahead(group, 3), 2), c:c + 1])
                last.then_inc(dense["n_ready"], 1)

            def step(group):
                g, q = number(group), slot(group, 2)
                d = dense
                nxt, prev = ahead(group, 1), None if very_first(group) else ahead(group, -1)
                rounds_of(act, group, overflow)
                if kind == "contrast" and prev:
                    tanh(prev)
                rows(nxt)
                if kind == "sage1":
                    ln_std(ahead(group, 2))
                    own(nxt)
                    if prev:
                        projection(prev)
                    act.wait_ge(d["mT_psum"], g + 1)
                    act.wait_ge(d["hid_b"], g)
                    act.activation(mT[:, :], tr[:, GROUP:2 * GROUP], ACT.Copy).then_inc(d["mT_ready"], 1)
                    for m, (psum, ready) in enumerate((("hid_a", "HT_a"), ("hid_b", "HT_b"))):
                        act.wait_ge(d[psum], g + 1)
                        act.wait_ge(d["out_psum"], g)
                        act.activation(HT[:, m, :], hid[:, m * 512:(m + 1) * 512], ACT.Relu, bias=k["b1l"][:, m:m + 1]).then_inc(d[ready], 1)
                if kind == "contrast":
                    if not (static(group) and number(group) < 2):
                        enhanced_norm(ahead(group, -2))
                    act.wait_ge(d["diff_done"], g + 1)
                    act.wait_ge(d["ssq_done"], g)
                    act.activation(sq[:, :, :], diff[:, :, :], ACT.Square).then_inc(d["sq_done"], 1)
                    act.wait_ge(d["hid_psum"], g + 1)
                    act.wait_ge(d["out_psum"], g)
                    act.activation(hc[0:HALF, :], hid[0:HALF, :], ACT.Relu, bias=k["c1"][:, 0:1]).then_inc(d["hc_ready"], 1)
                    own(nxt)
                if kind == "basis":
                    ln_std(ahead(group, 2))
                    own(nxt)
                if kind == "weighted":
                    ln_std(ahead(group, 2))
                    act.wait_ge(d["hid_psum"], g + 1)
                    act.wait_ge(d["out_psum"], g)
                    act.activation(gT[:, :], hid[:, :], ACT.Relu, bias=k["v1"][:, 0:1]).then_inc(d["gT_ready"], 1)
                    own(nxt)

            act.sem_inc(o_rows, 1)
            if normed:
                if kind != "contrast":
                    ln_std((0, 0))
                    ln_std((0, 1))
                own((0, 0))
            rows((0, 0))
            quads(act, step)
            if kind == "sage1":
                projection(final_group)
            if kind == "contrast":
                tanh(final_group)
                enhanced_norm(ahead(final_group, -1))
                enhanced_norm(final_group)

        @block.tensor
        def _(pe):
            def sum_chunk(group, S_c, hi_c, lo_c, first, last):
                agg = agg_of(group)
                if node_major:
                    for b in range(BLK):
                        W_ = S_c[:, b * P:(b + 1) * P]
                        if degree:
                            at = (b // 2) * 512 + (b % 2) * width
                            one = first and b % 2 == 0
                        else:
                            at = b * D
                            one = first and b == 0
                        pe.matmul(agg[:, at:at + width], W_, hi_c[:, 0:width], start=one, stop=False, skip_group_check=True)
                        ins = pe.matmul(agg[:, at:at + D], W_, lo_c, start=False, stop=last, skip_group_check=True)
                else:
                    pe.matmul(agg, hi_c, S_c, start=first, stop=False, skip_group_check=True)
                    ins = pe.matmul(agg, lo_c, S_c, start=False, stop=last, skip_group_check=True)
                return ins

            def overflow(group, i, o):
                pe.wait_ge(o_lo, o + 2)
                pe.wait_ge(o_seg, o + 2)
                for j in range(OVER):
                    ins = sum_chunk(group, S_o[:, j, :], hi_o[:, j, :], lo_o[:, j, :], False, False)
                ins.then_inc(o_agg, 1)

            def transposes(psum, of):
                for b in range(BLK):
                    ins = pe.transpose(psum[:, b * P:(b + 1) * P], of[:, b, :], k["ident"][:, :])
                return ins

            def outputs(group):
                g, prev = number(group), ahead(group, -1)
                pe.wait_ge(dense["HT_a"], g + 1)
                pe.wait_ge(dense["HT_b"], g + 1)
                pe.wait_ge(out_ready[slot(prev, 2)], turn(prev, 2) + 1)
                pe.wait_ge(p_ready[slot(prev, 2)], turn(prev, 2) + 1)
                for half in range(2):
                    for b in range(BLK):
                        at = half * GROUP + b * D
                        for m in range(2):
                            ins = pe.matmul(outp[:, at:at + D], HT[:, m, b * P:(b + 1) * P],
                                            k["W2"][:, m, half * D:(half + 1) * D], start=m == 0, stop=m == 1)
                ins.then_inc(dense["out_psum"], 1)

            def step(group):
                g, q, r = number(group), slot(group, 2), slot(group, RING)
                d = dense
                pe.wait_ge(lo_ready[r], turn(group, RING) + 1)
                pe.wait_ge(seg[r], turn(group, RING) + 1)
                if kind == "sage1":
                    pe.wait_ge(d["mean_ready"], g)
                elif kind == "basis":
                    pe.wait_ge(d["aT_ready"], done(g - 1))
                elif kind == "weighted":
                    pe.wait_ge(d["zT_ready"], done(g - 1))
                elif kind == "contrast":
                    pe.wait_ge(d["diff_done"], done(g - 1))
                else:
                    pe.wait_ge(out_ready[q], turn(group, 2))
                sum_chunk(group, S[:, q, 0, :], hi[:, q, 0, :], lo[:, q, 0, :], True, False)
                rounds_of(pe, group, lambda i, o: overflow(group, i, o))
                if kind == "weighted":
                    for c in range(1, MAIN):
                        sum_chunk(group, S[:, q, c, :], hi[:, q, c, :], lo[:, q, c, :], False, False)
                    pe.wait_ge(h_ready[r], turn(group, RING) + 1)
                    for b in range(BLK):
                        ins = pe.matmul(agg_of(group)[:, b * P:(b + 1) * P], h[:, q, b, :], k["ident"][:, :], start=False, stop=b == BLK - 1,
                                        skip_group_check=True)
                    ins.then_inc(agg_done[r], 1)
                    pe.wait_ge(d["zT_ready"], g + 1)
                    pe.wait_ge(d["gT_ready"], g)
                    pe.matmul(hid[:, :], k["V1"][:, :], zT[:, :], start=True, stop=True).then_inc(d["hid_psum"], 1)
                    pe.wait_ge(d["gT_ready"], g + 1)
                    pe.wait_ge(out_ready[(q + 1) % 2], turn(ahead(group, 1), 2))
                    for b in range(BLK):
                        ins = pe.matmul(outp[:, b * D:(b + 1) * D], gT[:, b * P:(b + 1) * P], k["V2"][:, :], start=True, stop=True)
                    ins.then_inc(d["out_psum"], 1)
                    return
                for c in range(1, MAIN):
                    ins = sum_chunk(group, S[:, q, c, :], hi[:, q, c, :], lo[:, q, c, :], False, c == MAIN - 1)
                ins.then_inc(agg_done[r], 1)
                if kind == "sage2":
                    return
                pe.wait_ge(h_ready[r], turn(group, RING) + 1)
                pe.wait_ge(d["hT_ready"], g)
                transposes(tr[:, 0:GROUP], h[:, slot(group, KEEP), :, :]).then_inc(d["hT_psum"], 1)
                if kind == "sage1":
                    if not very_first(group):
                        outputs(ahead(group, -1))
                    pe.wait_ge(d["mean_ready"], g + 1)
                    pe.wait_ge(d["mT_ready"], g)
                    transposes(tr[:, GROUP:2 * GROUP], mean[:, :, :]).then_inc(d["mT_psum"], 1)
                    pe.wait_ge(d["hT_ready"], g + 1)
                    pe.wait_ge(d["HT_b"], g)
                    for m in range(2):
                        pe.matmul(hid[:, m * 512:(m + 1) * 512], k["W1r"][:, m * P:(m + 1) * P], hT[:, :], start=True, stop=False)
                    pe.wait_ge(d["mT_ready"], g + 1)
                    for m, name in enumerate(("hid_a", "hid_b")):
                        pe.matmul(hid[:, m * 512:(m + 1) * 512], k["W1l"][:, m * P:(m + 1) * P], mT[:, :], start=False, stop=True
                                  ).then_inc(d[name], 1)
                if kind == "contrast":
                    pe.wait_ge(d["hT_ready"], g + 1)
                    pe.wait_ge(d["hc_ready"], g)
                    pe.matmul(hid[0:HALF, :], k["C1"][:, :], hT[:, :], start=True, stop=True).then_inc(d["hid_psum"], 1)
                    pe.wait_ge(d["hc_ready"], g + 1)
                    pe.wait_ge(cleared, 1)
                    pe.wait_ge(d["e_done"], g)
                    for b in range(BLK):
                        ins = pe.matmul(outp[:, b * D:(b + 1) * D], hc[:, b * P:(b + 1) * P], k["C2"][:, :], start=True, stop=True)
                    ins.then_inc(d["out_psum"], 1)
                if kind == "basis":
                    pe.wait_ge(d["hT_ready"], g + 1)
                    pe.wait_ge(d["aT_ready"], g + 1)
                    pe.wait_ge(out_ready[(q + 1) % 2], turn(ahead(group, 1), 2))
                    for b in range(BLK):
                        pe.matmul(outp[:, b * D:(b + 1) * D], hT[:, b * P:(b + 1) * P], k["root"][:, :], start=True, stop=False)
                        ins = pe.matmul(outp[:, b * D:(b + 1) * D], aT[:, b * P:(b + 1) * P], k["W"][:, :], start=False, stop=True)
                    ins.then_inc(d["out_psum"], 1)

            pe.sem_inc(o_agg, 1)
            quads(pe, step)
            if kind == "sage1":
                outputs(final_group)

        passed.close()
        nc.clear_and_free_semaphores(made)
        nc.all_engine_barrier()


def kernel(**inputs):
    import numpy as np
    import concourse.bacc as bacc
    from concourse import mybir as mb
    from concourse.bass_utils import run_bass_kernel_spmd as run

    a = {n: np.asarray(v) for n, v in inputs.items()}

    def rows(v):
        return np.ascontiguousarray(np.broadcast_to(v.reshape(1, -1), (128, v.size)))

    given = [
        ("x", a["x"]), ("src", a["src"]), ("dst", a["dst"]), ("edge_weight", a["edge_weight"]),
        ("W1l", a["L0_gnn_W1l"].T), ("b1l", a["L0_gnn_b1l"].reshape(2, 128).T), ("W1r", a["L0_gnn_W1r"].T),
        ("W2cat", np.concatenate([a["L0_gnn_W2l"].T, a["L0_gnn_W2r"].T], axis=1)), ("b2l", rows(a["L0_gnn_b2l"])),
        ("C1", a["L1_gnn_W1"]), ("c1", a["L1_gnn_b1"].reshape(-1, 1)), ("C2", a["L1_gnn_W2"]),
        ("c2", a["L1_gnn_b2"].reshape(1, -1)), ("gamma", rows(a["L1_gnn_gamma"])), ("beta", rows(a["L1_gnn_beta"])),
        ("bases", a["L2_gnn_bases"]), ("comp", rows(a["L2_gnn_comp"])), ("root", a["L2_gnn_root"]),
        ("bias", rows(a["L2_gnn_bias"])), ("V1", a["L3_gnn_W1"]), ("v1", a["L3_gnn_b1"].reshape(-1, 1)),
        ("V2", a["L3_gnn_W2"]), ("v2", rows(a["L3_gnn_b2"])),
    ]
    nc = bacc.Bacc("TRN2", target_bir_lowering=False, num_devices=1)
    arrays, args = {}, []
    for name, v in given:
        v = np.ascontiguousarray(v)
        arrays[f"in_{name}"] = v
        args.append(nc.dram_tensor(f"in_{name}", v.shape, mb.dt.from_np(v.dtype), kind="ExternalInput").ap())
    out = nc.dram_tensor("out_x", a["x"].shape, mb.dt.from_np(np.dtype("float32")), kind="ExternalOutput").ap()
    gnn_kernel(nc, *args, out)
    r = run(nc, [arrays], core_ids=[0])
    return r.results[0]["out_x"]
```

```python
import concourse.bass as bass
from concourse import mybir
from contextlib import ExitStack

P = 128
D = 128
HID = 256
HALF = 64
BLK = 4
GROUP = P * BLK
CHUNKS = (9, 5, 3, 2)
MAX_MAIN = CHUNKS[0]
OVER = 8
RING = 4
PRODUCTS = ((0, 0), (0, 1), (1, 0))
EPS = 1e-5
ALPHA = 0.2
REC = 4

F32 = mybir.dt.float32
F32R = mybir.dt.float32r
I32 = mybir.dt.int32
ALU = mybir.AluOpType
ACT = mybir.ActivationFunctionType
AX = mybir.AxisListType


def slot(group, ring):
    return group[1] % ring


def turn(group, ring):
    t, k = group
    return t * (RING // ring) + k // ring


def number(group):
    return group[0] * RING + group[1]


def before(group):
    return (group[1] - 2) % RING, group[0] + (group[1] - 2) // RING + 1


def static(group):
    return isinstance(group[0], int)


def very_first(group):
    return static(group) and number(group) == 0


def ahead(group, n):
    return (group[0], group[1] + n)


class Shape:

    def __init__(self, nodes, edges):
        self.nodes, self.edges = nodes, edges
        self.groups = -(-nodes // (GROUP * RING)) * RING
        self.tail_group = nodes // GROUP
        self.tail = nodes - self.tail_group * GROUP
        self.padded = self.groups * GROUP
        self.per_part = -(-(edges + 1 + MAX_MAIN * P + OVER * P) // P)
        while edges % self.per_part:
            self.per_part += 1
        self.edge_parts = edges // self.per_part
        self.table = self.groups + RING + 2
        cuts = [c for c in (RING * (self.groups // 96), RING * (self.groups // 28), RING * (self.groups * 20 // 256))
                if c >= 2 * RING]
        cuts = [0] + cuts + [self.groups]
        self.spans = [(a, b, m) for a, b, m in zip(cuts, cuts[1:], CHUNKS[-len(cuts) + 1:])]


def gnn_kernel(nc, x, src, dst, edge_weight, W1l, b1l, W1r, W2cat, b2l, C1, c1, C2, c2, gamma, beta,
               bases, comp, root, bias, V1, v1, V2, v2, out):
    s = Shape(x.shape[0], src.shape[0])
    assert s.edge_parts <= P and P * s.per_part >= s.edges + (MAX_MAIN + OVER) * P and s.tail % BLK == 0

    records = nc.dram_tensor("edge_records", [P * s.per_part + s.edges + OVER * P, REC], I32).ap()
    y_dram = nc.dram_tensor("sage_partial", [s.padded, D], F32).ap()
    p_dram = nc.dram_tensor("sage_projected", [s.padded, D], F32).ap()
    x1_dram = nc.dram_tensor("x_after_sage", [s.padded, D], F32).ap()
    x2_dram = nc.dram_tensor("x_after_contrast", [s.padded, D], F32).ap()
    x3_dram = nc.dram_tensor("x_after_basis", [s.padded, D], F32).ap()

    with ExitStack() as ctx:
        def sb(name, shape, dt=F32):
            return ctx.enter_context(nc.sbuf_tensor(name, shape, dt))

        k = {}
        k["table"] = sb("group_table", [1, s.table * REC], I32)
        k["base"] = sb("group_base", [P, s.table])
        k["iota"] = sb("node_of_column", [P, GROUP])
        k["ident"] = sb("identity", [P, P])
        k["eps"] = sb("eps", [P, 1])
        k["inv"] = sb("inverse_degree", [P, s.groups * BLK])
        k["W1l"] = sb("W1l_s", [P, HID])
        k["W1r"] = sb("W1r_s", [P, HID])
        k["b1l"] = sb("b1l_s", [P, 2])
        k["W2"] = sb("W2_s", [P, 2, 2 * D])
        k["b2l"] = sb("b2l_s", [P, D])
        k["C1"] = sb("C1_s", [P, HALF])
        k["c1"] = sb("c1_s", [HALF, 1])
        k["C2"] = sb("C2_s", [HALF + 1, D])
        k["gamma"] = sb("gamma_s", [P, D])
        k["beta"] = sb("beta_s", [P, D])
        k["W"] = sb("basis_W", [P, D])
        k["root"] = sb("root_s", [P, D])
        k["bias"] = sb("bias_s", [P, D])
        k["V1"] = sb("V1_s", [P, D])
        k["v1"] = sb("v1_s", [P, 1])
        k["V2"] = sb("V2_s", [P, D])
        k["v2"] = sb("v2_s", [P, D])

        setup(nc, s, k, src, dst, edge_weight, W1l, b1l, W1r, W2cat, b2l, C1, c1, C2, c2, gamma, beta,
              bases, comp, root, bias, V1, v1, V2, v2, records)
        for kind, x_of, rows, to, projected in (
                ("sage1", x, x, y_dram, p_dram), ("sage2", y_dram, p_dram, x1_dram, None),
                ("contrast", x1_dram, x1_dram, x2_dram, None), ("basis", x2_dram, x2_dram, x3_dram, None),
                ("weighted", x3_dram, x3_dram, out, None)):
            for span in s.spans:
                node_pass(nc, s, k, kind, span, records, x_of, rows, to, projected)


def setup(nc, s, k, src, dst, edge_weight, W1l, b1l, W1r, W2cat, b2l, C1, c1, C2, c2, gamma, beta,
          bases, comp, root, bias, V1, v1, V2, v2, records):
    E, J, T = s.edges, s.per_part, s.table
    with ExitStack() as ctx:
        def sb(name, shape, dt=F32):
            return ctx.enter_context(nc.sbuf_tensor(name, shape, dt))

        def sem(name):
            return ctx.enter_context(nc.semaphore("setup_" + name))

        src_i = sb("src_i", [P, J], I32)
        dst_i = sb("dst_i", [P, J], I32)
        next_i = sb("next_i", [P, J], I32)
        w_in = sb("w_in", [P, J])
        dst_f = sb("dst_f", [P, J])
        next_f = sb("next_f", [P, J])
        rec = sb("rec", [P, J, REC], I32)
        base_i = sb("base_i", [P, T], I32)
        iota_i = sb("iota_i", [P, GROUP], I32)
        below = sb("below", [P, T + 1])
        hits = sb("hits", [P, 2, J])
        hit = hits[:, 0, :]
        ones = sb("ones", [P, 1])
        bases_s = sb("bases_s", [P, 8, D])
        comp_s = sb("comp_s", [P, 8])
        w_acc = sb("w_acc", [P, 2, D])
        bound = sb("bound", [1, T + 1])
        unsorted = sb("unsorted", [1, 1])
        lo_f = sb("lo_f", [1, T])
        count_f = sb("count_f", [1, T])
        rounds_i = sb("rounds_i", [1, T], I32)
        rounds_f = sb("rounds_f", [1, T + 1])
        zero_f = sb("zero_f", [1, T + 1])
        prefix_f = sb("prefix_f", [1, T + 1])
        sums = ctx.enter_context(nc.psum_tensor("bound_sums", [1, 512], F32))

        edges_in = sem("edges_in")
        consts_in = sem("consts_in")
        records_out = sem("records_out")
        cleared = sem("cleared")
        iotas = sem("iotas")
        step = sem("vector_step")
        counted = sem("counted")
        summed = sem("summed")
        built = sem("records_built")

        n_edge_loads = 5 if s.edge_parts > 1 else 4
        consts = [(k["W1l"][:, :], W1l), (k["W1r"][:, :], W1r), (k["b1l"][:, :], b1l),
                  (k["W2"][:, 0, :], W2cat[0:P, :]), (k["W2"][:, 1, :], W2cat[P:HID, :]), (k["b2l"][:, :], b2l),
                  (k["C1"][:, :], C1), (k["c1"][:, :], c1), (k["C2"][0:HALF, :], C2),
                  (k["C2"][HALF:HALF + 1, :], c2), (k["gamma"][:, :], gamma), (k["beta"][:, :], beta),
                  (k["root"][:, :], root), (k["bias"][:, :], bias), (k["V1"][:, :], V1), (k["v1"][:, :], v1),
                  (k["V2"][:, :], V2), (k["v2"][:, :], v2), (comp_s[:, :], comp),
                  (bases_s[:, :, :], bases.rearrange("b i o -> i b o"))]
        block = ctx.enter_context(nc.Block())

        @block.sync
        def _(sp):
            def rows(a, n):
                return a[0:n * J].rearrange("(p j) -> p j", j=J)

            Q = s.edge_parts
            sp.wait_ge(cleared, 3)
            sp.dma_start(src_i[0:Q, :], rows(src, Q)).then_inc(edges_in, 16)
            sp.dma_start(dst_i[0:Q, :], rows(dst, Q)).then_inc(edges_in, 16)
            sp.dma_start(w_in[0:Q, :], rows(edge_weight, Q)).then_inc(edges_in, 16)
            sp.dma_start(next_i[0:Q - 1, :], dst[1:(Q - 1) * J + 1].rearrange("(p j) -> p j", j=J)).then_inc(edges_in, 16)
            sp.dma_start(next_i[Q - 1:Q, 0:J - 1], dst[(Q - 1) * J + 1:E].rearrange("(a j) -> a j", a=1)).then_inc(edges_in, 16)
            sp.wait_ge(built, 1)
            sp.dma_start(records[0:P * J, :].rearrange("(p j) c -> p (j c)", j=J), rec[:, :, :].rearrange("p j c -> p (j c)")).then_inc(records_out, 16)
            sp.wait_ge(records_out, 16)

        @block.scalar
        def _(act):
            for to, of in consts:
                act.dma_start(to, of).then_inc(consts_in, 16)
            act.wait_ge(consts_in, 16 * len(consts))

        @block.gpsimd
        def _(pool):
            pool.memset(src_i[:, :], 0)
            pool.memset(w_in[:, :], 0.0)
            pool.memset(dst_i[:, :], 1 << 23).then_inc(cleared, 1)
            pool.memset(next_i[:, :], 1 << 23).then_inc(cleared, 1)
            pool.memset(rec[:, :, :], 0).then_inc(cleared, 1)
            pool.memset(k["ident"][:, :], 0.0).then_inc(iotas, 1)
            pool.wait_ge(iotas, 1)
            pool.affine_select(out=k["ident"][:, :], in_=k["ident"][:, :], compare_op=ALU.not_equal, fill=1.0,
                               base=0, pattern=[[-1, P]], channel_multiplier=1)
            pool.memset(k["eps"][:, :], EPS)
            pool.iota(base_i[:, :], pattern=[[GROUP, T]], base=0, channel_multiplier=0)
            pool.iota(iota_i[:, :], pattern=[[1, BLK], [BLK, P]], base=0, channel_multiplier=0).then_inc(iotas, 1)

        @block.vector
        def _(dve):
            dve.memset(ones[:, :], 1.0)
            dve.memset(zero_f[:, :], 0.0)
            dve.memset(rounds_f[:, :], 0.0)
            dve.memset(k["table"][:, :], 0).then_inc(step, 1)
            dve.wait_ge(iotas, 2)
            dve.tensor_copy(k["base"][:, :], base_i[:, :])
            dve.tensor_copy(k["iota"][:, :], iota_i[:, :]).then_inc(step, 1)
            dve.wait_ge(edges_in, 16 * 5)
            dve.tensor_copy(dst_f[:, :], dst_i[:, :])
            dve.tensor_copy(next_f[:, :], next_i[:, :]).then_inc(step, 1)
            dve.wait_ge(step, 3)
            dve.tensor_copy(rec[:, :, 0], src_i[:, :])
            dve.tensor_copy(rec[:, :, 1], dst_f[:, :].bitcast(I32))
            dve.tensor_copy(rec[:, :, 2], w_in[:, :].bitcast(I32)).then_inc(built, 1)
            dve.tensor_tensor(hit, next_f[:, :], dst_f[:, :], ALU.is_lt).then_inc(step, 1)
            dve.wait_ge(step, 4)
            dve.tensor_reduce(below[:, T:T + 1], hit, AX.X, ALU.add).then_inc(step, 1)
            dve.wait_ge(step, 5)
            for g in range(T):
                if g >= 2:
                    dve.wait_ge(step, 4 + g)
                dve.tensor_scalar(hits[:, g % 2, :], dst_f[:, :], float(g * GROUP), 0.0, ALU.is_lt, ALU.add,
                                  accum_out=below[:, g:g + 1]).then_inc(step, 1)
            dve.wait_ge(step, 5 + T)
            dve.tensor_scalar(hit[:, 0:1], hit[:, 0:1], 0.0, None, ALU.mult).then_inc(counted, 1)
            dve.wait_ge(summed, 1)
            n = 6 + T - 1

            def link(ins):
                nonlocal n
                n += 1
                ins.then_inc(step, 1)
                dve.wait_ge(step, n)

            link(dve.tensor_copy(bound[:, :], sums[:, 0:T + 1]))
            link(dve.tensor_scalar(unsorted[:, :], bound[:, T:T + 1], 1.0, None, ALU.min))
            link(dve.tensor_scalar(lo_f[:, :], bound[:, 0:T], unsorted[:, 0:1], None, ALU.mult))
            link(dve.tensor_tensor(lo_f[:, :], bound[:, 0:T], lo_f[:, :], ALU.subtract))
            link(dve.memset(count_f[:, :], 0.0))
            link(dve.tensor_tensor(count_f[:, 0:T - 1], bound[:, 1:T], bound[:, 0:T - 1], ALU.subtract))
            link(dve.tensor_scalar(hit[0:1, 0:T], count_f[:, :], -1.0, float(E), ALU.mult, ALU.add))
            link(dve.tensor_scalar(hit[0:1, 0:T], hit[0:1, 0:T], unsorted[:, 0:1], None, ALU.mult))
            link(dve.tensor_tensor(count_f[:, :], count_f[:, :], hit[0:1, 0:T], ALU.add))
            for a, b, main in s.spans:
                b = T if b == s.groups else b
                link(dve.tensor_scalar(count_f[:, a:b], count_f[:, a:b], float(-main * P), 0.0, ALU.add, ALU.max))
            link(dve.tensor_scalar(count_f[:, :], count_f[:, :], float(OVER * P - 1), None, ALU.add))
            link(dve.memset(count_f[:, s.groups:T], 0.0))
            link(dve.tensor_copy(rounds_i[:, :], count_f[:, :]))
            link(dve.tensor_scalar(rounds_i[:, :], rounds_i[:, :], (OVER * P).bit_length() - 1, None, ALU.arith_shift_right))
            link(dve.tensor_copy(rounds_f[:, 1:T + 1], rounds_i[:, :]))
            link(dve.memset(prefix_f[:, :], 0.0))
            for a, b, _ in s.spans:
                link(dve.tensor_tensor_scan(prefix_f[:, a + 1:b], rounds_f[:, a + 1:b], zero_f[:, a + 1:b], 0.0, ALU.add, ALU.add))
            tab = k["table"][:, :].rearrange("a (g c) -> a g c", c=REC)
            dve.tensor_copy(tab[:, :, 0], lo_f[:, :])
            dve.tensor_copy(tab[:, :, 1], rounds_i[:, :])
            dve.tensor_copy(tab[:, :, 2], prefix_f[:, 0:T])
            for a, b, _ in s.spans:
                dve.tensor_tensor(tab[:, a:a + 1, 3], prefix_f[:, b - 1:b], rounds_f[:, b:b + 1], ALU.add)
            dve.wait_ge(consts_in, 16 * len(consts))
            link(dve.tensor_scalar(w_acc[:, 0, :], bases_s[:, 0, :], comp_s[:, 0:1], None, ALU.mult))
            for b in range(1, 8):
                to = k["W"][:, :] if b == 7 else w_acc[:, b % 2, :]
                link(dve.scalar_tensor_tensor(to, bases_s[:, b, :], comp_s[:, b:b + 1], w_acc[:, (b - 1) % 2, :], ALU.mult, ALU.add))

        @block.tensor
        def _(pe):
            pe.wait_ge(counted, 1)
            pe.matmul(sums[:, 0:T + 1], ones[:, :], below[:, :], start=True, stop=True).then_inc(summed, 1)


def node_pass(nc, s, k, kind, span, records, x_dram, rows_dram, out_dram, p_dram):
    base_group, end_group, MAIN = span
    GROUPS = end_group - base_group
    LAG = {"sage1": 2, "sage2": 0, "contrast": 2, "basis": 1, "weighted": 1}[kind]
    KEEP = RING if kind == "contrast" else 2
    X_AHEAD = 3
    normed = kind != "sage2"
    node_major = kind in ("sage1", "sage2", "contrast")
    degree = kind == "sage1"
    weighted = kind == "weighted"
    final = kind == "weighted"
    cols = MAIN + BLK

    with ExitStack() as ctx:
        def sb(name, shape, dt=F32):
            return ctx.enter_context(nc.sbuf_tensor(f"{kind}{base_group}_{name}", shape, dt))

        def pb(name, cols):
            return ctx.enter_context(nc.psum_tensor(f"{kind}{base_group}_{name}", [P, cols], F32))

        made = []

        def sem(name):
            made.append(nc.alloc_semaphore(f"{kind}{base_group}_{name}"))
            return made[-1]

        def sems(name, n):
            return [sem(f"{name}{i}") for i in range(n)]

        meta = sb("meta", [P, RING, MAIN, REC], I32)
        raw = sb("raw", [P, RING, MAIN, D])
        xin = sb("xin", [P, RING, BLK, D])
        msg = sb("msg", [P, 2, MAIN, D])
        hi = sb("msg_hi", [P, 2, MAIN, D], F32R)
        lo = sb("msg_lo", [P, 2, MAIN, D], F32R)
        rel = sb("rel_dst", [P, 2, MAIN])
        S = sb("onehot", [P, 2, MAIN, GROUP], F32R)
        st = sb("bn", [P, cols, 6])
        mv = sb("mean_var", [P, 2, cols, 2])
        std = sb("std", [P, cols])
        if kind == "contrast":
            powers = cols + 2 * BLK
            exponents = sb("exponents", [P, powers])
            exponents_o = sb("oexponents", [P, OVER])
            pow_x = sb("pow_in", [P, 2, powers])
            rstd = sb("pow_out", [P, 2, powers])
            var_o = sb("ovar", [P, OVER])
        else:
            rstd = sb("rstd", [P, 2, cols])
        nb = sb("neg_mean_rstd", [P, 2, cols])
        h = sb("h", [P, KEEP, BLK, D])
        xb = sb("x_plus_bias", [P, RING, BLK, D])
        o_s = sb("out_tile", [P, 2, BLK, D])
        zero_s = sb("zero", [1, 1])
        tick_s = sb("tick", [1, 2])
        meta_o = sb("ometa", [P, OVER, REC], I32)
        raw_o = sb("oraw", [P, OVER, D])
        msg_o = sb("omsg", [P, OVER, D])
        hi_o = sb("omsg_hi", [P, OVER, D], F32R)
        lo_o = sb("omsg_lo", [P, OVER, D], F32R)
        rel_o = sb("orel_dst", [P, OVER])
        S_o = sb("oonehot", [P, OVER, GROUP], F32R)
        st_o = sb("obn", [P, OVER, 6])
        mv_o = sb("omean_var", [P, OVER, 2])
        std_o = sb("ostd", [P, OVER])
        rstd_o = sb("orstd", [P, OVER])
        nb_o = sb("oneg_mean_rstd", [P, OVER])
        if degree:
            deg = sb("deg", [P, BLK])
            invg = sb("inv_deg", [P, BLK])
            mean = sb("mean", [P, BLK, D])
            W1l_p = sb("W1l_parts", [P, 2, HID], F32R)
            W1r_p = sb("W1r_parts", [P, 2, HID], F32R)
            W2_p = sb("W2_parts", [P, 2, 2, 2 * D], F32R)
            hT = sb("hT_parts", [P, 2, GROUP], F32R)
            mT = sb("meanT_parts", [P, 2, GROUP], F32R)
            HT = sb("hiddenT", [P, 2, GROUP])
            HT_p = sb("hiddenT_parts", [P, 2, 2, 2, GROUP], F32R)
            p_s = sb("p_tile", [P, 2, BLK, D])
            ones = sb("ones", [P, 2], F32R)
            deg_row = sb("deg_row", [2, GROUP])
            degrees = pb("degrees", 512)
            tr = pb("transposed", 512)
            hid = pb("hidden", 1024)
            outp = pb("out", 1024)
            out_blocks = outp[:, :].rearrange("p (b c) -> p b c", b=BLK)
        sum_banks = pb("agg", 512 if degree else 1024)
        if node_major:
            aggT = sb("aggT_copy", [P, GROUP])
            agg = pb("agg_rows", 512)
        if kind == "sage2":
            invg = sb("inv_deg", [P, BLK])
        if kind == "contrast":
            invg = sb("inv_deg", [P, BLK])
            diff = sb("diff", [P, BLK, D])
            sq = diff
            th = sb("tanh", [P, BLK])
            ta = sb("alpha_tanh", [P, BLK])
            hT = sb("hT", [P, GROUP])
            hc = sb("hiddenT", [HALF + 1, GROUP])
            e_s = sb("enhanced", [P, 2, BLK, D])
            st2 = sb("bn2", [P, BLK, 6])
            mv2 = sb("mean_var2", [P, BLK, 2])
            nb2 = sb("nb2", [P, BLK])
            n_s = sb("normed", [P, BLK, D])
            ng_s = sb("normed_gamma", [P, BLK, D])
            tr = pb("transposed", 512)
            hid = pb("hidden", 512)
            outp = pb("out", 512)
        if kind == "basis":
            aT = sb("aggT", [P, GROUP])
            hT = sb("hT", [P, GROUP])
            tr = pb("transposed", 512)
            outp = pb("out", 512)
        if kind == "weighted":
            zT = sb("zT", [P, GROUP])
            gT = sb("hiddenT", [P, GROUP])
            hid = pb("hidden", 512)
            outp = pb("out", 512)

        meta_in = sems("meta_in", RING)
        x_in = sems("x_in", RING)
        raw_in = [sems(f"raw_in{c}_", RING) for c in range(MAIN)]
        seg = sems("onehot_built", RING)
        stats = sem("stats")
        moments = sem("moments")
        std_ready = sem("std")
        rstd_ready = sem("rstd")
        coef = sem("coef")
        relset = sem("rel")
        rows_ready = sems("rows_ready", RING)
        lo_ready = sems("lo_ready", RING)
        h_ready = sems("h_ready", RING)
        xb_ready = sems("xb_ready", RING)
        agg_done = sems("agg_done", RING)
        out_ready = sems("out_ready", 2)
        stored = sems("stored", 2)
        cleared = sem("cleared")
        zeroed = sem("zeroed")
        tick = sem("tick")
        o_tick = sem("otick")
        meta_o_in = sem("ometa_in")
        raw_o_in = sems("oraw_in", OVER)
        o_stats = sem("ostats")
        o_moments = sem("omoments")
        o_std = sem("ostd")
        o_rstd = sem("orstd")
        o_coef = sem("ocoef")
        o_rel = sem("orel")
        o_seg = sem("oonehot_built")
        o_rows = sem("orows_ready")
        o_lo = sem("olo_ready")
        o_agg = sem("oagg_done")
        if weighted:
            unweighted = sem("unweighted")
            o_unweighted = sem("ounweighted")
        else:
            unweighted = o_unweighted = None
        aggT_copied = sem("aggT_copied")
        agg_rows = sem("agg_rows_done")
        if degree:
            p_ready = sems("p_ready", 2)
            p_stored = sems("p_stored", 2)
        dense = {n: sem(n) for n in {
            "sage1": ["deg_row_copied", "deg_columns", "deg_max", "inv_done", "mean_ready", "weights_high", "weights_ready", "hT_high",
                      "mT_high", "HT_high", "HT_low", "out_b_read", "p_a_read", "hT_psum", "mT_psum", "hT_ready", "mT_ready", "hid_a",
                      "hid_b", "HT_a", "HT_b", "out_psum"],
            "sage2": ["inv_copied"],
            "contrast": ["inv_copied", "diff_done", "sq_done", "ssq_done", "pow_clear", "pow_in", "pow_done", "tanh_done",
                         "ta_done", "hT_psum", "hT_ready", "hid_psum", "hc_ready", "out_psum", "e_done", "st2_done",
                         "mv2_done", "coef2", "n_ready", "ng_ready", "o_var"],
            "basis": ["hT_psum", "hT_ready", "aT_ready", "out_psum"],
            "weighted": ["zT_ready", "hid_psum", "gT_ready", "out_psum"],
        }[kind]}
        passed = ExitStack()
        block = passed.enter_context(nc.Block())

        def agg_of(group):
            q = 0 if degree else slot(group, 2)
            return sum_banks[:, q * 512:(q + 1) * 512]

        mf = meta[:, :, :, :].bitcast(F32)
        mof = meta_o[:, :, :].bitcast(F32)

        def node_group(group):
            return number(group) + base_group

        def past_end(group):
            return static(group) and number(group) >= GROUPS

        def done(count):
            return max(count, 0) if isinstance(count, int) else count

        looks_for_rounds = [True]

        def quads(eng, step, last=None):
            turns = GROUPS // RING

            def run():
                for q in range(RING):
                    step((0, q))
                if turns > 2:
                    with eng.Fori(1, turns - 1) as t:
                        for q in range(RING):
                            step((t, q))
                for q in range(RING):
                    (last or step)((turns - 1, q))

            most = -(-s.edges // (OVER * P))
            rounds = table(eng, (0, 0), 3, most * s.table)
            looks_for_rounds[0] = False
            with eng.If(rounds == 0):
                run()
            looks_for_rounds[0] = True
            with eng.If(rounds > 0):
                run()

        final_group = (GROUPS // RING - 1, RING - 1)

        def table(eng, group, word, most):
            at = node_group(group) * REC + word
            return eng.value_load(k["table"][0:1, bass.ds(at, 1)], min_val=0, max_val=most)

        def rounds_of(eng, group, body):
            if not looks_for_rounds[0]:
                return
            most = -(-s.edges // (OVER * P))
            n = table(eng, group, 1, most)
            with eng.If(n > 0):
                before = table(eng, group, 2, most * s.table)
                with eng.Fori(0, n) as i:
                    body(i, before + i)

        def rows_of(dram, g, n=GROUP):
            return dram[bass.ds(g * GROUP, n), :].rearrange("(p b) f -> p (b f)", b=BLK)

        @block.sync
        def _(sp):
            def load_meta(group):
                if past_end(group):
                    return
                r, u = slot(group, RING), turn(group, RING)
                for c in range(MAIN):
                    sp.wait_ge(raw_in[c][r], u * 16)
                sp.wait_ge(seg[r], u)
                if weighted:
                    sp.wait_ge(lo_ready[r], u)
                    sp.wait_ge(rows_ready[r], u)
                first = table(sp, group, 0, s.edges)
                sp.dma_start(meta[:, r, :, :].rearrange("p c w -> p (c w)"),
                             records[bass.ds(first, MAIN * P), :].rearrange("(p c) w -> p (c w)", c=MAIN)
                             ).then_inc(meta_in[r], 16)

            def load_x(group, where, parts=P):
                r, u = slot(group, RING), turn(group, RING)
                if normed:
                    sp.wait_ge(xb_ready[r], u)
                    sp.wait_ge(h_ready[r], u)
                else:
                    sp.wait_ge(out_ready[slot(group, 2)], done(turn(group, 2) - 1))
                sp.dma_start(xin[0:parts, r, :, :].rearrange("p b f -> p (b f)"), rows_of(x_dram, where, parts * BLK)
                             ).then_inc(x_in[r], 16)

            def x_or_tail(group):
                if past_end(group):
                    return
                g = node_group(group)
                if g < s.tail_group or (x_dram.shape[0] > s.nodes and g < s.groups):
                    load_x(group, g)
                elif g == s.tail_group and s.tail:
                    load_x(group, g, s.tail // BLK)
                else:
                    load_x(group, 0)

            def overflow(group):
                if not looks_for_rounds[0]:
                    return
                most = -(-s.edges // (OVER * P))
                n = table(sp, group, 1, most)
                with sp.If(n > 0):
                    first = table(sp, group, 0, s.edges)
                    before = table(sp, group, 2, s.table * most)
                    with sp.Fori(0, n) as i:
                        o = before + i
                        sp.wait_ge(o_rows, o + 1)
                        sp.wait_ge(o_seg, o + 1)
                        if weighted:
                            sp.wait_ge(o_lo, o + 1)
                        at = first + MAIN * P + i * (OVER * P)
                        sp.dma_start(meta_o[:, :, :].rearrange("p c w -> p (c w)"),
                                     records[bass.ds(at, OVER * P), :].rearrange("(p c) w -> p (c w)", c=OVER)
                                     ).then_inc(meta_o_in, 16)

            def store(group, parts=P):
                q, g = slot(group, 2), node_group(group)
                if degree:
                    sp.wait_ge(p_ready[q], turn(group, 2) + 1)
                    sp.dma_start(rows_of(p_dram, g), p_s[:, q, :, :].rearrange("p b f -> p (b f)")).then_inc(p_stored[q], 16)
                sp.wait_ge(out_ready[q], turn(group, 2) + 1)
                sp.dma_start(rows_of(out_dram, g, parts * BLK), o_s[0:parts, q, :, :].rearrange("p b f -> p (b f)")
                             ).then_inc(stored[q], 16)

            def store_if(group):
                if static(group) and number(group) < 0:
                    return
                if static(group) and final and node_group(group) >= s.tail_group:
                    if node_group(group) == s.tail_group and s.tail:
                        store(group, s.tail // BLK)
                    return
                store(group)

            def step(group):
                overflow(group)
                load_x(ahead(group, X_AHEAD), node_group(ahead(group, X_AHEAD)))
                store_if(ahead(group, -LAG))
                load_meta(ahead(group, 5))

            def last(group):
                overflow(group)
                x_or_tail(ahead(group, X_AHEAD))
                store_if(ahead(group, -LAG))
                load_meta(ahead(group, 5))

            for g in range(RING):
                load_meta((0, g))
            for g in range(X_AHEAD):
                load_x((0, g), base_group + g)
            load_meta((0, RING))
            quads(sp, step, last)
            for lag in range(LAG - 1, -1, -1):
                store_if(ahead(final_group, -lag))
            full = GROUPS if not final else min(GROUPS, s.tail_group + (s.tail > 0) - base_group)
            for q in range(2):
                n = (full + 1 - q) // 2
                sp.wait_ge(stored[q], 16 * n)
                if degree:
                    sp.wait_ge(p_stored[q], 16 * n)
            if GROUPS > 3 * RING:
                sp.wait_ge(meta_in[0], 16 * (GROUPS // RING + 1))

        bias_of = {"sage1": "b2l", "contrast": "beta", "basis": "bias", "weighted": "v2"}

        @block.gpsimd
        def _(pool):
            pool.memset(zero_s[:, :], 0.0).then_inc(zeroed, 1)
            pool.memset(tick_s[:, 0:1], 0.0).then_inc(tick, 1)
            pool.memset(tick_s[:, 1:2], 0.0).then_inc(o_tick, 1)
            pool.wait_ge(zeroed, 1)
            if degree:
                pool.memset(ones[:, :].bitcast(F32), 1.0).then_inc(cleared, 1)
            if kind == "contrast":
                pool.memset(hc[HALF:HALF + 1, :], 1.0).then_inc(cleared, 1)
                pool.wait_ge(cleared, 1)
                pool.memset(exponents_o[:, :], -0.5)
                pool.memset(exponents[:, 0:cols], -0.5)
                pool.memset(exponents[:, cols:cols + BLK], 0.5)
                pool.memset(exponents[:, cols + BLK:powers], -0.5).then_inc(cleared, 1)
                pool.wait_ge(cleared, 2)

            def carry(n, sem_):
                pool.wait_ge(sem_, n)
                pool.tensor_tensor(tick_s[:, 0:1], zero_s[:, :], zero_s[:, :], ALU.add).then_inc(sem_, 1)

            def gather(group):
                if past_end(group):
                    return
                r, u = slot(group, RING), turn(group, RING)
                pool.wait_ge(meta_in[r], (u + 1) * 16)
                pool.wait_ge(rows_ready[r], u)
                if not normed:
                    pool.wait_ge(lo_ready[r], u)
                if not static(group):
                    carry(number(group) - (2 * RING - 1), tick)
                for c in range(MAIN):
                    pool.indirect_dma_start(raw[:, r, c, :], None, rows_dram,
                                            bass.IndirectOffsetOnAxis(ap=meta[:, r, c, 0:1], axis=0)
                                            ).then_inc(raw_in[c][r], 16)

            def add_bias(group):
                if past_end(group):
                    return
                r, q = slot(group, RING), slot(group, 2)
                pool.wait_ge(x_in[r], (turn(group, RING) + 1) * 16)
                pool.wait_ge(out_ready[q], done(turn(group, 2) - 1))
                b = k[bias_of[kind]][:, :]
                pool.tensor_tensor(xb[:, r, :, :], xin[:, r, :, :], b.unsqueeze(1).to_broadcast([P, BLK, D]), ALU.add
                                   ).then_inc(xb_ready[r], 1)

            def overflow(i, o):
                pool.wait_ge(meta_o_in, (o + 1) * 16)
                pool.wait_ge(o_rows, o + 1)
                if not normed:
                    pool.wait_ge(o_lo, o + 1)
                pool.wait_ge(o_tick, o + 1)
                pool.tensor_tensor(tick_s[:, 1:2], zero_s[:, :], zero_s[:, :], ALU.add).then_inc(o_tick, 1)
                for j in range(OVER):
                    pool.indirect_dma_start(raw_o[:, j, :], None, rows_dram,
                                            bass.IndirectOffsetOnAxis(ap=meta_o[:, j, 0:1], axis=0)
                                            ).then_inc(raw_o_in[j], 16)
                if kind == "contrast":
                    pool.wait_ge(dense["o_var"], o + 1)
                    pool.tensor_tensor(rstd_o[:, :], var_o[:, :], exponents_o[:, :], ALU.pow).then_inc(o_std, 1)

            def raise_powers(n):
                q, g = slot(n, 2), number(n)
                pool.wait_ge(dense["pow_in"], g + 1)
                p = ahead(n, -2)
                if not past_end(p):
                    pool.wait_ge(coef, done(g - 1))
                    pool.wait_ge(h_ready[slot(p, RING)], done(turn(p, RING) + 1))
                    pool.wait_ge(rows_ready[slot(p, RING)], done(turn(p, RING) + 1))
                pool.wait_ge(dense["tanh_done"], done(g - 3))
                pool.wait_ge(dense["n_ready"], done(g - 4))
                pool.tensor_tensor(rstd[:, q, :], pow_x[:, q, :], exponents[:, :], ALU.pow).then_inc(dense["pow_done"], 1)

            def times_gamma(group):
                pool.wait_ge(dense["n_ready"], number(group) + 1)
                p = ahead(group, -1)
                pool.wait_ge(out_ready[slot(p, 2)], turn(p, 2) + 1)
                pool.tensor_tensor(ng_s[:, :, :], n_s[:, :, :], k["gamma"][:, :].unsqueeze(1).to_broadcast([P, BLK, D]),
                                   ALU.mult).then_inc(dense["ng_ready"], 1)

            def step(group):
                rounds_of(pool, group, overflow)
                gather(ahead(group, 4))
                if normed:
                    add_bias(ahead(group, 1))
                if kind == "contrast":
                    if not (static(group) and number(group) < 2):
                        times_gamma(ahead(group, -2))
                    raise_powers(ahead(group, 2))

            for g in range(RING):
                gather((0, g))
            if normed:
                add_bias((0, 0))
            if kind == "contrast":
                for g in range(2):
                    raise_powers((0, g))
            quads(pool, step)
            if kind == "contrast":
                times_gamma(ahead(final_group, -1))
                raise_powers(ahead(final_group, 3))
                times_gamma(final_group)

        @block.vector
        def _(dve):
            def ln_moments(group):
                if past_end(group):
                    return
                r, g = slot(group, RING), number(group)
                for c in range(MAIN):
                    dve.wait_ge(raw_in[c][r], (turn(group, RING) + 1) * 16)
                dve.wait_ge(x_in[r], (turn(group, RING) + 1) * 16)
                if kind != "contrast":
                    dve.wait_ge(std_ready, done(g - 1))
                for c in range(cols):
                    of = raw[:, r, c, :] if c < MAIN else xin[:, r, c - MAIN, :]
                    last = dve.bn_stats(st[:, c, :], of)
                last.then_inc(stats, 1)
                dve.wait_ge(stats, g + 1)
                relative(group)
                for c in range(cols):
                    last = dve.bn_aggr(mv[:, slot(group, 2), c, :], st[:, c, :])
                last.then_inc(moments, 1)
                if kind == "contrast":
                    dve.wait_ge(moments, g + 1)
                    dve.wait_ge(dense["pow_done"], done(g - 1))
                    ins = dve.tensor_scalar(pow_x[:, slot(group, 2), 0:cols], mv[:, slot(group, 2), :, 1], EPS, None, ALU.add)
                    if static(group) and g < 2:
                        ins.then_inc(dense["pow_in"], 1)

            def ln_coefficients(group):
                if past_end(group):
                    return
                q, g = slot(group, 2), number(group)
                dve.wait_ge(dense["pow_done"] if kind == "contrast" else std_ready, g + 1)
                p = ahead(group, -2)
                dve.wait_ge(h_ready[slot(p, RING)], turn(p, RING) + 1)
                dve.wait_ge(rows_ready[slot(p, RING)], turn(p, RING) + 1)
                if kind != "contrast":
                    dve.reciprocal(rstd[:, q, :], std[:, :]).then_inc(rstd_ready, 1)
                    dve.wait_ge(rstd_ready, g + 1)
                dve.scalar_tensor_tensor(nb[:, q, :], mv[:, q, :, 0], -1.0, rstd[:, q, 0:cols], ALU.mult, ALU.mult).then_inc(coef, 1)

            def relative(group):
                r, q, g = slot(group, RING), slot(group, 2), number(group)
                dve.wait_ge(meta_in[r], (turn(group, RING) + 1) * 16)
                dve.tensor_tensor(rel[:, q, :], mf[:, r, :, 1], k["base"][:, bass.ds(g + base_group, 1)].to_broadcast([P, MAIN]), ALU.subtract
                                  ).then_inc(relset, 1)

            def one_hot(group):
                r, q, g = slot(group, RING), slot(group, 2), number(group)
                if not normed:
                    relative(group)
                dve.wait_ge(relset, g + 1)
                for c in range(MAIN):
                    last = dve.tensor_scalar(S[:, q, c, :], k["iota"][:, :], rel[:, q, c:c + 1], None, ALU.is_equal)
                last.then_inc(seg[r], 1)

            def low_parts(group):
                r, q, g = slot(group, RING), slot(group, 2), number(group)
                dve.wait_ge(rows_ready[r], turn(group, RING) + 1)
                if weighted:
                    for c in range(MAIN):
                        last = dve.scalar_tensor_tensor(lo[:, q, c, :], msg[:, q, c, :], mf[:, r, c, 2:3], hi[:, q, c, 0:D].bitcast(F32),
                                                        ALU.mult, ALU.subtract)
                    last.then_inc(lo_ready[r], 1)
                    return
                of = msg[:, q, :, :] if normed else raw[:, r, :, :]
                dve.tensor_tensor(lo[:, q, :, :], of, hi[:, q, :, 0:D].bitcast(F32), ALU.subtract).then_inc(lo_ready[r], 1)

            def overflow(group):
                g = node_group(group)

                def relative_over(o):
                    dve.wait_ge(meta_o_in, (o + 1) * 16)
                    dve.tensor_tensor(rel_o[:, :], mof[:, :, 1], k["base"][:, bass.ds(g, 1)].to_broadcast([P, OVER]), ALU.subtract
                                      ).then_inc(o_rel, 1)

                def body(i, o):
                    if normed:
                        for j in range(OVER):
                            dve.wait_ge(raw_o_in[j], (o + 1) * 16)
                            last = dve.bn_stats(st_o[:, j, :], raw_o[:, j, :])
                        last.then_inc(o_stats, 1)
                        dve.wait_ge(o_stats, o + 1)
                        relative_over(o)
                        for j in range(OVER):
                            last = dve.bn_aggr(mv_o[:, j, :], st_o[:, j, :])
                        last.then_inc(o_moments, 1)
                        if kind == "contrast":
                            dve.wait_ge(o_moments, o + 1)
                            dve.tensor_scalar(var_o[:, :], mv_o[:, :, 1], EPS, None, ALU.add).then_inc(dense["o_var"], 1)
                    else:
                        relative_over(o)
                    dve.wait_ge(o_agg, o + 1)
                    dve.wait_ge(o_rel, o + 1)
                    for j in range(OVER):
                        last = dve.tensor_scalar(S_o[:, j, :], k["iota"][:, :], rel_o[:, j:j + 1], None, ALU.is_equal)
                    last.then_inc(o_seg, 1)
                    if normed:
                        dve.wait_ge(o_std, o + 1)
                        dve.wait_ge(o_rows, o + 1)
                        if kind != "contrast":
                            dve.reciprocal(rstd_o[:, :], std_o[:, :]).then_inc(o_rstd, 1)
                            dve.wait_ge(o_rstd, o + 1)
                        dve.scalar_tensor_tensor(nb_o[:, :], mv_o[:, :, 0], -1.0, rstd_o[:, :], ALU.mult, ALU.mult).then_inc(o_coef, 1)
                    dve.wait_ge(o_rows, o + 2)
                    if weighted:
                        for j in range(OVER):
                            last = dve.scalar_tensor_tensor(lo_o[:, j, :], msg_o[:, j, :], mof[:, j, 2:3], hi_o[:, j, 0:D].bitcast(F32),
                                                            ALU.mult, ALU.subtract)
                        last.then_inc(o_lo, 1)
                        return
                    of = msg_o[:, :, :] if normed else raw_o[:, :, :]
                    dve.tensor_tensor(lo_o[:, :, :], of, hi_o[:, :, 0:D].bitcast(F32), ALU.subtract).then_inc(o_lo, 1)

                rounds_of(dve, group, body)

            def prepare(group):
                if past_end(group):
                    return
                w, need = before(group)
                dve.wait_ge(agg_done[w], need)
                one_hot(group)
                low_parts(group)

            def out_sum(group):
                q = slot(group, 2)
                if kind == "contrast":
                    dve.wait_ge(dense["ng_ready"], number(group) + 1)
                    term = ng_s[:, :, :]
                else:
                    dve.wait_ge(dense["out_psum"], number(group) + 1)
                    term = outp[:, 0:GROUP].rearrange("p (b c) -> p b c", b=BLK)
                dve.wait_ge(stored[q], turn(group, 2) * 16)
                dve.wait_ge(xb_ready[slot(group, RING)], turn(group, RING) + 1)
                if kind == "sage1":
                    for half in (1, 0):
                        bb = slice(2 * half, 2 * half + 2)
                        if half == 0:
                            dve.wait_ge(dense["p_a_read"], number(group) + 1)
                        ins = dve.tensor_tensor(o_s[:, q, bb, :], out_blocks[:, bb, D:2 * D], xb[:, slot(group, RING), bb, :], ALU.add)
                        ins.then_inc(dense["out_b_read"] if half else out_ready[q], 1)
                    return
                dve.tensor_tensor(o_s[:, q, :, :], term, xb[:, slot(group, RING), :, :], ALU.add).then_inc(out_ready[q], 1)

            def hT_low(group):
                dve.wait_ge(dense["hT_high"], number(group) + 1)
                dve.wait_ge(dense["hid_b"], number(group))
                dve.tensor_tensor(hT[:, 1, :], tr[:, :], hT[:, 0, :].bitcast(F32), ALU.subtract).then_inc(dense["hT_ready"], 1)

            def mean_low(group):
                g = number(group)
                dve.wait_ge(dense["mT_high"], g + 1)
                dve.wait_ge(dense["hid_b"], g)
                dve.tensor_tensor(mT[:, 1, :], tr[:, :], mT[:, 0, :].bitcast(F32), ALU.subtract).then_inc(dense["mT_ready"], 1)

            def hidden_parts(group):
                g, q = number(group), slot(group, 2)
                dve.wait_ge(dense["out_psum"], done(g - 1))
                for m in range(2):
                    dve.wait_ge(dense["HT_a" if m == 0 else "HT_b"], g + 1)
                    dve.tensor_copy(HT_p[:, q, 0, m, :], HT[:, m, :]).then_inc(dense["HT_high"], 1)
                    dve.wait_ge(dense["HT_high"], 2 * g + m + 1)
                    dve.tensor_tensor(HT_p[:, q, 1, m, :], HT[:, m, :], HT_p[:, q, 0, m, :].bitcast(F32), ALU.subtract
                                      ).then_inc(dense["HT_low"], 1)

            def degree_mean(group):
                g = number(group)
                dve.wait_ge(dense["deg_columns"], g + 1)
                dve.tensor_scalar(deg[:, :], degrees[:, 0:2 * BLK].rearrange("p (b c) -> p b c", c=2)[:, :, 0], 1.0, None, ALU.max
                                  ).then_inc(dense["deg_max"], 1)
                dve.wait_ge(dense["deg_max"], g + 1)
                dve.reciprocal(k["inv"][:, bass.ds(node_group(group) * BLK, BLK)], deg[:, :])
                dve.reciprocal(invg[:, :], deg[:, :]).then_inc(dense["inv_done"], 1)
                dve.wait_ge(dense["inv_done"], g + 1)
                dve.wait_ge(dense["mT_psum"], g)
                dve.wait_ge(agg_rows, g + 1)
                dve.tensor_tensor(mean[:, :, :], agg[:, :].rearrange("p (b f) -> p b f", b=BLK),
                                  invg[:, :].unsqueeze(2).to_broadcast([P, BLK, D]), ALU.mult).then_inc(dense["mean_ready"], 1)

            def inverse_degree(group):
                p = ahead(group, -1)
                if kind == "contrast":
                    dve.wait_ge(dense["diff_done"], number(group))
                else:
                    dve.wait_ge(out_ready[slot(p, 2)], turn(p, 2) + 1)
                dve.tensor_copy(invg[:, :], k["inv"][:, bass.ds(node_group(group) * BLK, BLK)]).then_inc(dense["inv_copied"], 1)
                dve.wait_ge(dense["inv_copied"], number(group) + 1)

            def neighbour_difference(group):
                inverse_degree(group)
                dve.wait_ge(agg_rows, number(group) + 1)
                dve.wait_ge(dense["ssq_done"], number(group))
                dve.wait_ge(h_ready[slot(group, RING)], turn(group, RING) + 1)
                for b in range(BLK):
                    last = dve.scalar_tensor_tensor(diff[:, b, :], agg[:, b * D:(b + 1) * D], invg[:, b:b + 1],
                                                    h[:, slot(group, KEEP), b, :], ALU.mult, ALU.subtract)
                last.then_inc(dense["diff_done"], 1)

            def square_sum(group):
                g, q = number(group), slot(group, 2)
                dve.wait_ge(dense["sq_done"], g + 1)
                dve.wait_ge(dense["pow_done"], g + 1)
                dve.tensor_reduce(pow_x[:, q, cols:cols + BLK], sq[:, :, :], AX.X, ALU.add).then_inc(dense["ssq_done"], 1)
                if very_first(group):
                    dve.memset(pow_x[:, q, cols + BLK:powers], 1.0).then_inc(dense["pow_in"], 1)

            def enhance(group):
                g, q = number(group), slot(group, 2)
                dve.wait_ge(dense["tanh_done"], g + 1)
                dve.tensor_scalar(ta[:, :], th[:, :], ALPHA, None, ALU.mult).then_inc(dense["ta_done"], 1)
                dve.wait_ge(dense["ta_done"], g + 1)
                dve.wait_ge(dense["out_psum"], g + 1)
                dve.wait_ge(dense["n_ready"], done(g - 1))
                for b in range(BLK):
                    last = dve.scalar_tensor_tensor(e_s[:, q, b, :], outp[:, b * D:(b + 1) * D], ta[:, b:b + 1],
                                                    h[:, slot(group, KEEP), b, :], ALU.mult, ALU.add)
                last.then_inc(dense["e_done"], 1)
                dve.wait_ge(dense["e_done"], g + 1)
                for b in range(BLK):
                    last = dve.bn_stats(st2[:, b, :], e_s[:, q, b, :])
                last.then_inc(dense["st2_done"], 1)
                dve.wait_ge(dense["st2_done"], g + 1)

            def enhanced_moments(group):
                g, q = number(group), slot(ahead(group, 3), 2)
                for b in range(BLK):
                    last = dve.bn_aggr(mv2[:, b, :], st2[:, b, :])
                last.then_inc(dense["mv2_done"], 1)
                dve.wait_ge(dense["mv2_done"], g + 1)
                dve.wait_ge(dense["pow_done"], g + 2)
                dve.tensor_scalar(pow_x[:, q, cols + BLK:powers], mv2[:, :, 1], EPS, None, ALU.add).then_inc(dense["pow_in"], 1)

            def enhanced_coefficients(group):
                g, q = number(group), slot(ahead(group, 3), 2)
                dve.wait_ge(dense["pow_done"], g + 4)
                dve.wait_ge(dense["n_ready"], g)
                dve.scalar_tensor_tensor(nb2[:, :], mv2[:, :, 0], -1.0, rstd[:, q, cols + BLK:powers], ALU.mult, ALU.mult
                                         ).then_inc(dense["coef2"], 1)

            def step(group):
                g, q, r = number(group), slot(group, 2), slot(group, RING)
                d = dense
                prev = None if very_first(group) else ahead(group, -1)
                overflow(group)
                if normed:
                    ln_moments(ahead(group, 2))
                if kind == "sage1":
                    hT_low(group)
                    degree_mean(group)
                    ln_coefficients(ahead(group, 2))
                    prepare(ahead(group, 1))
                    mean_low(group)
                    if prev:
                        hidden_parts(prev)
                    if not (static(group) and number(group) < 2):
                        out_sum(ahead(group, -2))
                if kind == "sage2":
                    prepare(ahead(group, 1))
                    inverse_degree(group)
                    dve.wait_ge(agg_rows, g + 1)
                    dve.wait_ge(x_in[r], (turn(group, RING) + 1) * 16)
                    dve.wait_ge(stored[q], turn(group, 2) * 16)
                    for b in range(BLK):
                        last = dve.scalar_tensor_tensor(o_s[:, q, b, :], agg[:, b * D:(b + 1) * D], invg[:, b:b + 1],
                                                        xin[:, r, b, :], ALU.mult, ALU.add)
                    last.then_inc(out_ready[q], 1)
                if kind == "contrast":
                    second = None if static(group) and number(group) < 2 else ahead(group, -2)
                    ln_coefficients(ahead(group, 1))
                    if second:
                        enhanced_coefficients(second)
                    neighbour_difference(group)
                    prepare(ahead(group, 1))
                    if prev:
                        enhance(prev)
                    square_sum(group)
                    if prev:
                        enhanced_moments(prev)
                    if second:
                        out_sum(second)
                if kind == "basis":
                    if prev:
                        out_sum(prev)
                    dve.wait_ge(agg_done[r], turn(group, RING) + 1)
                    dve.tensor_copy(aT[:, :], agg_of(group)).then_inc(d["aT_ready"], 1)
                    ln_coefficients(ahead(group, 2))
                    prepare(ahead(group, 1))
                if kind == "weighted":
                    if prev:
                        out_sum(prev)
                    dve.wait_ge(agg_done[r], turn(group, RING) + 1)
                    dve.wait_ge(d["hid_psum"], g)
                    dve.tensor_copy(zT[:, :], agg_of(group)).then_inc(d["zT_ready"], 1)
                    ln_coefficients(ahead(group, 2))
                    prepare(ahead(group, 1))

            dve.sem_inc(o_seg, 1)
            dve.sem_inc(o_lo, 1)
            dve.sem_inc(o_coef, 1)
            if degree:
                parts = ((W1l_p, k["W1l"]), (W1r_p, k["W1r"]), (W2_p, k["W2"]))
                for to, of in parts:
                    ins = dve.tensor_copy(to[:, 0], of[:])
                ins.then_inc(dense["weights_high"], 1)
                dve.wait_ge(dense["weights_high"], 1)
                for to, of in parts:
                    ins = dve.tensor_tensor(to[:, 1], of[:], to[:, 0].bitcast(F32), ALU.subtract)
                ins.then_inc(dense["weights_ready"], 1)
            if kind == "contrast":
                dve.memset(pow_x[:, :, :], 1.0).then_inc(dense["pow_clear"], 1)
                dve.wait_ge(dense["pow_clear"], 1)
            if normed:
                ln_moments((0, 0))
                ln_coefficients((0, 0))
                ln_moments((0, 1))
                if kind != "contrast":
                    ln_coefficients((0, 1))
            prepare((0, 0))
            quads(dve, step)
            if kind == "contrast":
                enhanced_coefficients(ahead(final_group, -1))
                enhance(final_group)
                enhanced_moments(final_group)
                out_sum(ahead(final_group, -1))
                enhanced_coefficients(final_group)
            if kind == "sage1":
                hidden_parts(final_group)
                out_sum(ahead(final_group, -1))
            if LAG:
                out_sum(final_group)

        @block.scalar
        def _(act):
            def ln_std(group):
                if past_end(group):
                    return
                g = number(group)
                act.wait_ge(moments, g + 1)
                act.wait_ge(rstd_ready, g)
                act.activation(std[:, :], mv[:, slot(group, 2), :, 1], ACT.Sqrt, bias=k["eps"][:, 0:1]).then_inc(std_ready, 1)

            def normal_rows(to, hi_to, of, bias, scale, weight, ready, count):
                ins = act.activation(to, of, ACT.Relu, bias=bias, scale=scale)
                if weighted:
                    ins.then_inc(ready, 1)
                    act.wait_ge(ready, count)
                    return act.activation(hi_to, to, ACT.Copy, scale=weight)
                return act.activation(hi_to, of, ACT.Relu, bias=bias, scale=scale)

            def rows(group):
                if past_end(group):
                    return
                r, q, g = slot(group, RING), slot(group, 2), number(group)
                w, need = before(group)
                act.wait_ge(agg_done[w], need)
                if weighted:
                    p = ahead(group, -2)
                    act.wait_ge(lo_ready[slot(p, RING)], turn(p, RING) + 1)
                if normed:
                    act.wait_ge(coef, g + 1)
                    for c in range(MAIN):
                        last = normal_rows(msg[:, q, c, :], hi[:, q, c, 0:D], raw[:, r, c, :], nb[:, q, c:c + 1], rstd[:, q, c:c + 1],
                                           mf[:, r, c, 2:3], unweighted, g * MAIN + c + 1)
                else:
                    for c in range(MAIN):
                        act.wait_ge(raw_in[c][r], (turn(group, RING) + 1) * 16)
                    last = act.activation(hi[:, q, :, 0:D], raw[:, r, :, :], ACT.Copy)
                last.then_inc(rows_ready[r], 1)

            def own(group):
                if past_end(group):
                    return
                r, q, g = slot(group, RING), slot(group, 2), number(group)
                act.wait_ge(coef, g + 1)
                if kind == "contrast":
                    act.wait_ge(dense["e_done"], done(g - 3))
                elif kind == "weighted":
                    w, need = before(group)
                    act.wait_ge(agg_done[w], need)
                if kind != "weighted":
                    act.wait_ge(dense["hT_psum"], done(g - KEEP + 1))
                for b in range(BLK):
                    c = MAIN + b
                    last = act.activation(h[:, slot(group, KEEP), b, :], xin[:, r, b, :], ACT.Relu, bias=nb[:, q, c:c + 1], scale=rstd[:, q, c:c + 1])
                last.then_inc(h_ready[r], 1)

            def overflow(i, o):
                if normed:
                    if kind != "contrast":
                        act.wait_ge(o_moments, o + 1)
                        act.wait_ge(o_coef, o + 1)
                        act.activation(std_o[:, :], mv_o[:, :, 1], ACT.Sqrt, bias=k["eps"][:, 0:1]).then_inc(o_std, 1)
                    act.wait_ge(o_coef, o + 2)
                act.wait_ge(o_agg, o + 1)
                if weighted:
                    act.wait_ge(o_lo, o + 1)
                if normed:
                    for j in range(OVER):
                        last = normal_rows(msg_o[:, j, :], hi_o[:, j, 0:D], raw_o[:, j, :], nb_o[:, j:j + 1], rstd_o[:, j:j + 1],
                                           mof[:, j, 2:3], o_unweighted, o * OVER + j + 1)
                else:
                    for j in range(OVER):
                        act.wait_ge(raw_o_in[j], (o + 1) * 16)
                    last = act.activation(hi_o[:, :, 0:D], raw_o[:, :, :], ACT.Copy)
                last.then_inc(o_rows, 1)

            def projection(group, half):
                q = slot(group, 2)
                act.wait_ge(dense["out_psum"], number(group) + 1)
                act.wait_ge(p_stored[q], turn(group, 2) * 16)
                if half == 0:
                    act.activation(p_s[:, q, 0:2, :], out_blocks[:, 0:2, 0:D], ACT.Copy).then_inc(dense["p_a_read"], 1)
                    return
                act.wait_ge(dense["out_b_read"], number(group) + 1)
                act.activation(p_s[:, q, 2:4, :], out_blocks[:, 2:4, 0:D], ACT.Copy).then_inc(p_ready[q], 1)

            def tanh(group):
                act.wait_ge(dense["pow_done"], number(group) + 3)
                act.wait_ge(dense["ta_done"], number(group))
                act.activation(th[:, :], rstd[:, slot(group, 2), cols:cols + BLK], ACT.Tanh).then_inc(dense["tanh_done"], 1)

            def enhanced_norm(group):
                g = number(group)
                act.wait_ge(dense["coef2"], g + 1)
                act.wait_ge(dense["ng_ready"], g)
                for b in range(BLK):
                    c = cols + BLK + b
                    last = act.activation(n_s[:, b, :], e_s[:, slot(group, 2), b, :], ACT.Identity, bias=nb2[:, b:b + 1],
                                          scale=rstd[:, slot(ahead(group, 3), 2), c:c + 1])
                last.then_inc(dense["n_ready"], 1)

            def copy_hT(group, read):
                act.wait_ge(dense["hT_psum"], number(group) + 1)
                act.wait_ge(dense[read], number(group))
                act.activation(hT[:, :], tr[:, 0:GROUP], ACT.Copy).then_inc(dense["hT_ready"], 1)

            def step(group):
                g, q = number(group), slot(group, 2)
                d = dense
                nxt, prev = ahead(group, 1), None if very_first(group) else ahead(group, -1)
                rounds_of(act, group, overflow)
                if node_major:
                    act.wait_ge(agg_done[slot(group, RING)], turn(group, RING) + 1)
                    act.wait_ge(agg_rows, g)
                    act.activation(aggT[:, :], agg_of(group), ACT.Copy).then_inc(aggT_copied, 1)
                if kind == "contrast":
                    copy_hT(group, "hid_psum")
                    if prev:
                        tanh(prev)
                if degree:
                    act.wait_ge(d["deg_columns"], g)
                    act.activation(deg_row[:, :], degrees[0:2, :], ACT.Copy).then_inc(d["deg_row_copied"], 1)
                    ln_std(ahead(group, 2))
                    act.wait_ge(d["hT_psum"], g + 1)
                    act.wait_ge(d["hid_b"], g)
                    act.activation(hT[:, 0, :], tr[:, :], ACT.Copy).then_inc(d["hT_high"], 1)
                rows(nxt)
                if kind == "sage1":
                    act.wait_ge(d["mT_psum"], g + 1)
                    act.wait_ge(d["hid_b"], g)
                    act.activation(mT[:, 0, :], tr[:, :], ACT.Copy).then_inc(d["mT_high"], 1)
                    own(nxt)
                    second = None if static(group) and number(group) < 2 else ahead(group, -2)
                    if second:
                        projection(second, 0)
                    for m, (psum, ready) in enumerate((("hid_a", "HT_a"), ("hid_b", "HT_b"))):
                        act.wait_ge(d[psum], g + 1)
                        act.wait_ge(d["HT_low"], 2 * g)
                        act.activation(HT[:, m, :], hid[:, m * 512:(m + 1) * 512], ACT.Relu, bias=k["b1l"][:, m:m + 1]).then_inc(d[ready], 1)
                    if second:
                        projection(second, 1)
                if kind == "contrast":
                    if not (static(group) and number(group) < 2):
                        enhanced_norm(ahead(group, -2))
                    act.wait_ge(d["diff_done"], g + 1)
                    act.activation(sq[:, :, :], diff[:, :, :], ACT.Square).then_inc(d["sq_done"], 1)
                    act.wait_ge(d["hid_psum"], g + 1)
                    act.wait_ge(d["out_psum"], g)
                    act.activation(hc[0:HALF, :], hid[0:HALF, :], ACT.Relu, bias=k["c1"][:, 0:1]).then_inc(d["hc_ready"], 1)
                    own(nxt)
                if kind == "basis":
                    copy_hT(group, "out_psum")
                    ln_std(ahead(group, 2))
                    own(nxt)
                if kind == "weighted":
                    ln_std(ahead(group, 2))
                    act.wait_ge(d["hid_psum"], g + 1)
                    act.wait_ge(d["out_psum"], g)
                    act.activation(gT[:, :], hid[:, :], ACT.Relu, bias=k["v1"][:, 0:1]).then_inc(d["gT_ready"], 1)
                    own(nxt)

            act.sem_inc(o_rows, 1)
            if normed:
                if kind != "contrast":
                    ln_std((0, 0))
                    ln_std((0, 1))
                own((0, 0))
            rows((0, 0))
            quads(act, step)
            if kind == "sage1":
                for group in (ahead(final_group, -1), final_group):
                    for half in range(2):
                        projection(group, half)
            if kind == "contrast":
                tanh(final_group)
                enhanced_norm(ahead(final_group, -1))
                enhanced_norm(final_group)

        @block.tensor
        def _(pe):
            def sum_chunk(group, S_c, hi_c, lo_c, first, last):
                if degree:
                    pe.matmul(degrees[0:2, :], ones[:, :], S_c, start=first, stop=last, skip_group_check=True)
                pe.matmul(agg_of(group), hi_c, S_c, start=first, stop=False, skip_group_check=True)
                return pe.matmul(agg_of(group), lo_c, S_c, start=False, stop=last, skip_group_check=True)

            def overflow(group, i, o):
                pe.wait_ge(o_lo, o + 2)
                pe.wait_ge(o_seg, o + 2)
                for j in range(OVER):
                    ins = sum_chunk(group, S_o[:, j, :], hi_o[:, j, :], lo_o[:, j, :], False, False)
                ins.then_inc(o_agg, 1)

            def transposes(psum, of):
                for b in range(BLK):
                    ins = pe.transpose(psum[:, b * P:(b + 1) * P], of[:, b, :], k["ident"][:, :])
                return ins

            def sum_rows(group):
                g = number(group)
                if degree:
                    pe.wait_ge(dense["deg_row_copied"], g + 1)
                    pe.wait_ge(dense["mean_ready"], g)
                elif kind == "contrast":
                    pe.wait_ge(dense["diff_done"], g)
                else:
                    p = ahead(group, -1)
                    pe.wait_ge(out_ready[slot(p, 2)], turn(p, 2) + 1)
                pe.wait_ge(aggT_copied, g + 1)
                for b in range(BLK):
                    ins = pe.transpose(agg[:, b * D:(b + 1) * D], aggT[:, b * P:(b + 1) * P], k["ident"][:, :])
                ins.then_inc(agg_rows, 1)
                if degree:
                    for b in range(BLK):
                        ins = pe.transpose(degrees[:, 2 * b:2 * b + 2], deg_row[:, b * P:(b + 1) * P], k["ident"][0:2, 0:2])
                    ins.then_inc(dense["deg_columns"], 1)

            def enhanced(group):
                pe.wait_ge(dense["hc_ready"], number(group) + 1)
                pe.wait_ge(cleared, 1)
                pe.wait_ge(dense["e_done"], number(group))
                for b in range(BLK):
                    ins = pe.matmul(outp[:, b * D:(b + 1) * D], hc[:, b * P:(b + 1) * P], k["C2"][:, :], start=True, stop=True)
                ins.then_inc(dense["out_psum"], 1)

            def outputs(group, half):
                g, q, prev = number(group), slot(group, 2), ahead(group, -1)
                pe.wait_ge(dense["HT_low"], 2 * (g + 1))
                pe.wait_ge(out_ready[slot(prev, 2)], turn(prev, 2) + 1)
                pe.wait_ge(p_ready[slot(prev, 2)], turn(prev, 2) + 1)
                for b in (2 * half, 2 * half + 1):
                    for m in range(2):
                        for n, (a, w) in enumerate(PRODUCTS):
                            ins = pe.matmul(out_blocks[:, b, :], HT_p[:, q, a, m, b * P:(b + 1) * P], W2_p[:, w, m, :],
                                            start=m == 0 and n == 0, stop=m == 1 and n == 2)
                if half:
                    ins.then_inc(dense["out_psum"], 1)

            def hidden(parts, of, m, first):
                for n, (a, w) in enumerate(PRODUCTS):
                    ins = pe.matmul(hid[:, m * 512:(m + 1) * 512], parts[:, w, m * P:(m + 1) * P], of[:, a, :],
                                    start=first and n == 0, stop=not first and n == 2)
                return ins

            def step(group):
                g, q, r = number(group), slot(group, 2), slot(group, RING)
                d = dense
                pe.wait_ge(lo_ready[r], turn(group, RING) + 1)
                pe.wait_ge(seg[r], turn(group, RING) + 1)
                if kind == "sage1":
                    pe.wait_ge(aggT_copied, g)
                    pe.wait_ge(d["deg_max"], g)
                elif kind == "basis":
                    pe.wait_ge(d["aT_ready"], done(g - 1))
                elif kind == "weighted":
                    pe.wait_ge(d["zT_ready"], done(g - 1))
                else:
                    pe.wait_ge(aggT_copied, done(g - 1))
                sum_chunk(group, S[:, q, 0, :], hi[:, q, 0, :], lo[:, q, 0, :], True, False)
                rounds_of(pe, group, lambda i, o: overflow(group, i, o))
                if kind == "weighted":
                    for c in range(1, MAIN):
                        sum_chunk(group, S[:, q, c, :], hi[:, q, c, :], lo[:, q, c, :], False, False)
                    pe.wait_ge(h_ready[r], turn(group, RING) + 1)
                    for b in range(BLK):
                        ins = pe.matmul(agg_of(group)[:, b * P:(b + 1) * P], h[:, q, b, :], k["ident"][:, :], start=False, stop=b == BLK - 1,
                                        skip_group_check=True)
                    ins.then_inc(agg_done[r], 1)
                    pe.wait_ge(d["zT_ready"], g + 1)
                    pe.wait_ge(d["gT_ready"], g)
                    pe.matmul(hid[:, :], k["V1"][:, :], zT[:, :], start=True, stop=True).then_inc(d["hid_psum"], 1)
                    p = ahead(group, -1)
                    pe.wait_ge(d["gT_ready"], g + 1)
                    pe.wait_ge(out_ready[slot(p, 2)], turn(p, 2) + 1)
                    for b in range(BLK):
                        ins = pe.matmul(outp[:, b * D:(b + 1) * D], gT[:, b * P:(b + 1) * P], k["V2"][:, :], start=True, stop=True)
                    ins.then_inc(d["out_psum"], 1)
                    return
                for c in range(1, MAIN):
                    ins = sum_chunk(group, S[:, q, c, :], hi[:, q, c, :], lo[:, q, c, :], False, c == MAIN - 1)
                ins.then_inc(agg_done[r], 1)
                if kind == "sage2":
                    sum_rows(group)
                    return
                pe.wait_ge(h_ready[r], turn(group, RING) + 1)
                pe.wait_ge(d["hT_ready"], g)
                if kind == "sage1":
                    pe.wait_ge(d["mT_ready"], g)
                transposes(tr[:, 0:GROUP], h[:, slot(group, KEEP), :, :]).then_inc(d["hT_psum"], 1)
                late = kind == "sage1" and not (static(group) and number(group) < 2)
                if late:
                    outputs(ahead(group, -2), 0)
                if kind in ("sage1", "contrast"):
                    sum_rows(group)
                if kind == "sage1":
                    pe.wait_ge(d["hT_ready"], g + 1)
                    pe.wait_ge(d["HT_b"], g)
                    for m in range(2):
                        hidden(W1r_p, hT, m, True)
                    pe.wait_ge(d["mean_ready"], g + 1)
                    transposes(tr[:, :], mean[:, :, :]).then_inc(d["mT_psum"], 1)
                    if late:
                        outputs(ahead(group, -2), 1)
                    pe.wait_ge(d["mT_ready"], g + 1)
                    for m, name in enumerate(("hid_a", "hid_b")):
                        hidden(W1l_p, mT, m, False).then_inc(d[name], 1)
                if kind == "contrast":
                    if not very_first(group):
                        enhanced(ahead(group, -1))
                    pe.wait_ge(d["hT_ready"], g + 1)
                    pe.wait_ge(d["hc_ready"], g)
                    pe.matmul(hid[0:HALF, :], k["C1"][:, :], hT[:, :], start=True, stop=True).then_inc(d["hid_psum"], 1)
                if kind == "basis":
                    pe.wait_ge(d["hT_ready"], g + 1)
                    pe.wait_ge(d["aT_ready"], g + 1)
                    pe.wait_ge(out_ready[(q + 1) % 2], turn(ahead(group, 1), 2))
                    for b in range(BLK):
                        pe.matmul(outp[:, b * D:(b + 1) * D], hT[:, b * P:(b + 1) * P], k["root"][:, :], start=True, stop=False)
                        ins = pe.matmul(outp[:, b * D:(b + 1) * D], aT[:, b * P:(b + 1) * P], k["W"][:, :], start=False, stop=True)
                    ins.then_inc(d["out_psum"], 1)

            pe.sem_inc(o_agg, 1)
            if degree:
                pe.wait_ge(cleared, 1)
                pe.wait_ge(dense["weights_ready"], 1)
            quads(pe, step)
            if kind == "contrast":
                enhanced(final_group)
            if kind == "sage1":
                for group in (ahead(final_group, -1), final_group):
                    for half in range(2):
                        outputs(group, half)

        passed.close()
        nc.clear_and_free_semaphores(made)
        nc.all_engine_barrier()


def kernel(**inputs):
    import numpy as np
    import concourse.bacc as bacc
    from concourse import mybir as mb
    from concourse.bass_utils import run_bass_kernel_spmd as run

    a = {n: np.asarray(v) for n, v in inputs.items()}

    def rows(v):
        return np.ascontiguousarray(np.broadcast_to(v.reshape(1, -1), (128, v.size)))

    given = [
        ("x", a["x"]), ("src", a["src"]), ("dst", a["dst"]), ("edge_weight", a["edge_weight"]),
        ("W1l", a["L0_gnn_W1l"].T), ("b1l", a["L0_gnn_b1l"].reshape(2, 128).T), ("W1r", a["L0_gnn_W1r"].T),
        ("W2cat", np.concatenate([a["L0_gnn_W2l"].T, a["L0_gnn_W2r"].T], axis=1)), ("b2l", rows(a["L0_gnn_b2l"])),
        ("C1", a["L1_gnn_W1"]), ("c1", a["L1_gnn_b1"].reshape(-1, 1)), ("C2", a["L1_gnn_W2"]),
        ("c2", a["L1_gnn_b2"].reshape(1, -1)), ("gamma", rows(a["L1_gnn_gamma"])), ("beta", rows(a["L1_gnn_beta"])),
        ("bases", a["L2_gnn_bases"]), ("comp", rows(a["L2_gnn_comp"])), ("root", a["L2_gnn_root"]),
        ("bias", rows(a["L2_gnn_bias"])), ("V1", a["L3_gnn_W1"]), ("v1", a["L3_gnn_b1"].reshape(-1, 1)),
        ("V2", a["L3_gnn_W2"]), ("v2", rows(a["L3_gnn_b2"])),
    ]
    nc = bacc.Bacc("TRN2", target_bir_lowering=False, num_devices=1)
    arrays, args = {}, []
    for name, v in given:
        v = np.ascontiguousarray(v)
        arrays[f"in_{name}"] = v
        args.append(nc.dram_tensor(f"in_{name}", v.shape, mb.dt.from_np(v.dtype), kind="ExternalInput").ap())
    out = nc.dram_tensor("out_x", a["x"].shape, mb.dt.from_np(np.dtype("float32")), kind="ExternalOutput").ap()
    gnn_kernel(nc, *args, out)
    r = run(nc, [arrays], core_ids=[0])
    return r.results[0]["out_x"]
```
